# Optimizing a Trainium2 kernel written in Bass

```python
import numpy as np
import jax
import jax.numpy as jnp

def _softmax(x, axis=-1):
    return jax.nn.softmax(x, axis=axis)

def _gelu(x):
    return jax.nn.gelu(x, approximate=True)

def _silu(x):
    return jax.nn.silu(x)

def _sigmoid(x):
    return jax.nn.sigmoid(x)

def _layernorm(x, axis=-1, eps=1e-05):
    m = jnp.mean(x, axis=axis, keepdims=True)
    v = jnp.var(x, axis=axis, keepdims=True)
    return (x - m) / jnp.sqrt(v + eps)

def _scatter_add(tgt, idx, src, axis=0):
    return tgt.at[idx].add(src)

def _segment_sum(src, seg, n):
    return jax.ops.segment_sum(src, seg, n)
kernel_name = 'mk_hybrid_d1_jaxref_r8_31123a'

def setup_inputs(seed: int=0):
    np.random.seed(seed)
    _w = jnp.asarray

    def _L0_attn_a_setup():
        import jax, jax.numpy as jnp
        import numpy as np
        DIM = 128
        NUM_HEAD = 16
        DIM_HEAD = DIM // NUM_HEAD
        RMS_EPS = 1.1920929e-07
        EPS_LIN = 1e-06
        THETA = 10000.0

        def rmsnorm(x, g, eps=RMS_EPS):
            return x * jax.lax.rsqrt(jnp.mean(x * x, axis=-1, keepdims=True) + eps) * g

        def rope_cos_sin(seq_len, dim_head, dtype=jnp.float32):
            inv_freq = 1.0 / THETA ** (jnp.arange(0, dim_head, 2, dtype=dtype) / dim_head)
            t = jnp.arange(seq_len, dtype=dtype)
            freqs = jnp.outer(t, inv_freq)
            return (jnp.cos(freqs), jnp.sin(freqs))

        def apply_rope(t, cos, sin):
            tr = t[..., 0::2]
            ti = t[..., 1::2]
            out_r = tr * cos - ti * sin
            out_i = tr * sin + ti * cos
            return jnp.stack([out_r, out_i], axis=-1).reshape(t.shape)
        key = jax.random.key(seed)
        ks = jax.random.split(key, 5)
        B, L = (4, 512)
        x = jax.random.normal(ks[0], (B, L, DIM), dtype=jnp.float32)
        Wqkv = jax.random.normal(ks[1], (3 * DIM, DIM), dtype=jnp.float32) * 0.02
        bqkv = jax.random.normal(ks[2], (3 * DIM,), dtype=jnp.float32) * 0.02
        gq = jnp.ones((DIM,), dtype=jnp.float32)
        gk = jnp.ones((DIM,), dtype=jnp.float32)
        Wout = jax.random.normal(ks[3], (DIM, DIM), dtype=jnp.float32) * 0.02
        bout = jax.random.normal(ks[4], (DIM,), dtype=jnp.float32) * 0.02
        gout = jnp.ones((DIM,), dtype=jnp.float32)
        return {'x': x, 'Wqkv': Wqkv, 'bqkv': bqkv, 'gq': gq, 'gk': gk, 'Wout': Wout, 'bout': bout, 'gout': gout}
    _L0_attn_a_in = _L0_attn_a_setup()

    def _L0_attn_b_setup():
        import jax, jax.numpy as jnp
        import numpy as np
        import math
        B, T, C = (64, 64, 128)
        LAYER_ID, N_LAYER = (6, 12)

        def _wkv(w, u, k, v):
            b, t, c = k.shape

            def step(carry, kv):
                aa, bb, pp = carry
                kt, vt = kv
                ww = u + kt
                q = jnp.maximum(pp, ww)
                e1 = jnp.exp(pp - q)
                e2 = jnp.exp(ww - q)
                y = (e1 * aa + e2 * vt) / (e1 * bb + e2)
                ww2 = pp + w
                q2 = jnp.maximum(ww2, kt)
                e1 = jnp.exp(ww2 - q2)
                e2 = jnp.exp(kt - q2)
                return ((e1 * aa + e2 * vt, e1 * bb + e2, q2), y)
            init = (jnp.zeros((b, c), k.dtype), jnp.zeros((b, c), k.dtype), jnp.full((b, c), -1e+38, k.dtype))
            _, ys = jax.lax.scan(step, init, (jnp.swapaxes(k, 0, 1), jnp.swapaxes(v, 0, 1)))
            return jnp.swapaxes(ys, 0, 1)
        key = jax.random.key(seed)
        k1, k2, k3, k4, k5 = jax.random.split(key, 5)
        r01 = LAYER_ID / N_LAYER
        r10 = 1.0 - r01
        i = jnp.arange(C, dtype=jnp.float32)
        ddd = i / C
        time_decay = -5.0 + 8.0 * (i / (C - 1)) ** (0.7 + 1.3 * r01)
        zigzag = ((jnp.arange(C) + 1) % 3 - 1).astype(jnp.float32) * 0.5
        time_first = jnp.full((C,), math.log(0.3), jnp.float32) + zigzag
        time_mix_k = (ddd ** r10).reshape(1, 1, C)
        time_mix_v = (ddd ** r10 + 0.3 * r01).reshape(1, 1, C)
        time_mix_r = (ddd ** (0.5 * r10)).reshape(1, 1, C)
        x = jax.random.normal(k1, (B, T, C), jnp.float32)
        Wk = jax.random.normal(k2, (C, C), jnp.float32) * 0.02
        Wv = jax.random.normal(k3, (C, C), jnp.float32) * 0.02
        Wr = jax.random.normal(k4, (C, C), jnp.float32) * 0.02
        Wo = jax.random.normal(k5, (C, C), jnp.float32) * 0.02
        return {'x': x, 'time_decay': time_decay, 'time_first': time_first, 'time_mix_k': time_mix_k, 'time_mix_v': time_mix_v, 'time_mix_r': time_mix_r, 'Wk': Wk, 'Wv': Wv, 'Wr': Wr, 'Wo': Wo}
    _L0_attn_b_in = _L0_attn_b_setup()

    def _L0_ffn_setup():
        import jax, jax.numpy as jnp
        import numpy as np
        D, H, N, K = (128, 256, 8, 2)
        B, S = (4, 256)
        key = jax.random.key(seed)
        ks = jax.random.split(key, 4)
        x = jax.random.normal(ks[0], (B, S, D), dtype=jnp.float32)
        Wr = jax.random.normal(ks[1], (N, D), dtype=jnp.float32) / np.sqrt(D)
        br = jnp.zeros((N,), jnp.float32)
        Wl1 = jax.random.normal(ks[2], (N, D, 2 * H), dtype=jnp.float32) / np.sqrt(D)
        bl1 = jnp.zeros((N, 2 * H), jnp.float32)
        Wl2 = jax.random.normal(ks[3], (N, H, D), dtype=jnp.float32) / np.sqrt(H)
        bl2 = jnp.zeros((N, D), jnp.float32)
        biases_N = jnp.zeros((N,), jnp.float32)
        return {'x': x, 'Wr': Wr, 'br': br, 'Wl1': Wl1, 'bl1': bl1, 'Wl2': Wl2, 'bl2': bl2, 'biases_N': biases_N}
    _L0_ffn_in = _L0_ffn_setup()
    _d = {'L0_attn_a_x': _L0_attn_a_in['x'], 'L0_attn_a_Wqkv': _L0_attn_a_in['Wqkv'], 'L0_attn_a_bqkv': _L0_attn_a_in['bqkv'], 'L0_attn_a_gq': _L0_attn_a_in['gq'], 'L0_attn_a_gk': _L0_attn_a_in['gk'], 'L0_attn_a_Wout': _L0_attn_a_in['Wout'], 'L0_attn_a_bout': _L0_attn_a_in['bout'], 'L0_attn_a_gout': _L0_attn_a_in['gout'], 'L0_attn_b_time_decay': _L0_attn_b_in['time_decay'], 'L0_attn_b_time_first': _L0_attn_b_in['time_first'], 'L0_attn_b_time_mix_k': _L0_attn_b_in['time_mix_k'], 'L0_attn_b_time_mix_v': _L0_attn_b_in['time_mix_v'], 'L0_attn_b_time_mix_r': _L0_attn_b_in['time_mix_r'], 'L0_attn_b_Wk': _L0_attn_b_in['Wk'], 'L0_attn_b_Wv': _L0_attn_b_in['Wv'], 'L0_attn_b_Wr': _L0_attn_b_in['Wr'], 'L0_attn_b_Wo': _L0_attn_b_in['Wo'], 'L0_ffn_Wr': _L0_ffn_in['Wr'], 'L0_ffn_br': _L0_ffn_in['br'], 'L0_ffn_Wl1': _L0_ffn_in['Wl1'], 'L0_ffn_bl1': _L0_ffn_in['bl1'], 'L0_ffn_Wl2': _L0_ffn_in['Wl2'], 'L0_ffn_bl2': _L0_ffn_in['bl2'], 'L0_ffn_biases_N': _L0_ffn_in['biases_N']}
    _x0 = _d['L0_attn_a_x']
    _d['L0_attn_a_x'] = jax.random.normal(jax.random.fold_in(jax.random.key(seed), 1), (8, 1024, 128), dtype=_x0.dtype)
    del _x0
    return _d

def reference(L0_attn_a_x, L0_attn_a_Wqkv, L0_attn_a_bqkv, L0_attn_a_gq, L0_attn_a_gk, L0_attn_a_Wout, L0_attn_a_bout, L0_attn_a_gout, L0_attn_b_time_decay, L0_attn_b_time_first, L0_attn_b_time_mix_k, L0_attn_b_time_mix_v, L0_attn_b_time_mix_r, L0_attn_b_Wk, L0_attn_b_Wv, L0_attn_b_Wr, L0_attn_b_Wo, L0_ffn_Wr, L0_ffn_br, L0_ffn_Wl1, L0_ffn_bl1, L0_ffn_Wl2, L0_ffn_bl2, L0_ffn_biases_N):

    def _L0_attn_a_ref(x, Wqkv, bqkv, gq, gk, Wout, bout, gout):
        import jax, jax.numpy as jnp
        import numpy as np
        DIM = 128
        NUM_HEAD = 16
        DIM_HEAD = DIM // NUM_HEAD
        RMS_EPS = 1.1920929e-07
        EPS_LIN = 1e-06
        THETA = 10000.0

        def rmsnorm(x, g, eps=RMS_EPS):
            return x * jax.lax.rsqrt(jnp.mean(x * x, axis=-1, keepdims=True) + eps) * g

        def rope_cos_sin(seq_len, dim_head, dtype=jnp.float32):
            inv_freq = 1.0 / THETA ** (jnp.arange(0, dim_head, 2, dtype=dtype) / dim_head)
            t = jnp.arange(seq_len, dtype=dtype)
            freqs = jnp.outer(t, inv_freq)
            return (jnp.cos(freqs), jnp.sin(freqs))

        def apply_rope(t, cos, sin):
            tr = t[..., 0::2]
            ti = t[..., 1::2]
            out_r = tr * cos - ti * sin
            out_i = tr * sin + ti * cos
            return jnp.stack([out_r, out_i], axis=-1).reshape(t.shape)
        B, L, D = x.shape
        qkv = x @ Wqkv.T + bqkv
        q, k, v = jnp.split(qkv, 3, axis=-1)
        q = rmsnorm(q, gq)
        k = rmsnorm(k, gk)
        split = lambda t: t.reshape(B, L, NUM_HEAD, DIM_HEAD).transpose(0, 2, 1, 3)
        q, k, v = (split(q), split(k), split(v))
        cos, sin = rope_cos_sin(L, DIM_HEAD)
        cos = cos[None, None]
        sin = sin[None, None]
        q = apply_rope(q, cos, sin)
        k = apply_rope(k, cos, sin)
        qf = jax.nn.relu(q)
        kf = jax.nn.relu(k)
        vpad = jnp.concatenate([v, jnp.ones_like(v[..., :1])], axis=-1)
        vk = jnp.einsum('bhlp,bhld->bhpd', vpad, kf)
        res = jnp.einsum('bhpd,bhld->bhlp', vk, qf)
        attn = res[..., :-1] / (res[..., -1:] + EPS_LIN)
        attn = attn.transpose(0, 2, 1, 3).reshape(B, L, D)
        out = rmsnorm(attn @ Wout.T + bout, gout)
        return out

    def _L0_attn_b_ref(x, time_decay, time_first, time_mix_k, time_mix_v, time_mix_r, Wk, Wv, Wr, Wo):
        import jax, jax.numpy as jnp
        import numpy as np
        import math
        B, T, C = (64, 64, 128)
        LAYER_ID, N_LAYER = (6, 12)

        def _wkv(w, u, k, v):
            b, t, c = k.shape

            def step(carry, kv):
                aa, bb, pp = carry
                kt, vt = kv
                ww = u + kt
                q = jnp.maximum(pp, ww)
                e1 = jnp.exp(pp - q)
                e2 = jnp.exp(ww - q)
                y = (e1 * aa + e2 * vt) / (e1 * bb + e2)
                ww2 = pp + w
                q2 = jnp.maximum(ww2, kt)
                e1 = jnp.exp(ww2 - q2)
                e2 = jnp.exp(kt - q2)
                return ((e1 * aa + e2 * vt, e1 * bb + e2, q2), y)
            init = (jnp.zeros((b, c), k.dtype), jnp.zeros((b, c), k.dtype), jnp.full((b, c), -1e+38, k.dtype))
            _, ys = jax.lax.scan(step, init, (jnp.swapaxes(k, 0, 1), jnp.swapaxes(v, 0, 1)))
            return jnp.swapaxes(ys, 0, 1)
        xx = jnp.pad(x, ((0, 0), (1, 0), (0, 0)))[:, :-1]
        xk = x * time_mix_k + xx * (1.0 - time_mix_k)
        xv = x * time_mix_v + xx * (1.0 - time_mix_v)
        xr = x * time_mix_r + xx * (1.0 - time_mix_r)
        k = jnp.einsum('btc,dc->btd', xk, Wk)
        v = jnp.einsum('btc,dc->btd', xv, Wv)
        sr = jax.nn.sigmoid(jnp.einsum('btc,dc->btd', xr, Wr))
        w = -jnp.exp(time_decay)
        rwkv = sr * _wkv(w, time_first, k, v)
        return jnp.einsum('btc,dc->btd', rwkv, Wo)

    def _L0_ffn_ref(x, Wr, br, Wl1, bl1, Wl2, bl2, biases_N):
        import jax, jax.numpy as jnp
        import numpy as np
        D, H, N, K = (128, 256, 8, 2)
        B, S = (4, 256)
        Bb, Ss, Dd = x.shape
        scores_BSN = jnp.einsum('bsd,nd->bsn', x, Wr) + br
        w_BSN = jax.nn.softmax(scores_BSN, axis=-1)
        _, idx_BSK = jax.lax.top_k(scores_BSN + biases_N[None, None, :], K)
        val_BSK = jnp.take_along_axis(w_BSN, idx_BSK, axis=-1)
        val_BSK = val_BSK / jnp.sum(val_BSK, axis=-1, keepdims=True)
        M = Bb * Ss
        x_MD = x.reshape(M, Dd)
        idx_MK = idx_BSK.reshape(M, K)
        val_MK = val_BSK.reshape(M, K)
        h_NM2H = jnp.einsum('md,ndh->nmh', x_MD, Wl1) + bl1[:, None, :]
        a_NMH, b_NMH = (h_NM2H[..., :H], h_NM2H[..., H:])
        y_NMD = jnp.einsum('nmh,nhd->nmd', jax.nn.silu(a_NMH) * b_NMH, Wl2) + bl2[:, None, :]
        ew_MN = jnp.zeros((M, N), x.dtype)
        ew_MN = ew_MN.at[jnp.arange(M)[:, None], idx_MK].set(val_MK)
        y_MD = jnp.einsum('mn,nmd->md', ew_MN, y_NMD)
        return y_MD.reshape(Bb, Ss, Dd)
    x = L0_attn_a_x
    x = x + _L0_attn_a_ref(_layernorm(x, axis=-1), L0_attn_a_Wqkv, L0_attn_a_bqkv, L0_attn_a_gq, L0_attn_a_gk, L0_attn_a_Wout, L0_attn_a_bout, L0_attn_a_gout)
    x = x + _L0_ffn_ref(_layernorm(x, axis=-1), L0_ffn_Wr, L0_ffn_br, L0_ffn_Wl1, L0_ffn_bl1, L0_ffn_Wl2, L0_ffn_bl2, L0_ffn_biases_N)
    x = x + _L0_attn_b_ref(_layernorm(x, axis=-1), L0_attn_b_time_decay, L0_attn_b_time_first, L0_attn_b_time_mix_k, L0_attn_b_time_mix_v, L0_attn_b_time_mix_r, L0_attn_b_Wk, L0_attn_b_Wv, L0_attn_b_Wr, L0_attn_b_Wo)
    x = x + _L0_ffn_ref(_layernorm(x, axis=-1), L0_ffn_Wr, L0_ffn_br, L0_ffn_Wl1, L0_ffn_bl1, L0_ffn_Wl2, L0_ffn_bl2, L0_ffn_biases_N)
    return x

_drawn_inputs = setup_inputs


def setup_inputs(seed=0):
    import zlib

    import numpy as np

    out = dict(_drawn_inputs(seed))
    spreads = {'L0_attn_a_gq': (1.0, 0.2),
     'L0_attn_a_gk': (1.0, 0.2),
     'L0_attn_a_gout': (1.0, 0.2),
     'L0_ffn_br': (0.0, 0.1),
     'L0_ffn_bl1': (0.0, 0.1),
     'L0_ffn_bl2': (0.0, 0.1),
     'L0_ffn_biases_N': (0.0, 0.1)}
    factors = {'L0_attn_b_time_decay': 4.0,
     'L0_attn_b_time_first': 8.0,
     'L0_attn_b_time_mix_k': 8.0,
     'L0_attn_b_time_mix_v': 7.779,
     'L0_attn_b_time_mix_r': 8.0,
     'L0_attn_b_Wk': 8.0,
     'L0_attn_b_Wr': 6.704}
    for name, (base, spread) in spreads.items():
        noise = np.random.default_rng([zlib.crc32(name.encode()), seed]).standard_normal(out[name].shape)
        drawn = base * np.exp(spread * noise) if base else spread * noise
        out[name] = jnp.asarray(drawn.astype(out[name].dtype))
    for name, factor in factors.items():
        out[name] = (out[name] * factor).astype(out[name].dtype)
    return out
```

```python
from contextlib import ExitStack

import concourse.bass as bass
from concourse import mybir

F32 = mybir.dt.float32
BF16 = mybir.dt.bfloat16
I32 = mybir.dt.int32
U32 = mybir.dt.uint32
ALU = mybir.AluOpType
ACT = mybir.ActivationFunctionType
AX = mybir.AxisListType

P = 128
BATCH, SEQ, D = 8, 1024, 128
TOKENS = BATCH * SEQ
TPC = 4
CHUNK = TPC * P
HALVES = SEQ // CHUNK
CHUNKS = TOKENS // CHUNK
TILES = TOKENS // P
HEADS, DH = 16, 8
NE, TOPK, HID = 8, 2, 256
HCH = HID // P
ROW_W = D + 2
NO_RESULT = TOKENS * TOPK
REGION = TOKENS + P
STEP = 8
XTILES = -(-(TOKENS * TOPK // P + NE - 1) // STEP) * STEP
LOADED = XTILES + STEP
RES_W = D + HEADS
RES_PITCH = 256
LN_EPS, RMS_EPS, LIN_EPS = 1e-5, 1.1920929e-07, 1e-6
NO_PAST = -1e38

B_QKV, B_OUT = 0, 3 * D
B_UP, B_DOWN = B_OUT + D, B_OUT + D + NE * 2 * HID
B_ALL = B_DOWN + NE * D

K_ID, K_TRI, K_BLOCK = 0, P, 2 * P
K_HEAD = 3 * P
K_IOTA = K_HEAD + HEADS
K_REGION = K_IOTA + NE
K_PART = K_REGION + NE
K_TILE = K_PART + 1
K_TOKEN = K_TILE + LOADED
K_ALL = K_TOKEN + TILES

V_DECAY, V_FIRST, V_MIXK, V_MIXV, V_MIXR = range(5)


def program(nc, x, cosine, sine, consts, w_qkv, w_out, g_qk, g_qk_swapped, g_out, bias_cols, w_router,
            router_rows, w_up, w_down, channel, w_k, w_v, w_r, w_o, out):
    with ExitStack() as ctx:
        def sb(name, shape, dt=F32):
            return ctx.enter_context(nc.sbuf_tensor(name, shape, dt))

        def sem(name):
            return ctx.enter_context(nc.semaphore(name))

        def sem2(name):
            return [sem(f"{name}{c}") for c in range(HALVES)]

        def dram(name, shape, dt=F32):
            return nc.dram_tensor(name, shape, dt).ap()

        x1_dram = dram("x1_dram", [TOKENS, D])
        x3_dram = dram("x3_dram", [TOKENS, D])
        queue_dram = dram("queue_dram", [NE * REGION, ROW_W])
        result_dram = dram("result_dram", [NO_RESULT + P + STEP, D])
        split_dram = dram("split_dram", [3, B_ALL], BF16)

        k_sb = sb("k_sb", [P, K_ALL])
        wqkv_sb = sb("wqkv_sb", [P, 3 * D])
        wout_sb = sb("wout_sb", [P, D])
        wrouter_sb = sb("wrouter_sb", [P, NE])
        rows_sb = sb("rows_sb", [P, 2 * NE])
        wup_sb = sb("wup_sb", [P, NE * 2 * HID])
        wdown_sb = sb("wdown_sb", [P, NE * HCH * D])
        gqk_sb = sb("gqk_sb", [P, 2 * D])
        gqks_sb = sb("gqks_sb", [P, 2 * D])
        gout_sb = sb("gout_sb", [P, D])
        expo = sb("expo", [P, 4, CHUNK])
        cos_sb, sin_sb = (expo[:, 2 * i:2 * i + 2, :].rearrange("p a (t d) -> p (a t) d", d=D) for i in range(2))
        ex = sb("ex", [P, 4, CHUNK])
        past, past_j = (ex[:, 2 * i:2 * i + 2, :].rearrange("p a n -> p (a n)")[:, 0:(NE - 1) * LOADED].rearrange(
            "p (e t) -> p e t", e=NE - 1) for i in range(2))
        rope_c = sb("rope_c", [P, SEQ // P, 2 * D])
        rope_s = sb("rope_s", [P, SEQ // P, 2 * D])
        bias_sb = sb("bias_sb", [P, B_ALL // P])
        bias_left = sb("bias_left", [P, B_ALL // P])
        bias_parts = sb("bias_parts", [P, 3, B_ALL // P], BF16)
        bias_rows = sb("bias_rows", [P, B_ALL], BF16)
        ones_bf = sb("ones_bf", [P, P], BF16)
        tri_bf = sb("tri_bf", [P, P], BF16)
        ones8 = sb("ones8", [P, NE])
        ln_eps = sb("ln_eps", [P, 1])
        rms_eps = sb("rms_eps", [P, 1])
        ch_sb = sb("ch_sb", [P, 5])
        w_sb = sb("w_sb", [P, 1])
        exp_decay = sb("exp_decay", [P, 1])
        mix_left = sb("mix_left", [P, 3])
        wkvr_sb = sb("wkvr_sb", [P, 3, D])
        wnow_sb = sb("wnow_sb", [P, 3, D])
        wpast_sb = sb("wpast_sb", [P, 3, D])
        wo_sb = sb("wo_sb", [P, D])
        tail_rows = sb("tail_rows", [P, ROW_W])
        ident = k_sb[:, K_ID:K_ID + P]

        xin = [sb(f"xin{c}", [P, TPC, D]) for c in range(HALVES)]
        xmid = [sb(f"xmid{c}", [P, TPC, D]) for c in range(HALVES)]
        xres = [sb(f"xres{c}", [P, TPC, D]) for c in range(HALVES)]
        hmix = sb("hmix", [P, TPC, D])
        hffn = [sb(f"hffn{c}", [P, TPC, ROW_W]) for c in range(HALVES)]
        stats = sb("stats", [P, TPC, 6])
        meanvar = sb("meanvar", [P, TPC, 2])
        deviation = sb("deviation", [P, TPC])
        rstd = sb("rstd", [P, TPC])
        hmix_t = sb("hmix_t", [P, CHUNK])
        hffn_t = sb("hffn_t", [P, CHUNK])

        qk = sb("qk", [P, TPC, 2 * D])
        rope1 = sb("rope1", [P, TPC, 2 * D])
        rope2 = sb("rope2", [P, TPC, 2 * D])
        vpad = [sb(f"vpad{c}", [P, TPC, D + 1]) for c in range(HALVES)]
        qf = [sb(f"qf{c}", [P, TPC, D]) for c in range(HALVES)]
        kf = [sb(f"kf{c}", [P, TPC, D]) for c in range(HALVES)]
        qf_t = [sb(f"qf_t{c}", [P, CHUNK]) for c in range(HALVES)]
        squares = sb("squares", [P, 2, TPC, D])
        sumsq = sb("sumsq", [P, 2, TPC])
        qk_dev = sb("qk_dev", [P, 2, TPC])
        qk_rstd = sb("qk_rstd", [P, 2, TPC])
        state = sb("state", [P, RES_W])
        den_a = sb("den_a", [P, TPC, HEADS])
        rden = sb("rden", [P, TPC, HEADS])
        attn = sb("attn", [P, TPC, D])
        attn_t = sb("attn_t", [P, CHUNK])
        osq = sb("osq", [P, TPC])
        o_dev = sb("o_dev", [P, TPC])
        o_rstd = sb("o_rstd", [P, TPC])
        onorm = sb("onorm", [P, TPC, D])

        score = sb("score", [P, TPC, NE])
        biased = sb("biased", [P, TPC, NE])
        top8 = sb("top8", [P, TPC, 8])
        top_at = sb("top_at", [P, TPC, 8], U32)
        top_f = sb("top_f", [P, TPC, TOPK])
        onehot = sb("onehot", [P, TPC, TOPK, NE])
        member = sb("member", [P, TPC, NE], BF16)
        seen = sb("seen", [P, NE], BF16)
        seen_new = sb("seen_new", [P, NE])
        place8 = sb("place8", [P, TPC, NE])
        picked = sb("picked", [P, TPC, TOPK, NE])
        place_f = sb("place_f", [P, TPC, TOPK])
        place_i = [sb(f"place_i{c}", [P, TPC * TOPK], I32) for c in range(HALVES)]
        score_all = sb("score_all", [P, TILES, NE])
        onehot_all = sb("onehot_all", [P, TILES, TOPK, NE])
        big = sb("big", [P, TILES, TOPK, NE])
        small_a = sb("small_a", [P, TILES, NE])
        top_all = sb("top_all", [P, TILES])
        gate_w = sb("gate_w", [P, TILES, TOPK])
        gate_sum = sb("gate_sum", [P, TILES])
        gate_all = sb("gate_all", [P, TILES, TOPK])
        count = sb("count", [P, NE])
        count_i = sb("count_i", [P, NE], I32)
        ntile_i = sb("ntile_i", [P, NE], I32)
        ntile = sb("ntile", [P, NE])
        cum = sb("cum", [P, NE])
        cum_rows = sb("cum_rows", [P, NE])
        jump = sb("jump", [P, NE])
        tail_f = sb("tail_f", [P, NE])
        tail_i = sb("tail_i", [P, NE], I32)
        last_row = sb("last_row", [P, 1])
        expert_all = sb("expert_all", [P, LOADED])
        row_f = sb("row_f", [1, LOADED])
        row_g = sb("row_g", [1, LOADED])
        tile_row = sb("tile_row", [1, LOADED], I32)
        tile_expert = sb("tile_expert", [1, LOADED], I32)

        xtile = [sb(f"xtile{i}", [P, ROW_W]) for i in range(STEP)]
        result_row = [sb(f"result_row{i}", [P, 1], I32) for i in range(STEP)]
        xtile_t = [sb(f"xtile_t{i}", [P, P]) for i in range(2)]
        silu = [sb(f"silu{i}", [P, HID]) for i in range(2)]
        gated = [sb(f"gated{i}", [P, HID]) for i in range(2)]
        gated_t = [sb(f"gated_t{i}", [P, HID]) for i in range(2)]
        ytile = [sb(f"ytile{i}", [P, D]) for i in range(STEP)]

        back_x = [sb(f"back_x{c}", [P, TPC * TOPK, D]) for c in range(HALVES)]
        gate = sb("gate", [P, TPC * TOPK])
        hseq = sb("hseq", [P, 1 + SEQ])
        top = sb("top", [P, 1 + SEQ])
        num = sb("num", [P, 1 + SEQ])
        den = sb("den", [P, 1 + SEQ])
        def halves(a):
            return (a[:, 2 * i:2 * i + 2, :].rearrange("p j n -> p (j n)") for i in range(2))

        y_num, y_den = halves(rope1)
        y_b, e_r = halves(rope2)
        qmax, ev = halves(qk)
        rwkv = sb("rwkv", [P, CHUNK])

        quad = ctx.enter_context(nc.psum_tensor("quad", [P, 4, 512], F32))
        bank = [ctx.enter_context(nc.psum_tensor(f"bank{i}", [P, 512], F32)) for i in range(4, 8)]
        ps_t, ps_vk, ps_out, ps_route = bank
        ps_up = [quad[:, 0, :], quad[:, 1, :]]
        ps_gt = [quad[:, 2, :], quad[:, 3, :]]
        ps_xt = [bank[0], bank[1]]
        ps_y = [bank[2], bank[3]]
        ps_res = quad[:, 0:2, :].rearrange("p a (b n) -> p (a b) n", n=RES_PITCH)
        ps_k, ps_v, ps_r = quad[:, 0, :], quad[:, 1, :], quad[:, 2, :]
        ps_score = ps_route[:, 0:TPC * NE].rearrange("p (j e) -> p j e", e=NE)
        ps_rank = ps_route[:, 64:64 + TPC * NE].rearrange("p (j e) -> p j e", e=NE)
        ps_count = ps_route[:, 128:128 + NE]
        ps_out4 = ps_out[:, :].rearrange("p (j n) -> p j n", j=TPC)

        weights_in, rope_in, bias_in, split_out, rows_in = (
            sem("weights_in"), sem("rope_in"), sem("bias_in"), sem("split_out"), sem("rows_in"))
        dve_step, act_step = sem("dve_step"), sem("act_step")
        setup_done, split_done, decay_ready = sem("setup_done"), sem("split_done"), sem("decay_ready")
        x_loaded, combined = sem2("x_loaded"), sem("combined")
        x_stored = sem2("x_stored")
        var_ready, dev_ready = sem("var_ready"), sem("dev_ready")
        h_ready, h_turned, ht_ready = sem("h_ready"), sem("h_turned"), sem("ht_ready")
        qkv_ready, v_ready, qk_ready = sem("qkv_ready"), sem("v_ready"), sem("qk_ready")
        qkdev_ready, kf_ready, qf_ready = sem("qkdev_ready"), sem("kf_ready"), sem("qf_ready")
        vk_ready, qf_turned, qft_ready = sem("vk_ready"), sem("qf_turned"), sem("qft_ready")
        state_ready, res_ready, attn_ready = sem("state_ready"), sem("res_ready"), sem("attn_ready")
        attn_turned, attnt_ready = sem("attn_turned"), sem("attnt_ready")
        out_ready, odev_ready, xres_ready = sem("out_ready"), sem("odev_ready"), sem("xres_ready")
        var2_ready, dev2_ready = sem("var2_ready"), sem("dev2_ready")
        h2_ready, h2_turned, h2t_ready = sem("h2_ready"), sem("h2_turned"), sem("h2t_ready")
        score_ready, member_ready, rank_ready = sem("score_ready"), sem("member_ready"), sem("rank_ready")
        place_ready = sem("place_ready")
        queued = sem2("queued")
        seen_ready, count_ready, tail_ready, tails_queued = (
            sem("seen_ready"), sem("count_ready"), sem("tail_ready"), sem("tails_queued"))
        table_ready, gate_in, gate_exp = sem("table_ready"), sem("gate_in"), sem("gate_exp")
        xtile_in = [sem(f"xtile_in{i}") for i in range(STEP)]
        xtile_turned, xtilet_ready, up_ready, silu_ready, gated_ready = (
            sem("xtile_turned"), sem("xtilet_ready"), sem("up_ready"), sem("silu_ready"), sem("gated_ready"))
        gated_turned, gatedt_ready, y_ready, ytile_ready = (
            sem("gated_turned"), sem("gatedt_ready"), sem("y_ready"), sem("ytile_ready"))
        y_stored = [sem(f"y_stored{i}") for i in range(STEP)]
        results_in, place_taken = sem2("results_in"), sem("place_taken")
        kvr_ready, expo_ready, ex_ready, er_ready = sem("kvr_ready"), sem("expo_ready"), sem("ex_ready"), sem("er_ready")
        rwkv_ready, mixed_ready = sem("rwkv_ready"), sem("mixed_ready")
        h3_ready, h3_turned, hseq_ready = sem("h3_ready"), sem("h3_turned"), sem("hseq_ready")
        var3_ready, dev3_ready = sem("var3_ready"), sem("dev3_ready")
        out_stored = sem2("out_stored")

        block = ctx.enter_context(nc.Block())

        def rows(dram_ap, chunk):
            return dram_ap[bass.ds(chunk * CHUNK, CHUNK), :].rearrange("(j p) d -> p j d", p=P)

        FIRST, SECOND = 0, 1
        N_TURN, N_UP, N_GATE, N_BACK = XTILES + 3, XTILES + 2, XTILES + 1, XTILES
        SCATTERS = 16 * TPC * TOPK
        WEIGHTS = [(k_sb[:], consts), (wqkv_sb[:], w_qkv), (wout_sb[:], w_out), (wrouter_sb[:], w_router),
                   (rows_sb[:], router_rows), (gout_sb[:], g_out), (ch_sb[:], channel), (wkvr_sb[:, 0, :], w_k),
                   (wkvr_sb[:, 1, :], w_v), (wkvr_sb[:, 2, :], w_r), (wo_sb[:], w_o), (wup_sb[:], w_up),
                   (wdown_sb[:], w_down)]
        ROPE = [(cos_sb, cosine), (sin_sb, sine), (gqk_sb[:], g_qk), (gqks_sb[:], g_qk_swapped)]

        @block.sync
        def _(sp):
            sp.dma_start(bias_sb[:], bias_cols).then_inc(bias_in, 16)
            for c in range(HALVES):
                sp.dma_start(xin[c][:], rows(x, c)).then_inc(x_loaded[c], 16)
            for dst, src in WEIGHTS:
                sp.dma_start(dst, src).then_inc(weights_in, 16)
            for dst, src in ROPE:
                sp.dma_start(dst, src).then_inc(rope_in, 16)
            sp.wait_ge(split_done, 1)
            for i in range(3):
                sp.dma_start(split_dram[i, :].rearrange("(p n) -> p n", p=P), bias_parts[:, i, :]).then_inc(split_out, 16)
            sp.wait_ge(split_out, 3 * 16)
            sp.wait_ge(setup_done, 1)
            sp.dma_start(bias_rows[0:3, :], split_dram).then_inc(rows_in, 16)

            def load_results(chunk, c):
                rows_of = result_dram[bass.ds(chunk * (CHUNK * TOPK), CHUNK * TOPK), :]
                sp.dma_start(back_x[c][:].rearrange("p (j k) d -> p j k d", k=TOPK),
                             rows_of.rearrange("(j p k) d -> p j k d", p=P, k=TOPK)).then_inc(results_in[c], 16)

            def residual(b, src, dst, used, done, last):
                for c in range(HALVES):
                    if not last:
                        sp.wait_ge(used, b * HALVES + (done + c + 1))
                        sp.dma_start(xin[c][:], rows(src, b * HALVES + (HALVES + c))).then_inc(x_loaded[c], 16)
                        if src is x1_dram:
                            load_results(b * HALVES + (HALVES + c), c)
                    sp.wait_ge(xres_ready, b * HALVES + (dst[1] + c + 1))
                    sp.dma_start(rows(dst[0], b * HALVES + c), xres[c][:]).then_inc(x_stored[c], 16)

            def experts(f):
                for c in range(HALVES):
                    sp.wait_ge(queued[c], 16 + SCATTERS * BATCH * (f + 1))
                sp.wait_ge(tails_queued, 16 * NE * (f + 1))
                sp.wait_ge(table_ready, f + 1)

                def load(t, i):
                    row = sp.value_load(tile_row[0:1, bass.ds(t, 1)], min_val=0, max_val=NE * REGION - P)
                    sp.dma_start(xtile[i][:], queue_dram[bass.ds(row, P), :]).then_inc(xtile_in[i], 16)

                for t in range(STEP):
                    load(t, t)
                with sp.Fori(0, XTILES // STEP) as n:
                    for i in range(STEP):
                        sp.wait_ge(gated_ready, n * STEP + (i + 1 + f * N_GATE))
                        load(n * STEP + (i + STEP), i)
                for i in range(STEP):
                    sp.wait_ge(xtile_in[i], 16 * (LOADED // STEP) * (f + 1))
                    sp.wait_ge(y_stored[i], 16 * (N_BACK // STEP * (f + 1) + 1))
                for c in range(HALVES):
                    load_results(c, c)

            with sp.Fori(0, BATCH - 1) as b:
                residual(b, x, (x1_dram, 0), xres_ready, 0, False)
            residual(BATCH - 1, x, (x1_dram, 0), xres_ready, 0, True)
            experts(FIRST)
            for c in range(HALVES):
                sp.wait_ge(x_stored[c], 16 * (BATCH + 1))
                sp.dma_start(xin[c][:], rows(x1_dram, c)).then_inc(x_loaded[c], 16)
            with sp.Fori(0, BATCH - 1) as b:
                residual(b, x1_dram, (x3_dram, CHUNKS), combined, 0, False)
            residual(BATCH - 1, x1_dram, (x3_dram, CHUNKS), combined, 0, True)
            experts(SECOND)
            for c in range(HALVES):
                sp.wait_ge(x_stored[c], 16 * (2 * BATCH + 1))
                sp.dma_start(xin[c][:], rows(x3_dram, c)).then_inc(x_loaded[c], 16)

            def final(b, last):
                for c in range(HALVES):
                    sp.wait_ge(combined, b * HALVES + (CHUNKS + c + 1))
                    sp.dma_start(rows(out, b * HALVES + c), xmid[c][:]).then_inc(out_stored[c], 16)
                    if not last:
                        sp.dma_start(xin[c][:], rows(x3_dram, b * HALVES + (HALVES + c))).then_inc(x_loaded[c], 16)
                        load_results(b * HALVES + (HALVES + c), c)

            with sp.Fori(0, BATCH - 1) as b:
                final(b, False)
            final(BATCH - 1, True)
            for c in range(HALVES):
                sp.wait_ge(out_stored[c], 16 * (BATCH + 1))

        @block.gpsimd
        def _(pool):
            def scatter(b, c, f):
                pool.wait_ge(place_ready, b * HALVES + (c + 1 + f * CHUNKS))
                pool.sem_inc(place_taken, 1)
                for j in range(TPC):
                    for k in range(TOPK):
                        m = j * TOPK + k
                        nc.gpsimd.indirect_dma_start(
                            queue_dram, bass.IndirectOffsetOnAxis(ap=place_i[c][:, m:m + 1], axis=0),
                            hffn[c][:, j, :], None).then_inc(queued[c], 16)

            def tails(f):
                pool.wait_ge(tail_ready, f + 1)
                for e in range(NE):
                    nc.gpsimd.indirect_dma_start(
                        queue_dram, bass.IndirectOffsetOnAxis(ap=tail_i[:, e:e + 1], axis=0),
                        tail_rows[:], None).then_inc(tails_queued, 16)

            def experts(f):
                with pool.Fori(0, XTILES // STEP) as n:
                    for i in range(STEP):
                        pool.wait_ge(ytile_ready, n * STEP + (i + 1 + f * N_BACK))
                        pool.sem_inc(place_taken, 1)
                        nc.gpsimd.indirect_dma_start(
                            result_dram, bass.IndirectOffsetOnAxis(ap=result_row[i][:, 0:1], axis=0),
                            ytile[i][:], None, bounds_check=NO_RESULT - 1, oob_is_err=False).then_inc(y_stored[i], 16)

            pool.wait_ge(setup_done, 1)
            for c in range(HALVES):
                pool.dma_start(queue_dram[bass.ds((c + 1) * REGION - 1, 1), :], tail_rows[0:1, :]).then_inc(queued[c], 16)
            for i in range(STEP):
                pool.dma_start(result_dram[bass.ds(NO_RESULT + P + i, 1), :], tail_rows[0:1, 0:D]).then_inc(y_stored[i], 16)
            with pool.Fori(0, BATCH) as b:
                for c in range(HALVES):
                    scatter(b, c, FIRST)
            tails(FIRST)
            experts(FIRST)
            with pool.Fori(0, BATCH) as b:
                for c in range(HALVES):
                    scatter(b, c, SECOND)
            tails(SECOND)
            experts(SECOND)

        @block.scalar
        def _(act):
            step = [0]

            def begin():
                act.sem_clear(act_step)
                step[0] = 0

            def settle(ins):
                step[0] += 1
                ins.then_inc(act_step, 1)
                act.wait_ge(act_step, step[0])

            act.wait_ge(weights_in, 16 * len(WEIGHTS))
            nc.scalar.activation(exp_decay[:], ch_sb[:, V_DECAY:V_DECAY + 1], ACT.Exp).then_inc(decay_ready, 1)
            act.wait_ge(setup_done, 2)

            def deviations(var, dev, n1):
                act.wait_ge(var, n1)
                nc.scalar.activation(deviation[:], meanvar[:, :, 1], ACT.Sqrt, bias=ln_eps[:, 0:1]).then_inc(dev, 1)

            def turned(done, dst, ready, n1):
                act.wait_ge(done, n1)
                nc.scalar.activation(dst, ps_t[:, :], ACT.Copy).then_inc(ready, 1)

            def attention_in(b, c):
                n1 = b * HALVES + (c + 1)
                deviations(var_ready, dev_ready, n1)
                turned(h_turned, hmix_t[:], ht_ready, n1)
                act.wait_ge(qkv_ready, n1)
                nc.scalar.activation(qk[:], quad[:, :, 0:2 * D], ACT.Copy).then_inc(qk_ready, 1)
                nc.scalar.activation(vpad[c][:, :, 0:D], quad[:, :, 2 * D:3 * D], ACT.Copy).then_inc(v_ready, 1)
                act.wait_ge(qk_ready, n1)
                for half in range(2):
                    for j in range(TPC):
                        last = nc.scalar.activation(squares[:, half, j, :], qk[:, j, half * D:(half + 1) * D], ACT.Square,
                                                    accum_out=sumsq[:, half, j:j + 1])
                settle(last)
                nc.scalar.activation(qk_dev[:], sumsq[:], ACT.Sqrt, bias=rms_eps[:, 0:1], scale=1.0 / D).then_inc(qkdev_ready, 1)
                turned(qf_turned, qf_t[c][:], qft_ready, n1)

            def attention_out(b, c):
                n1 = b * HALVES + (c + 1)
                turned(attn_turned, attn_t[:], attnt_ready, n1)
                act.wait_ge(out_ready, n1)
                for j in range(TPC):
                    last = nc.scalar.activation(squares[:, 0, j, :], ps_out4[:, j, :], ACT.Square, accum_out=osq[:, j:j + 1])
                settle(last)
                nc.scalar.activation(o_dev[:], osq[:], ACT.Sqrt, bias=rms_eps[:, 0:1], scale=1.0 / D).then_inc(odev_ready, 1)

            def route(n1):
                deviations(var2_ready, dev2_ready, n1)
                turned(h2_turned, hffn_t[:], h2t_ready, n1)

            def plan(f):
                act.wait_ge(gate_in, f + 1)
                nc.scalar.activation(small_a[:], small_a[:], ACT.Exp).then_inc(gate_exp, 1)

            def experts(f):
                T, U, G, B = f * N_TURN, f * N_UP, f * N_GATE, f * N_BACK

                def turn_x(i, n1):
                    act.wait_ge(xtile_turned, n1)
                    nc.scalar.activation(xtile_t[i][:], ps_xt[i][:, 0:P], ACT.Copy).then_inc(xtilet_ready, 1)

                def silu_up(i, n1):
                    act.wait_ge(up_ready, n1)
                    nc.scalar.activation(silu[i][:], ps_up[i][:, 0:HID], ACT.Silu).then_inc(silu_ready, 1)

                for t in range(2):
                    turn_x(t, t + 1 + T)
                silu_up(0, 1 + U)
                turn_x(0, 3 + T)
                silu_up(1, 2 + U)
                with act.Fori(0, XTILES // STEP) as n:
                    for i in range(STEP):
                        turn_x((i + 1) % 2, n * STEP + (i + 4 + T))
                        act.wait_ge(gated_ready, n * STEP + (i + 1 + G))
                        silu_up(i % 2, n * STEP + (i + 3 + U))
                        act.wait_ge(y_ready, n * STEP + (i + 1 + B))
                        act.wait_ge(y_stored[i], (n + (1 + f * (N_BACK // STEP))) * 16)
                        nc.scalar.activation(ytile[i][:], ps_y[i % 2][:, 0:D], ACT.Copy).then_inc(ytile_ready, 1)

            def mixing(b, c):
                n1 = b * HALVES + (c + 1)
                deviations(var3_ready, dev3_ready, n1)
                turned(h3_turned, hseq[:, 1 + c * CHUNK:1 + (c + 1) * CHUNK], hseq_ready, n1)
                act.wait_ge(kvr_ready, n1)
                nc.scalar.activation(e_r, ps_r, ACT.Exp, scale=-1.0).then_inc(er_ready, 1)
                act.wait_ge(expo_ready, n1)
                nc.scalar.activation(ex[:], expo[:], ACT.Exp).then_inc(ex_ready, 1)

            with act.Fori(0, BATCH) as b:
                begin()
                for c in range(HALVES):
                    attention_in(b, c)
                for c in range(HALVES):
                    attention_out(b, c)
                    route(b * HALVES + (c + 1))
            plan(FIRST)
            experts(FIRST)
            with act.Fori(0, BATCH) as b:
                for c in range(HALVES):
                    mixing(b, c)
                    route(b * HALVES + (c + 1 + CHUNKS))
            plan(SECOND)
            experts(SECOND)

        @block.tensor
        def _(pe):
            def turn(src):
                for j in range(TPC):
                    last = nc.tensor.transpose(ps_t[:, j * P:(j + 1) * P], src[:, j, 0:D], ident)
                return last

            def bias(dst, column, width, stop):
                return nc.tensor.matmul(dst, ones_bf[:], bias_rows[:, bass.ds(column, width)], start=False, stop=stop)

            def attention_in(b, c):
                n1 = b * HALVES + (c + 1)
                pe.wait_ge(h_ready, n1)
                if c:
                    pe.wait_ge(qft_ready, n1 - 1)
                turn(hmix).then_inc(h_turned, 1)
                pe.wait_ge(ht_ready, n1)
                if c:
                    pe.wait_ge(v_ready, n1 - 1)
                for j in range(TPC):
                    nc.tensor.matmul(quad[:, j, 0:3 * D], hmix_t[:, j * P:(j + 1) * P], wqkv_sb[:], start=True, stop=False)
                    last = bias(quad[:, j, 0:3 * D], B_QKV, 3 * D, True)
                last.then_inc(qkv_ready, 1)
                pe.wait_ge(kf_ready, n1)
                pe.wait_ge(v_ready, n1)
                for j in range(TPC):
                    last = nc.tensor.matmul(ps_vk[:, 0:D + 1], kf[c][:, j, :], vpad[c][:, j, :],
                                            start=(c == 0 and j == 0), stop=(c == HALVES - 1 and j == TPC - 1))
                if c == HALVES - 1:
                    last.then_inc(vk_ready, 1)
                pe.wait_ge(qf_ready, n1)
                turn(qf[c]).then_inc(qf_turned, 1)

            def attention_out(b, c):
                n1 = b * HALVES + (c + 1)
                if c == 0:
                    pe.wait_ge(state_ready, b + 1)
                    pe.wait_ge(qft_ready, n1 + 1)
                for j in range(TPC):
                    last = nc.tensor.matmul(ps_res[:, j, 0:RES_W], qf_t[c][:, j * P:(j + 1) * P], state[:],
                                            start=True, stop=True)
                last.then_inc(res_ready, 1)
                pe.wait_ge(attn_ready, n1)
                turn(attn).then_inc(attn_turned, 1)
                pe.wait_ge(attnt_ready, n1)
                for j in range(TPC):
                    nc.tensor.matmul(ps_out4[:, j, :], attn_t[:, j * P:(j + 1) * P], wout_sb[:], start=True, stop=False)
                    last = bias(ps_out4[:, j, :], B_OUT, D, True)
                last.then_inc(out_ready, 1)

            def route(c, n1):
                pe.wait_ge(h2_ready, n1)
                turn(hffn[c]).then_inc(h2_turned, 1)
                pe.wait_ge(h2t_ready, n1)
                for j in range(TPC):
                    last = nc.tensor.matmul(ps_score[:, j, :], hffn_t[:, j * P:(j + 1) * P], wrouter_sb[:], start=True, stop=True)
                last.then_inc(score_ready, 1)
                pe.wait_ge(member_ready, n1)
                nc.tensor.matmul(ps_rank, tri_bf[:], member[:], start=True, stop=False)
                for j in range(TPC - 1):
                    left = TPC - 1 - j
                    nc.tensor.matmul(ps_rank[:, j + 1:, :], ones_bf[:],
                                     member[:, j:j + 1, :].to_broadcast([P, left, NE]), start=False, stop=False)
                nc.tensor.matmul(ps_rank, ones_bf[:], seen[:, None, :].to_broadcast([P, TPC, NE]),
                                 start=False, stop=True).then_inc(rank_ready, 1)

            def plan(f):
                pe.wait_ge(seen_ready, (f + 1) * CHUNKS)
                nc.tensor.matmul(ps_count, ones_bf[:], seen[:], start=True, stop=True).then_inc(count_ready, 1)

            def experts(f):
                T, G, B = f * N_TURN, f * N_GATE, f * N_BACK
                loads = f * (LOADED // STEP)

                def expert(t):
                    return pe.value_load(tile_expert[0:1, bass.ds(t, 1)], min_val=0, max_val=NE - 1)

                def turn_x(i, nload):
                    pe.wait_ge(xtile_in[i], nload)
                    nc.tensor.transpose(ps_xt[i % 2][:, 0:P], xtile[i][:, 0:D], ident).then_inc(xtile_turned, 1)

                def up(i, e, n1):
                    pe.wait_ge(xtilet_ready, n1)
                    nc.tensor.matmul(ps_up[i], xtile_t[i][:], wup_sb[:, bass.ds(e * (2 * HID), 2 * HID)], start=True, stop=False)
                    bias(ps_up[i], e * (2 * HID) + B_UP, 2 * HID, True).then_inc(up_ready, 1)

                def turn_gated(i, n1):
                    pe.wait_ge(gated_ready, n1)
                    for h in range(HCH):
                        last = nc.tensor.transpose(ps_gt[i][:, h * P:(h + 1) * P], gated[i][:, h * P:(h + 1) * P], ident)
                    last.then_inc(gated_turned, 1)

                def down(i, e, n1):
                    pe.wait_ge(gatedt_ready, n1)
                    for h in range(HCH):
                        nc.tensor.matmul(ps_y[i][:, 0:D], gated_t[i][:, h * P:(h + 1) * P],
                                         wdown_sb[:, bass.ds(e * (HCH * D) + h * D, D)], start=(h == 0), stop=False)
                    bias(ps_y[i][:, 0:D], e * D + B_DOWN, D, True).then_inc(y_ready, 1)

                pe.wait_ge(table_ready, f + 1)
                for t in range(2):
                    turn_x(t, 16 * (1 + loads))
                up(0, expert(0), 1 + T)
                turn_x(2, 16 * (1 + loads))
                up(1, expert(1), 2 + T)
                turn_gated(0, 1 + G)
                with pe.Fori(0, XTILES // STEP) as n:
                    e = [expert(n * STEP + t) for t in range(2)]
                    for i in range(STEP):
                        e.append(expert(n * STEP + (i + 2)))
                        turn_x((i + 3) % STEP, (n + ((i + 3) // STEP + 1 + loads)) * 16)
                        up(i % 2, e[i + 2], n * STEP + (i + 3 + T))
                        turn_gated((i + 1) % 2, n * STEP + (i + 2 + G))
                        down(i % 2, e[i], n * STEP + (i + 1 + B))

            def mixing(b, c):
                n1 = b * HALVES + (c + 1)
                pe.wait_ge(h3_ready, n1)
                turn(hmix).then_inc(h3_turned, 1)
                pe.wait_ge(hseq_ready, n1)
                for i, dst in enumerate((ps_k, ps_v, ps_r)):
                    nc.tensor.matmul(dst, wnow_sb[:, i, :], hseq[:, 1 + c * CHUNK:1 + (c + 1) * CHUNK], start=True, stop=False)
                    last = nc.tensor.matmul(dst, wpast_sb[:, i, :], hseq[:, c * CHUNK:(c + 1) * CHUNK], start=False, stop=True)
                last.then_inc(kvr_ready, 1)
                pe.wait_ge(rwkv_ready, n1)
                for j in range(TPC):
                    last = nc.tensor.matmul(ps_out4[:, j, :], rwkv[:, j * P:(j + 1) * P], wo_sb[:], start=True, stop=True)
                last.then_inc(mixed_ready, 1)

            pe.wait_ge(setup_done, 2)
            pe.wait_ge(weights_in, 16 * len(WEIGHTS))
            pe.wait_ge(rows_in, 16)
            with pe.Fori(0, BATCH) as b:
                for c in range(HALVES):
                    attention_in(b, c)
                for c in range(HALVES):
                    attention_out(b, c)
                    route(c, b * HALVES + (c + 1))
            plan(FIRST)
            experts(FIRST)
            with pe.Fori(0, BATCH) as b:
                for c in range(HALVES):
                    mixing(b, c)
                    route(c, b * HALVES + (c + 1 + CHUNKS))
            plan(SECOND)
            experts(SECOND)

        @block.vector
        def _(dve):
            step = [0]

            def begin():
                dve.sem_clear(dve_step)
                step[0] = 0

            def settle(ins):
                step[0] += 1
                ins.then_inc(dve_step, 1)
                dve.wait_ge(dve_step, step[0])

            dve.wait_ge(bias_in, 16)
            settle(nc.vector.tensor_copy(bias_parts[:, 0, :], bias_sb[:]))
            settle(nc.vector.tensor_tensor(bias_left[:], bias_sb[:], bias_parts[:, 0, :], ALU.subtract))
            settle(nc.vector.tensor_copy(bias_parts[:, 1, :], bias_left[:]))
            settle(nc.vector.tensor_tensor(bias_left[:], bias_left[:], bias_parts[:, 1, :], ALU.subtract))
            nc.vector.tensor_copy(bias_parts[:, 2, :], bias_left[:]).then_inc(split_done, 1)
            nc.vector.memset(bias_rows[:], 0.0)
            nc.vector.memset(ones_bf[:], 1.0)
            nc.vector.memset(ones8[:], 1.0)
            nc.vector.memset(ln_eps[:], LN_EPS)
            nc.vector.memset(rms_eps[:], RMS_EPS)
            nc.vector.memset(tail_rows[:, 0:D], 0.0)
            nc.vector.memset(tail_rows[:, D + 1:ROW_W], -1.0)
            nc.vector.memset(hseq[:, 0:1], 0.0)
            nc.vector.memset(top[:, 0:1], NO_PAST)
            nc.vector.memset(num[:, 0:1], 0.0)
            nc.vector.memset(den[:, 0:1], 0.0)
            for c in range(HALVES):
                nc.vector.memset(vpad[c][:], 1.0)
            dve.wait_ge(weights_in, 16 * len(WEIGHTS))
            nc.vector.tensor_scalar(tail_rows[:, D:D + 1], k_sb[:, K_PART:K_PART + 1], float(NO_RESULT), None, ALU.add)
            nc.vector.tensor_copy(tri_bf[:], k_sb[:, K_TRI:K_TRI + P]).then_inc(setup_done, 1)
            dve.wait_ge(rope_in, 16 * len(ROPE))
            for half in range(2):
                cols = slice(half * D, (half + 1) * D)
                for table, src, g in ((rope_c, cos_sb, gqk_sb), (rope_s, sin_sb, gqks_sb)):
                    nc.vector.tensor_tensor(table[:, :, cols], src, g[:, None, cols].to_broadcast([P, SEQ // P, D]), ALU.mult)
            settle(nc.vector.tensor_scalar(mix_left[:], ch_sb[:, V_MIXK:V_MIXR + 1], -1.0, 1.0, ALU.mult, ALU.add))
            for i in range(3):
                nc.vector.tensor_scalar(wnow_sb[:, i, :], wkvr_sb[:, i, :], ch_sb[:, V_MIXK + i:V_MIXK + i + 1], None, ALU.mult)
                nc.vector.tensor_scalar(wpast_sb[:, i, :], wkvr_sb[:, i, :], mix_left[:, i:i + 1], None, ALU.mult)
            dve.wait_ge(decay_ready, 1)
            nc.vector.tensor_scalar(w_sb[:], exp_decay[:], -1.0, None, ALU.mult).then_inc(setup_done, 1)
            dve.wait_ge(setup_done, 2)

            def layernorm(src, dst, var, dev, normed, n1):
                for j in range(TPC):
                    last = nc.vector.bn_stats(stats[:, j, :], src[:, j, :])
                settle(last)
                for j in range(TPC):
                    last = nc.vector.bn_aggr(meanvar[:, j, :], stats[:, j, :])
                last.then_inc(var, 1)
                dve.wait_ge(dev, n1)
                settle(nc.vector.reciprocal(rstd[:], deviation[:]))
                for j in range(TPC):
                    last = nc.vector.tensor_scalar(dst[:, j, 0:D], src[:, j, :], meanvar[:, j, 0:1], rstd[:, j:j + 1],
                                                   ALU.subtract, ALU.mult)
                last.then_inc(normed, 1)

            def route(b, c, n1, chunk, f):
                dve.wait_ge(queued[c], (b + f * BATCH) * SCATTERS + 16)
                layernorm(xres[c], hffn[c], var2_ready, dev2_ready, h2_ready, n1)
                dve.wait_ge(score_ready, n1)
                settle(nc.vector.tensor_tensor(score[:], ps_score, rows_sb[:, None, 0:NE].to_broadcast([P, TPC, NE]), ALU.add))
                settle(nc.vector.tensor_tensor(biased[:], score[:], rows_sb[:, None, NE:2 * NE].to_broadcast([P, TPC, NE]), ALU.add))
                nc.vector.tensor_copy(score_all[:, bass.ds(chunk * TPC, TPC), :], score[:])
                nc.vector.tensor_copy(hffn[c][:, :, D], k_sb[:, bass.ds(chunk * TPC + K_TOKEN, TPC)])
                for j in range(TPC):
                    last = nc.vector.max(top8[:, j, :], biased[:, j, :])
                settle(last)
                for j in range(TPC):
                    last = nc.vector.max_index(top_at[:, j, :], top8[:, j, :], biased[:, j, :])
                settle(last)
                settle(nc.vector.tensor_copy(top_f[:], top_at[:, :, 0:TOPK]))
                nc.vector.tensor_copy(hffn[c][:, :, D + 1], top_f[:, :, 1])
                settle(nc.vector.tensor_tensor(
                    onehot[:], top_f[:, :, :, None].to_broadcast([P, TPC, TOPK, NE]),
                    k_sb[:, None, None, K_IOTA:K_IOTA + NE].to_broadcast([P, TPC, TOPK, NE]), ALU.is_equal))
                nc.vector.tensor_tensor(member[:], onehot[:, :, 0, :], onehot[:, :, 1, :], ALU.add).then_inc(member_ready, 1)
                nc.vector.tensor_copy(onehot_all[:, bass.ds(chunk * TPC, TPC), :, :], onehot[:])
                dve.wait_ge(rank_ready, n1)
                nc.vector.tensor_reduce(seen_new[:], member[:].rearrange("p j e -> p e j"), AX.X, ALU.add)
                settle(nc.vector.tensor_tensor(place8[:], ps_rank, k_sb[:, None, K_REGION:K_REGION + NE].to_broadcast([P, TPC, NE]), ALU.add))
                nc.vector.tensor_tensor(seen[:], seen[:], seen_new[:], ALU.add).then_inc(seen_ready, 1)
                settle(nc.vector.tensor_tensor(picked[:], onehot[:], place8[:, :, None, :].to_broadcast([P, TPC, TOPK, NE]), ALU.mult))
                settle(nc.vector.tensor_reduce(place_f[:], picked[:], AX.X, ALU.add))
                nc.vector.tensor_copy(place_i[c][:], place_f[:].rearrange("p j k -> p (j k)")).then_inc(place_ready, 1)

            def plan(f):
                begin()
                dve.wait_ge(count_ready, f + 1)
                settle(nc.vector.tensor_copy(count[:], ps_count))
                nc.vector.memset(seen[:], 0.0)
                nc.vector.tensor_scalar(tail_f[:], count[:], k_sb[:, K_PART:K_PART + 1], None, ALU.add)
                settle(nc.vector.tensor_scalar(count_i[:], count[:], float(P - 1), None, ALU.add))
                nc.vector.tensor_tensor(tail_f[:], tail_f[:], k_sb[:, K_REGION:K_REGION + NE], ALU.add)
                settle(nc.vector.tensor_scalar(ntile_i[:], count_i[:], P.bit_length() - 1, None, ALU.arith_shift_right))
                nc.vector.tensor_copy(tail_i[:], tail_f[:]).then_inc(tail_ready, 1)
                settle(nc.vector.tensor_copy(ntile[:], ntile_i[:]))
                settle(nc.vector.tensor_tensor_scan(cum[:], ones8[:], ntile[:], 0.0, ALU.mult, ALU.add))
                nc.vector.tensor_scalar(cum_rows[:], cum[:], float(P), None, ALU.mult)
                nc.vector.tensor_scalar(jump[:], ntile[:], -float(P), float(REGION), ALU.mult, ALU.add)
                settle(nc.vector.tensor_scalar(last_row[:], count[:, NE - 1:NE], float((NE - 1) * REGION), None, ALU.add))
                tile_at = k_sb[:, K_TILE:K_TILE + LOADED]
                shape = [P, NE - 1, LOADED]
                settle(nc.vector.tensor_tensor(past, tile_at[:, None, :].to_broadcast(shape),
                                               cum_rows[:, 0:NE - 1, None].to_broadcast(shape), ALU.is_ge))
                settle(nc.vector.tensor_tensor(past_j[0:1], past[0:1], jump[0:1, 0:NE - 1, None].to_broadcast([1, NE - 1, LOADED]), ALU.mult))
                nc.vector.tensor_reduce(expert_all[:], past.rearrange("p e t -> p t e"), AX.X, ALU.add)
                settle(nc.vector.tensor_reduce(row_f[:], past_j[0:1].rearrange("p e t -> p t e"), AX.X, ALU.add))
                nc.vector.tensor_copy(tile_expert[:], expert_all[0:1, :])
                settle(nc.vector.tensor_tensor(row_g[:], row_f[:], tile_at[0:1], ALU.add))
                nc.vector.tensor_scalar(tile_row[:], row_g[:], last_row[0:1, :], None, ALU.min).then_inc(table_ready, 1)
                settle(nc.vector.tensor_reduce(top_all[:], score_all[:], AX.X, ALU.max))
                nc.vector.tensor_tensor(small_a[:], score_all[:], top_all[:, :, None].to_broadcast([P, TILES, NE]), ALU.subtract).then_inc(gate_in, 1)
                dve.wait_ge(gate_exp, f + 1)
                settle(nc.vector.tensor_tensor(big[:], onehot_all[:], small_a[:, :, None, :].to_broadcast([P, TILES, TOPK, NE]), ALU.mult))
                settle(nc.vector.tensor_reduce(gate_w[:], big[:], AX.X, ALU.add))
                settle(nc.vector.tensor_tensor(gate_sum[:], gate_w[:, :, 0], gate_w[:, :, 1], ALU.add))
                settle(nc.vector.reciprocal(gate_sum[:], gate_sum[:]))
                settle(nc.vector.tensor_tensor(gate_all[:], gate_w[:], gate_sum[:, :, None].to_broadcast([P, TILES, TOPK]), ALU.mult))

            def experts(f):
                U, G = f * N_UP, f * N_GATE

                def place(i, t, n):
                    dve.wait_ge(xtile_in[i], (n + (1 + f * (LOADED // STEP))) * 16)
                    dve.wait_ge(y_stored[i], (n + (1 + f * (N_BACK // STEP))) * 16)
                    nc.vector.scalar_tensor_tensor(result_row[i][:], xtile[i][:, D + 1:ROW_W], expert_all[:, bass.ds(t, 1)],
                                                   xtile[i][:, D:D + 1], ALU.is_equal, ALU.add)

                def gate_up(i, n1):
                    dve.wait_ge(silu_ready, n1)
                    nc.vector.tensor_tensor(gated[i][:], silu[i][:], ps_up[i][:, HID:2 * HID], ALU.mult).then_inc(gated_ready, 1)

                def turn(i, n1):
                    dve.wait_ge(gated_turned, n1)
                    nc.vector.tensor_copy(gated_t[i][:], ps_gt[i][:, 0:HID]).then_inc(gatedt_ready, 1)

                place(0, 0, 0)
                gate_up(0, 1 + U)
                with dve.Fori(0, XTILES // STEP) as n:
                    for i in range(STEP):
                        turn(i % 2, n * STEP + (i + 1 + G))
                        place((i + 1) % STEP, n * STEP + (i + 1), n + (i + 1) // STEP)
                        gate_up((i + 1) % 2, n * STEP + (i + 2 + U))

            def combine(b, c, f):
                n = b * HALVES + c
                settle(nc.vector.tensor_copy(gate[:].rearrange("p (j k) -> p j k", k=TOPK), gate_all[:, bass.ds(n * TPC, TPC), :]))
                dve.wait_ge(x_loaded[c], (b + (1 + (f + 1) * BATCH)) * 16)
                dve.wait_ge(results_in[c], (b + (1 + f * BATCH)) * 16)
                if f == SECOND:
                    dve.wait_ge(out_stored[c], (b + 1) * 16)
                for k in range(TOPK):
                    for j in range(TPC):
                        m = j * TOPK + k
                        last = nc.vector.scalar_tensor_tensor(xmid[c][:, j, :], back_x[c][:, m, :], gate[:, m:m + 1],
                                                              (xin if k == 0 else xmid)[c][:, j, :], ALU.mult, ALU.add)
                    if k == 0:
                        settle(last)
                last.then_inc(combined, 1)
                dve.wait_ge(combined, b * HALVES + (c + 1 + f * CHUNKS))

            def attention_in(b, c):
                n1 = b * HALVES + (c + 1)
                dve.wait_ge(x_loaded[c], (b + 1) * 16)
                layernorm(xin[c], hmix, var_ready, dev_ready, h_ready, n1)
                dve.wait_ge(qk_ready, n1)
                at = slice(c * TPC, (c + 1) * TPC)
                nc.vector.tensor_tensor(rope1[:], qk[:], rope_c[:, at, :], ALU.mult)
                pairs = lambda a: a.rearrange("p j (m r) -> p j m r", r=2)
                a, s, o = pairs(qk[:]), pairs(rope_s[:, at, :]), pairs(rope2[:])
                for r in range(2):
                    last = nc.vector.tensor_tensor(o[:, :, :, r], a[:, :, :, 1 - r], s[:, :, :, r], ALU.mult)
                settle(last)
                settle(nc.vector.tensor_tensor(rope1[:], rope1[:], rope2[:], ALU.add))
                dve.wait_ge(qkdev_ready, n1)
                settle(nc.vector.reciprocal(qk_rstd[:], qk_dev[:]))
                for half, dst, ready in ((1, kf[c], kf_ready), (0, qf[c], qf_ready)):
                    for j in range(TPC):
                        last = nc.vector.tensor_scalar(dst[:, j, :], rope1[:, j, half * D:(half + 1) * D],
                                                       qk_rstd[:, half, j:j + 1], 0.0, ALU.mult, ALU.max)
                    last.then_inc(ready, 1)

            def attention_out(b, c):
                n1 = b * HALVES + (c + 1)
                dve.wait_ge(res_ready, n1)
                settle(nc.vector.tensor_scalar(den_a[:], ps_res[:, :, D:RES_W], LIN_EPS, None, ALU.add))
                settle(nc.vector.reciprocal(rden[:], den_a[:]))
                heads = lambda a: a.rearrange("p j (h d) -> p j h d", d=DH)
                nc.vector.tensor_tensor(heads(attn[:]), heads(ps_res[:, :, 0:D]),
                                        rden[:, :, :, None].to_broadcast([P, TPC, HEADS, DH]), ALU.mult).then_inc(attn_ready, 1)
                dve.wait_ge(out_ready, n1)
                dve.wait_ge(odev_ready, n1)
                settle(nc.vector.reciprocal(o_rstd[:], o_dev[:]))
                for j in range(TPC):
                    last = nc.vector.scalar_tensor_tensor(onorm[:, j, :], ps_out4[:, j, :], o_rstd[:, j:j + 1], gout_sb[:], ALU.mult, ALU.mult)
                settle(last)
                dve.wait_ge(x_stored[c], (b + 1) * 16)
                nc.vector.tensor_tensor(xres[c][:], onorm[:], xin[c][:], ALU.add).then_inc(xres_ready, 1)
                dve.wait_ge(xres_ready, n1)

            def attention(b):
                begin()
                for c in range(HALVES):
                    attention_in(b, c)
                dve.wait_ge(vk_ready, b + 1)
                nc.vector.tensor_tensor(state[:, 0:D], ps_vk[:, 0:D], k_sb[:, K_BLOCK:K_BLOCK + P], ALU.mult)
                nc.vector.tensor_scalar(state[:, D:RES_W], k_sb[:, K_HEAD:K_HEAD + HEADS], ps_vk[:, D:D + 1], None, ALU.mult).then_inc(state_ready, 1)
                for c in range(HALVES):
                    attention_out(b, c)
                    route(b, c, b * HALVES + (c + 1), b * HALVES + c, FIRST)

            def mixing(b, c):
                n1 = b * HALVES + (c + 1)
                layernorm(xmid[c], hmix, var3_ready, dev3_ready, h3_ready, n1)
                before = slice(c * CHUNK, (c + 1) * CHUNK)
                after = slice(1 + c * CHUNK, 1 + (c + 1) * CHUNK)
                first = ch_sb[:, V_FIRST:V_FIRST + 1]
                dve.wait_ge(kvr_ready, n1)
                settle(nc.vector.tensor_tensor_scan(top[:, after], w_sb[:].to_broadcast([P, CHUNK]), ps_k,
                                                    top[:, c * CHUNK:c * CHUNK + 1], ALU.add, ALU.max))
                settle(nc.vector.scalar_tensor_tensor(qmax, ps_k, first, top[:, before], ALU.add, ALU.max))
                nc.vector.scalar_tensor_tensor(expo[:, 2, :], top[:, before], w_sb[:, 0:1], top[:, after], ALU.add, ALU.subtract)
                nc.vector.tensor_tensor(expo[:, 3, :], ps_k, top[:, after], ALU.subtract)
                nc.vector.tensor_tensor(expo[:, 0, :], top[:, before], qmax, ALU.subtract)
                nc.vector.scalar_tensor_tensor(expo[:, 1, :], ps_k, first, qmax, ALU.add, ALU.subtract).then_inc(expo_ready, 1)
                dve.wait_ge(ex_ready, n1)
                settle(nc.vector.tensor_tensor(ev, ex[:, 3, :], ps_v, ALU.mult))
                nc.vector.tensor_tensor_scan(num[:, after], ex[:, 2, :], ev, num[:, c * CHUNK:c * CHUNK + 1], ALU.mult, ALU.add)
                settle(nc.vector.tensor_tensor_scan(den[:, after], ex[:, 2, :], ex[:, 3, :], den[:, c * CHUNK:c * CHUNK + 1], ALU.mult, ALU.add))
                nc.vector.tensor_tensor(y_num, ex[:, 0, :], num[:, before], ALU.mult)
                nc.vector.tensor_tensor(y_b, ex[:, 1, :], ps_v, ALU.mult)
                settle(nc.vector.tensor_tensor(y_den, ex[:, 0, :], den[:, before], ALU.mult))
                nc.vector.tensor_tensor(y_num, y_num, y_b, ALU.add)
                settle(nc.vector.tensor_tensor(y_den, y_den, ex[:, 1, :], ALU.add))
                dve.wait_ge(er_ready, n1)
                settle(nc.vector.scalar_tensor_tensor(y_den, e_r, 1.0, y_den, ALU.add, ALU.mult))
                settle(nc.vector.reciprocal(y_den, y_den))
                nc.vector.tensor_tensor(rwkv[:], y_num, y_den, ALU.mult).then_inc(rwkv_ready, 1)
                dve.wait_ge(mixed_ready, n1)
                dve.wait_ge(x_stored[c], (b + (1 + BATCH)) * 16)
                nc.vector.tensor_tensor(xres[c][:], ps_out4, xmid[c][:], ALU.add).then_inc(xres_ready, 1)
                dve.wait_ge(xres_ready, n1 + CHUNKS)

            nc.vector.memset(seen[:], 0.0)
            for c in range(HALVES):
                dve.sem_inc(x_stored[c], 16)
                dve.sem_inc(out_stored[c], 16)
            with dve.Fori(0, BATCH) as b:
                attention(b)
            plan(FIRST)
            experts(FIRST)
            with dve.Fori(0, BATCH) as b:
                begin()
                for c in range(HALVES):
                    combine(b, c, FIRST)
                    mixing(b, c)
                    route(b, c, b * HALVES + (c + 1 + CHUNKS), b * HALVES + c, SECOND)
            plan(SECOND)
            experts(SECOND)
            with dve.Fori(0, BATCH) as b:
                begin()
                for c in range(HALVES):
                    combine(b, c, SECOND)


def kernel(**inputs):
    import numpy as np
    import concourse.bacc as bacc
    from concourse.bass_utils import run_bass_kernel_spmd

    def wide(v):
        return np.ascontiguousarray(np.broadcast_to(v.reshape(1, -1), (P, v.size)))

    def dense(a):
        return np.ascontiguousarray(a)

    a = {k: np.asarray(v) for k, v in inputs.items()}
    at = lambda name: a["L0_attn_a_" + name]
    mt = lambda name: a["L0_attn_b_" + name]
    ff = lambda name: a["L0_ffn_" + name]

    freq = (1.0 / np.float32(10000.0) ** (np.arange(0, DH, 2, dtype=np.float32) / np.float32(DH))).astype(np.float32)
    angle = np.outer(np.arange(SEQ, dtype=np.float32), freq)
    by_feature = lambda t: dense(np.tile(np.repeat(t, 2, axis=1), (1, HEADS)).reshape(SEQ // P, P, D).transpose(1, 0, 2))
    sign = np.tile(np.array([-1.0, 1.0], np.float32), D // 2)
    cosine = by_feature(np.cos(angle).astype(np.float32))
    sine = dense(by_feature(np.sin(angle).astype(np.float32)) * sign)

    consts = np.zeros((P, K_ALL), np.float32)
    part, feature = np.arange(P), np.arange(D)
    consts[:, K_ID:K_ID + P] = np.eye(P)
    consts[:, K_TRI:K_TRI + P] = np.triu(np.ones((P, P)), 1)
    consts[:, K_BLOCK:K_BLOCK + P] = feature[:, None] // DH == feature[None, :] // DH
    consts[:, K_HEAD:K_HEAD + HEADS] = feature[:, None] // DH == np.arange(HEADS)[None, :]
    consts[:, K_IOTA:K_IOTA + NE] = np.arange(NE)
    consts[:, K_REGION:K_REGION + NE] = np.arange(NE) * REGION
    consts[:, K_PART] = part
    consts[:, K_TILE:K_TILE + LOADED] = np.arange(LOADED) * P
    consts[:, K_TOKEN:K_TOKEN + TILES] = (np.arange(TILES)[None, :] * P + part[:, None]) * TOPK

    swap = lambda g: g.reshape(-1, 2)[:, ::-1].reshape(-1)
    biases = np.concatenate([at("bqkv"), at("bout"), ff("bl1").reshape(-1), ff("bl2").reshape(-1)])
    arrays = {
        "x": dense(at("x").reshape(TOKENS, D)),
        "cosine": cosine, "sine": sine, "consts": consts,
        "w_qkv": dense(at("Wqkv").T), "w_out": dense(at("Wout").T),
        "g_qk": wide(np.concatenate([at("gq"), at("gk")])),
        "g_qk_swapped": wide(np.concatenate([swap(at("gq")), swap(at("gk"))])),
        "g_out": wide(at("gout")), "bias_cols": dense(biases.reshape(P, B_ALL // P)),
        "w_router": dense(ff("Wr").T), "router_rows": wide(np.concatenate([ff("br"), ff("biases_N")])),
        "w_up": dense(ff("Wl1").transpose(1, 0, 2).reshape(D, -1)),
        "w_down": dense(ff("Wl2").reshape(NE, HCH, P, D).transpose(2, 0, 1, 3).reshape(P, -1)),
        "channel": dense(np.stack([mt("time_decay"), mt("time_first"), mt("time_mix_k").reshape(-1),
                                   mt("time_mix_v").reshape(-1), mt("time_mix_r").reshape(-1)], axis=1)),
        "w_k": dense(mt("Wk").T), "w_v": dense(mt("Wv").T), "w_r": dense(mt("Wr").T), "w_o": dense(mt("Wo").T),
    }
    nc = bacc.Bacc("TRN2", target_bir_lowering=False, num_devices=1)
    args = {name: nc.dram_tensor(name, v.shape, mybir.dt.from_np(v.dtype), kind="ExternalInput").ap()
            for name, v in arrays.items()}
    out = nc.dram_tensor("out", (TOKENS, D), F32, kind="ExternalOutput").ap()
    program(nc, out=out, **args)
    result = run_bass_kernel_spmd(nc, [arrays], core_ids=[0])
    return result.results[0]["out"].reshape(BATCH, SEQ, D)
```

```python
from contextlib import ExitStack

import concourse.bass as bass
from concourse import mybir

F32 = mybir.dt.float32
BF16 = mybir.dt.bfloat16
I32 = mybir.dt.int32
U32 = mybir.dt.uint32
ALU = mybir.AluOpType
ACT = mybir.ActivationFunctionType
AX = mybir.AxisListType

P = 128
BATCH, SEQ, D = 8, 1024, 128
TOKENS = BATCH * SEQ
TPC = 4
CHUNK = TPC * P
HALVES = SEQ // CHUNK
CHUNKS = TOKENS // CHUNK
TILES = TOKENS // P
HEADS, DH = 16, 8
NE, TOPK, HID = 8, 2, 256
HCH = HID // P
ROW_W = D + 2
NO_RESULT = TOKENS * TOPK
REGION = TOKENS + P
STEP = 8
XTILES = -(-(TOKENS * TOPK // P + NE - 1) // STEP) * STEP
LOADED = XTILES + STEP
RES_W = D + HEADS
BT = HALVES * TPC
LN_EPS, RMS_EPS, LIN_EPS = 1e-5, 1.1920929e-07, 1e-6
NO_PAST = -1e38

B_QKV, B_OUT = 0, 3 * D
B_UP, B_DOWN = B_OUT + D, B_OUT + D + NE * 2 * HID
B_ALL = B_DOWN + NE * D

K_ID, K_TRI, K_BLOCK = 0, P, 2 * P
K_HEAD = 3 * P
K_IOTA = K_HEAD + HEADS
K_REGION = K_IOTA + NE
K_PART = K_REGION + NE
K_TILE = K_PART + 1
K_TOKEN = K_TILE + LOADED
K_ALL = K_TOKEN + TILES

V_DECAY, V_FIRST, V_MIXK, V_MIXV, V_MIXR = range(5)


def program(nc, x, cosine, sine, consts, w_qkv, w_out, g_qk, g_qk_swapped, g_out, bias_cols, w_router,
            router_rows, w_up, w_down, channel, w_k, w_v, w_r, w_o, out):
    with ExitStack() as ctx:
        def sb(name, shape, dt=F32):
            return ctx.enter_context(nc.sbuf_tensor(name, shape, dt))

        def sem(name):
            return ctx.enter_context(nc.semaphore(name))

        def sem2(name):
            return [sem(f"{name}{c}") for c in range(HALVES)]

        def dram(name, shape, dt=F32):
            return nc.dram_tensor(name, shape, dt).ap()

        x1_dram = dram("x1_dram", [TOKENS, D])
        x3_dram = dram("x3_dram", [TOKENS, D])
        queue_dram = dram("queue_dram", [NE * REGION, ROW_W])
        result_dram = dram("result_dram", [NO_RESULT + P + STEP, D])
        split_dram = dram("split_dram", [3, B_ALL], BF16)

        k_sb = sb("k_sb", [P, K_ALL])
        wqkv_sb = sb("wqkv_sb", [P, 3 * D])
        wout_sb = sb("wout_sb", [P, D])
        wrouter_sb = sb("wrouter_sb", [P, NE])
        rows_sb = sb("rows_sb", [P, 2 * NE])
        wup_sb = sb("wup_sb", [P, NE * 2 * HID])
        wdown_sb = sb("wdown_sb", [P, NE * HCH * D])
        gqk_sb = sb("gqk_sb", [P, 2 * D])
        gqks_sb = sb("gqks_sb", [P, 2 * D])
        gout_sb = sb("gout_sb", [P, D])
        expo = sb("expo", [P, 4, SEQ])
        cos_sb, sin_sb = (expo[:, i, :].rearrange("p (t d) -> p t d", d=D) for i in range(2))
        past, past_j = (expo[:, i, 0:(NE - 1) * LOADED].rearrange("p (e t) -> p e t", e=NE - 1) for i in (2, 3))
        rope_c = sb("rope_c", [P, SEQ // P, 2 * D])
        rope_s = sb("rope_s", [P, SEQ // P, 2 * D])
        bias_sb = sb("bias_sb", [P, B_ALL // P])
        bias_left = sb("bias_left", [P, B_ALL // P])
        bias_parts = sb("bias_parts", [P, 3, B_ALL // P], BF16)
        bias_rows = sb("bias_rows", [P, B_ALL], BF16)
        ones_bf = sb("ones_bf", [P, P], BF16)
        tri_bf = sb("tri_bf", [P, P], BF16)
        ones8 = sb("ones8", [P, NE])
        ln_eps = sb("ln_eps", [P, 1])
        rms_eps = sb("rms_eps", [P, 1])
        ch_sb = sb("ch_sb", [P, 5])
        w_sb = sb("w_sb", [P, 1])
        exp_decay = sb("exp_decay", [P, 1])
        mix_left = sb("mix_left", [P, 3])
        wkvr_sb = sb("wkvr_sb", [P, 3, D])
        wnow_sb = sb("wnow_sb", [P, 3, D])
        wpast_sb = sb("wpast_sb", [P, 3, D])
        wo_sb = sb("wo_sb", [P, D])
        tail_rows = sb("tail_rows", [P, ROW_W])
        ident = k_sb[:, K_ID:K_ID + P]

        halves = lambda name, shape, dt=F32: [sb(f"{name}{c}", shape, dt) for c in range(HALVES)]
        xin = halves("xin", [P, TPC, D])
        xold = halves("xold", [P, TPC, D])
        xmid = halves("xmid", [P, TPC, D])
        xres = halves("xres", [P, TPC, D])
        hmix = halves("hmix", [P, TPC, D])
        hffn = halves("hffn", [P, TPC, ROW_W])
        stats = halves("stats", [P, TPC, 6])
        moment = halves("moment", [P, TPC, 2])
        dev = halves("dev", [P, TPC])
        rstd = halves("rstd", [P, TPC])
        stats2 = halves("stats2_", [P, TPC, 6])
        moment2 = halves("moment2_", [P, TPC, 2])
        dev2 = halves("dev2_", [P, TPC])
        rstd2 = halves("rstd2_", [P, TPC])
        hmix_t = halves("hmix_t", [P, CHUNK])
        hffn_t = halves("hffn_t", [P, CHUNK])

        qkv = halves("qkv", [P, TPC, 3 * D + 1])
        rope1 = sb("rope1", [P, TPC, 2 * D])
        rope2 = sb("rope2", [P, TPC, 2 * D])
        qf = halves("qf", [P, TPC, D])
        num = sb("num", [P, 1 + SEQ])
        den = sb("den", [P, 1 + SEQ])
        kf, onorm = ([a[:, 1 + c * CHUNK:1 + (c + 1) * CHUNK].rearrange("p (j d) -> p j d", d=D) for c in range(HALVES)]
                     for a in (num, den))
        qf_t = halves("qf_t", [P, CHUNK])
        squares = sb("squares", [P, 2, TPC, D])
        out_squares = sb("out_squares", [P, TPC, D])
        sumsq = halves("sumsq", [P, 2, TPC])
        qk_dev = halves("qk_dev", [P, 2, TPC])
        qk_rstd = halves("qk_rstd", [P, 2, TPC])
        state = sb("state", [P, RES_W])
        den_a = halves("den_a", [P, TPC, HEADS])
        rden = halves("rden", [P, TPC, HEADS])
        attn = halves("attn", [P, TPC, D])
        attn_t = halves("attn_t", [P, CHUNK])
        out_sum = halves("out_sum", [P, TPC])
        out_dev = halves("out_dev", [P, TPC])
        out_rstd = halves("out_rstd", [P, TPC])

        score = sb("score", [P, BT, NE])
        biased = sb("biased", [P, BT, NE])
        top8 = sb("top8", [P, BT, 8])
        top_at = sb("top_at", [P, BT, 8], U32)
        top_f = sb("top_f", [P, BT, TOPK])
        onehot = sb("onehot", [P, BT, TOPK, NE])
        member = sb("member", [P, BT, NE], BF16)
        seen = sb("seen", [P, NE], BF16)
        seen_new = sb("seen_new", [P, NE])
        place8 = sb("place8", [P, BT, NE])
        picked = sb("picked", [P, BT, TOPK, NE])
        place_f = sb("place_f", [P, BT, TOPK])
        place_i = sb("place_i", [P, BT * TOPK], I32)
        score_all = sb("score_all", [P, TILES, NE])
        onehot_all = sb("onehot_all", [P, TILES, TOPK, NE])
        big = expo[:, 0, :].rearrange("p (t k e) -> p t k e", k=TOPK, e=NE)
        small_a = expo[:, 1, 0:TILES * NE].rearrange("p (t e) -> p t e", e=NE)
        top_all = sb("top_all", [P, TILES])
        gate_w = sb("gate_w", [P, TILES, TOPK])
        gate_sum = sb("gate_sum", [P, TILES])
        gate_all = sb("gate_all", [P, TILES, TOPK])
        count = sb("count", [P, NE])
        count_i = sb("count_i", [P, NE], I32)
        ntile_i = sb("ntile_i", [P, NE], I32)
        ntile = sb("ntile", [P, NE])
        cum = sb("cum", [P, NE])
        cum_rows = sb("cum_rows", [P, NE])
        jump = sb("jump", [P, NE])
        tail_f = sb("tail_f", [P, NE])
        tail_i = sb("tail_i", [P, NE], I32)
        last_row = sb("last_row", [P, 1])
        expert_all = sb("expert_all", [P, LOADED])
        row_f = sb("row_f", [1, LOADED])
        row_g = sb("row_g", [1, LOADED])
        tile_row = sb("tile_row", [1, LOADED], I32)
        tile_expert = sb("tile_expert", [1, LOADED], I32)

        xtile = [sb(f"xtile{i}", [P, ROW_W]) for i in range(STEP)]
        result_row = [sb(f"result_row{i}", [P, 1], I32) for i in range(STEP)]
        xtile_t = [sb(f"xtile_t{i}", [P, P]) for i in range(2)]
        silu = [sb(f"silu{i}", [P, HID]) for i in range(2)]
        gated = [sb(f"gated{i}", [P, HID]) for i in range(2)]
        gated_t = [sb(f"gated_t{i}", [P, HID]) for i in range(2)]
        ytile = [sb(f"ytile{i}", [P, D]) for i in range(STEP)]

        back_x = [qkv[c][:].rearrange("p j n -> p (j n)")[:, 0:TPC * TOPK * D].rearrange("p (m d) -> p m d", d=D) for c in range(HALVES)]
        gate = sb("gate", [P, BT * TOPK])
        hseq = sb("hseq", [P, 1 + SEQ])
        top = sb("top", [P, 1 + SEQ])
        y_num, y_den = (rope_c[:, i * TPC:(i + 1) * TPC, :].rearrange("p j n -> p (j n)") for i in range(2))
        y_b, e_r = (rope_s[:, i * TPC:(i + 1) * TPC, :].rearrange("p j n -> p (j n)") for i in range(2))
        qmax, ev = (a[:].rearrange("p j n -> p (j n)") for a in (rope1, rope2))
        rwkv = squares[:].rearrange("p a j n -> p (a j n)")

        banks = ctx.enter_context(nc.psum_tensor("banks", [P, 8, CHUNK], F32))
        bank = [banks[:, i, :] for i in range(8)]
        tiles4 = lambda a: a.rearrange("p (j n) -> p j n", j=TPC)
        ps_half = [bank[0], bank[1]]
        ps_small = bank[2]
        ps_vk = bank[3]
        ps_turn = [bank[4], bank[5]]
        ps_qkv = [bank[6], bank[7]]
        ps_den = [ps_small[:, c * TPC * HEADS:(c + 1) * TPC * HEADS].rearrange("p (j h) -> p j h", j=TPC) for c in range(HALVES)]
        ps_score = ps_small[:, 128:128 + BT * NE].rearrange("p (j e) -> p j e", e=NE)
        ps_rank = ps_small[:, 192:192 + BT * NE].rearrange("p (j e) -> p j e", e=NE)
        ps_count = ps_small[:, 256:256 + NE]
        ps_up, ps_gt, ps_xt, ps_y = (bank[2 * i:2 * i + 2] for i in range(4))
        pair = lambda i: banks[:, i:i + 2, :].rearrange("p a n -> p (a n)")
        ps_r = pair(0)
        ps_turn3 = bank[3]
        ps_k, ps_v = pair(4), pair(6)

        weights_in, rope_in, bias_in, split_out, rows_in = (
            sem("weights_in"), sem("rope_in"), sem("bias_in"), sem("split_out"), sem("rows_in"))
        dve_step, act_step = sem("dve_step"), sem("act_step")
        setup_done, split_done, decay_ready = sem("setup_done"), sem("split_done"), sem("decay_ready")
        x_loaded, xold_loaded, x_stored = sem2("x_loaded"), sem2("xold_loaded"), sem2("x_stored")
        var_ready, dev_ready, h_ready, h_turned, ht_ready = (
            sem2("var_ready"), sem2("dev_ready"), sem2("h_ready"), sem2("h_turned"), sem2("ht_ready"))
        qkv_done, qkv_taken, qkv_ready, qkdev_ready = (
            sem("qkv_done"), sem("qkv_taken"), sem2("qkv_ready"), sem2("qkdev_ready"))
        kf_ready, qf_ready, qf_turned, qft_ready = sem2("kf_ready"), sem2("qf_ready"), sem2("qf_turned"), sem2("qft_ready")
        vk_ready, state_ready, res_ready = sem("vk_ready"), sem("state_ready"), sem("res_ready")
        attn_ready, attn_turned, attnt_ready = sem2("attn_ready"), sem2("attn_turned"), sem2("attnt_ready")
        out_ready, outdev_ready, xres_ready = sem2("out_ready"), sem2("outdev_ready"), sem2("xres_ready")
        var2_ready, dev2_ready, h2_ready, h2_turned, h2t_ready = (
            sem2("var2_ready"), sem2("dev2_ready"), sem2("h2_ready"), sem2("h2_turned"), sem2("h2t_ready"))
        score_ready, member_ready, rank_ready = sem("score_ready"), sem("member_ready"), sem("rank_ready")
        place_ready = sem("place_ready")
        queued = sem2("queued")
        seen_ready, count_ready, tail_ready, tails_queued = (
            sem("seen_ready"), sem("count_ready"), sem("tail_ready"), sem("tails_queued"))
        table_ready, gate_in, gate_exp = sem("table_ready"), sem("gate_in"), sem("gate_exp")
        xtile_in = [sem(f"xtile_in{i}") for i in range(STEP)]
        xtile_turned, xtilet_ready, up_ready, silu_ready, gated_ready = (
            sem("xtile_turned"), sem("xtilet_ready"), sem("up_ready"), sem("silu_ready"), sem("gated_ready"))
        gated_turned, gatedt_ready, y_ready, ytile_ready = (
            sem("gated_turned"), sem("gatedt_ready"), sem("y_ready"), sem("ytile_ready"))
        y_stored = [sem(f"y_stored{i}") for i in range(STEP)]
        results_in, place_taken = sem2("results_in"), sem("place_taken")
        gates_ready, gate_taken, weighted, first_added, xmid_ready = (
            sem("gates_ready"), sem("gate_taken"), sem2("weighted"), sem2("first_added"), sem2("xmid_ready"))
        k_ready, v_ready, r_ready = sem("k_ready"), sem("v_ready"), sem("r_ready")
        past_expo, past_ex, now_expo, now_ex, er_ready = (
            sem("past_expo"), sem("past_ex"), sem("now_expo"), sem("now_ex"), sem("er_ready"))
        rwkv_ready, mixed_ready = sem2("rwkv_ready"), sem2("mixed_ready")
        out_stored = sem2("out_stored")

        block = ctx.enter_context(nc.Block())

        def rows(dram_ap, chunk):
            return dram_ap[bass.ds(chunk * CHUNK, CHUNK), :].rearrange("(j p) d -> p j d", p=P)

        FIRST, SECOND = 0, 1
        N_TURN, N_UP, N_GATE, N_BACK = XTILES + 3, XTILES + 2, XTILES + 1, XTILES
        SCATTERS = 16 * TPC * TOPK

        WEIGHTS = [(k_sb[:], consts), (wqkv_sb[:], w_qkv), (wout_sb[:], w_out), (wrouter_sb[:], w_router),
                   (rows_sb[:], router_rows), (gout_sb[:], g_out), (ch_sb[:], channel), (wkvr_sb[:, 0, :], w_k),
                   (wkvr_sb[:, 1, :], w_v), (wkvr_sb[:, 2, :], w_r), (wo_sb[:], w_o), (wup_sb[:], w_up),
                   (wdown_sb[:], w_down)]
        ROPE = [(cos_sb, cosine), (sin_sb, sine), (gqk_sb[:], g_qk), (gqks_sb[:], g_qk_swapped)]

        def combine(eng, ops, c, m, f):
            eng.wait_ge(x_loaded[c], m * 16 + 16 * BATCH)
            eng.wait_ge(weighted[c], m)
            if f == SECOND:
                eng.wait_ge(out_stored[c], m * 16 - 16 * BATCH)
            y = back_x[c].rearrange("p (j k) d -> p j k d", k=TOPK)
            ops.tensor_tensor(xmid[c][:], xin[c][:], y[:, :, 0, :], ALU.add).then_inc(first_added[c], 1)
            eng.wait_ge(first_added[c], m)
            ops.tensor_tensor(xmid[c][:], xmid[c][:], y[:, :, 1, :], ALU.add).then_inc(xmid_ready[c], 1)

        @block.sync
        def _(sp):
            sp.dma_start(bias_sb[:], bias_cols).then_inc(bias_in, 16)
            for c in range(HALVES):
                sp.dma_start(xin[c][:], rows(x, c)).then_inc(x_loaded[c], 16)
            for dst, src in WEIGHTS:
                sp.dma_start(dst, src).then_inc(weights_in, 16)
            for dst, src in ROPE:
                sp.dma_start(dst, src).then_inc(rope_in, 16)
            sp.wait_ge(split_done, 1)
            for i in range(3):
                sp.dma_start(split_dram[i, :].rearrange("(p n) -> p n", p=P), bias_parts[:, i, :]).then_inc(split_out, 16)
            sp.wait_ge(split_out, 3 * 16)
            sp.wait_ge(setup_done, 1)
            sp.dma_start(bias_rows[0:3, :], split_dram).then_inc(rows_in, 16)

            def load_results(chunk, c):
                rows_of = result_dram[bass.ds(chunk * (CHUNK * TOPK), CHUNK * TOPK), :]
                sp.dma_start(back_x[c].rearrange("p (j k) d -> p j k d", k=TOPK),
                             rows_of.rearrange("(j p k) d -> p j k d", p=P, k=TOPK)).then_inc(results_in[c], 16)

            def store(c, m, dst, row):
                sp.wait_ge(xres_ready[c], m)
                sp.dma_start(rows(dst, row * HALVES + c), xres[c][:]).then_inc(x_stored[c], 16)

            def experts(f):
                for c in range(HALVES):
                    sp.wait_ge(queued[c], 16 + SCATTERS * BATCH * (f + 1))
                sp.wait_ge(tails_queued, 16 * NE * (f + 1))
                sp.wait_ge(table_ready, f + 1)

                def load(t, i):
                    row = sp.value_load(tile_row[0:1, bass.ds(t, 1)], min_val=0, max_val=NE * REGION - P)
                    sp.dma_start(xtile[i][:], queue_dram[bass.ds(row, P), :]).then_inc(xtile_in[i], 16)

                for t in range(STEP):
                    load(t, t)
                with sp.Fori(0, XTILES // STEP) as n:
                    for i in range(STEP):
                        sp.wait_ge(gated_ready, n * STEP + (i + 1 + f * N_GATE))
                        load(n * STEP + (i + STEP), i)
                for i in range(STEP):
                    sp.wait_ge(xtile_in[i], 16 * (LOADED // STEP) * (f + 1))
                    sp.wait_ge(y_stored[i], 16 * (N_BACK // STEP * (f + 1) + 1))
                for c in range(HALVES):
                    load_results(c, c)

            for c in range(HALVES):
                sp.dma_start(xold[c][:], rows(x, c)).then_inc(xold_loaded[c], 16)
            with sp.Fori(1, BATCH) as m:
                for c in range(HALVES):
                    sp.wait_ge(h_ready[c], m)
                    sp.dma_start(xin[c][:], rows(x, m * HALVES + c)).then_inc(x_loaded[c], 16)
                for c in range(HALVES):
                    store(c, m, x1_dram, m - 1)
                    sp.dma_start(xold[c][:], rows(x, m * HALVES + c)).then_inc(xold_loaded[c], 16)
            for c in range(HALVES):
                store(c, BATCH, x1_dram, BATCH - 1)
                sp.wait_ge(x_stored[c], 16 * (BATCH + 1))
                sp.dma_start(xin[c][:], rows(x1_dram, c)).then_inc(x_loaded[c], 16)
            experts(FIRST)
            with sp.Fori(BATCH + 1, 2 * BATCH) as m:
                for c in range(HALVES):
                    sp.wait_ge(xmid_ready[c], m - BATCH)
                    sp.dma_start(xin[c][:], rows(x1_dram, m * HALVES + (c - BATCH * HALVES))).then_inc(x_loaded[c], 16)
                    load_results(m * HALVES + (c - BATCH * HALVES), c)
                for c in range(HALVES):
                    store(c, m, x3_dram, m - (1 + BATCH))
            for c in range(HALVES):
                store(c, 2 * BATCH, x3_dram, BATCH - 1)
                sp.wait_ge(x_stored[c], 16 * (2 * BATCH + 1))
                sp.dma_start(xin[c][:], rows(x3_dram, c)).then_inc(x_loaded[c], 16)
            experts(SECOND)
            with sp.Fori(BATCH + 1, 2 * BATCH) as m:
                for c in range(HALVES):
                    sp.wait_ge(xmid_ready[c], m)
                    sp.dma_start(rows(out, m * HALVES + (c - (1 + BATCH) * HALVES)), xmid[c][:]).then_inc(out_stored[c], 16)
                    sp.dma_start(xin[c][:], rows(x3_dram, m * HALVES + (c - BATCH * HALVES))).then_inc(x_loaded[c], 16)
                    load_results(m * HALVES + (c - BATCH * HALVES), c)
            for c in range(HALVES):
                sp.wait_ge(xmid_ready[c], 2 * BATCH)
                sp.dma_start(rows(out, CHUNKS - HALVES + c), xmid[c][:]).then_inc(out_stored[c], 16)
            for c in range(HALVES):
                sp.wait_ge(out_stored[c], 16 * (BATCH + 1))

        @block.gpsimd
        def _(pool):
            def scatter(m):
                pool.wait_ge(place_ready, m)
                pool.sem_inc(place_taken, 1)
                for c in range(HALVES):
                    for j in range(TPC):
                        for k in range(TOPK):
                            at = (c * TPC + j) * TOPK + k
                            nc.gpsimd.indirect_dma_start(
                                queue_dram, bass.IndirectOffsetOnAxis(ap=place_i[:, at:at + 1], axis=0),
                                hffn[c][:, j, :], None).then_inc(queued[c], 16)

            def tails(f):
                pool.wait_ge(tail_ready, f + 1)
                for e in range(NE):
                    nc.gpsimd.indirect_dma_start(
                        queue_dram, bass.IndirectOffsetOnAxis(ap=tail_i[:, e:e + 1], axis=0),
                        tail_rows[:], None).then_inc(tails_queued, 16)

            def experts(f):
                with pool.Fori(0, XTILES // STEP) as n:
                    for i in range(STEP):
                        pool.wait_ge(ytile_ready, n * STEP + (i + 1 + f * N_BACK))
                        pool.sem_inc(place_taken, 1)
                        nc.gpsimd.indirect_dma_start(
                            result_dram, bass.IndirectOffsetOnAxis(ap=result_row[i][:, 0:1], axis=0),
                            ytile[i][:], None, bounds_check=NO_RESULT - 1, oob_is_err=False).then_inc(y_stored[i], 16)

            pool.wait_ge(setup_done, 1)
            for c in range(HALVES):
                pool.dma_start(queue_dram[bass.ds((c + 1) * REGION - 1, 1), :], tail_rows[0:1, :]).then_inc(queued[c], 16)
            for i in range(STEP):
                pool.dma_start(result_dram[bass.ds(NO_RESULT + P + i, 1), :], tail_rows[0:1, 0:D]).then_inc(y_stored[i], 16)
            with pool.Fori(1, BATCH + 1) as m:
                scatter(m)
            tails(FIRST)
            experts(FIRST)
            for c in range(HALVES):
                combine(pool, nc.gpsimd, c, 1, FIRST)
            with pool.Fori(BATCH + 1, 2 * BATCH) as m:
                for c in range(HALVES):
                    pool.wait_ge(xres_ready[c], m)
                    pool.sem_inc(place_taken, 1)
                    combine(pool, nc.gpsimd, c, m - (BATCH - 1), FIRST)
                scatter(m)
            scatter(2 * BATCH)
            tails(SECOND)
            experts(SECOND)
            with pool.Fori(BATCH + 1, 2 * BATCH + 1) as m:
                combine(pool, nc.gpsimd, 1, m, SECOND)

        @block.scalar
        def _(act):
            step = [0]

            def begin():
                act.sem_clear(act_step)
                step[0] = 0

            def settle(ins):
                step[0] += 1
                ins.then_inc(act_step, 1)
                act.wait_ge(act_step, step[0])

            act.wait_ge(weights_in, 16 * len(WEIGHTS))
            nc.scalar.activation(exp_decay[:], ch_sb[:, V_DECAY:V_DECAY + 1], ACT.Exp).then_inc(decay_ready, 1)
            act.wait_ge(setup_done, 2)

            def deviations(c, m, var, moment, dev, ready):
                act.wait_ge(var[c], m)
                nc.scalar.activation(dev[c][:], moment[c][:, :, 1], ACT.Sqrt, bias=ln_eps[:, 0:1]).then_inc(ready[c], 1)

            def turned(c, m, done, src, dst, ready):
                act.wait_ge(done[c], m)
                nc.scalar.activation(dst, src, ACT.Copy).then_inc(ready[c], 1)

            def empty_qkv(c, m):
                for j in range(TPC):
                    act.wait_ge(qkv_done, m * BT + (c * TPC + j + 1 - BT))
                    last = nc.scalar.activation(qkv[c][:, j, 0:3 * D], ps_qkv[j % 2][:, 0:3 * D], ACT.Copy).then_inc(qkv_taken, 1)
                act.wait_ge(qkv_taken, m * BT + ((c + 1) * TPC - BT))
                act.sem_inc(qkv_ready[c], 1)

            def norms(c):
                for half in range(2):
                    for j in range(TPC):
                        last = nc.scalar.activation(squares[:, half, j, :], qkv[c][:, j, half * D:(half + 1) * D], ACT.Square,
                                                    accum_out=sumsq[c][:, half, j:j + 1])
                settle(last)
                nc.scalar.activation(qk_dev[c][:], sumsq[c][:], ACT.Sqrt, bias=rms_eps[:, 0:1], scale=1.0 / D).then_inc(qkdev_ready[c], 1)

            def out_norms(c, m):
                act.wait_ge(out_ready[c], m)
                for j in range(TPC):
                    last = nc.scalar.activation(out_squares[:, j, :], tiles4(ps_half[c])[:, j, :], ACT.Square,
                                                accum_out=out_sum[c][:, j:j + 1])
                settle(last)
                nc.scalar.activation(out_dev[c][:], out_sum[c][:], ACT.Sqrt, bias=rms_eps[:, 0:1], scale=1.0 / D).then_inc(outdev_ready[c], 1)

            def attention(done, ahead):
                both = range(HALVES)
                begin()
                if done is not None:
                    for c in both:
                        turned(c, done, attn_turned, ps_half[c], attn_t[c][:], attnt_ready)
                if ahead is not None:
                    for c in both:
                        deviations(c, ahead, var_ready, moment, dev, dev_ready)
                for c in both:
                    if done is not None:
                        out_norms(c, done)
                    if ahead is not None:
                        turned(c, ahead, h_turned, ps_turn[c], hmix_t[c][:], ht_ready)
                if ahead is not None:
                    empty_qkv(0, ahead)
                if done is not None:
                    for c in both:
                        deviations(c, done, var2_ready, moment2, dev2, dev2_ready)
                if ahead is not None:
                    norms(0)
                    empty_qkv(1, ahead)
                    norms(1)
                if done is not None:
                    for c in both:
                        turned(c, done, h2_turned, ps_half[c], hffn_t[c][:], h2t_ready)
                if ahead is not None:
                    for c in both:
                        turned(c, ahead, qf_turned, ps_turn[c], qf_t[c][:], qft_ready)

            def plan(f):
                act.wait_ge(gate_in, f + 1)
                nc.scalar.activation(small_a, small_a, ACT.Exp).then_inc(gate_exp, 1)

            def experts(f):
                T, U, G, B = f * N_TURN, f * N_UP, f * N_GATE, f * N_BACK

                def turn_x(i, n1):
                    act.wait_ge(xtile_turned, n1)
                    nc.scalar.activation(xtile_t[i][:], ps_xt[i][:, 0:P], ACT.Copy).then_inc(xtilet_ready, 1)

                def silu_up(i, n1):
                    act.wait_ge(up_ready, n1)
                    nc.scalar.activation(silu[i][:], ps_up[i][:, 0:HID], ACT.Silu).then_inc(silu_ready, 1)

                for t in range(2):
                    turn_x(t, t + 1 + T)
                silu_up(0, 1 + U)
                turn_x(0, 3 + T)
                silu_up(1, 2 + U)
                with act.Fori(0, XTILES // STEP) as n:
                    for i in range(STEP):
                        turn_x((i + 1) % 2, n * STEP + (i + 4 + T))
                        act.wait_ge(gated_ready, n * STEP + (i + 1 + G))
                        silu_up(i % 2, n * STEP + (i + 3 + U))
                        act.wait_ge(y_ready, n * STEP + (i + 1 + B))
                        act.wait_ge(y_stored[i], (n + (1 + f * (N_BACK // STEP))) * 16)
                        nc.scalar.activation(ytile[i][:], ps_y[i % 2][:, 0:D], ACT.Copy).then_inc(ytile_ready, 1)

            def weight(m, f):
                nc.scalar.activation(gate[:].rearrange("p (j k) -> p j k", k=TOPK),
                                     gate_all[:, bass.ds(m * BT - (1 + f * BATCH) * BT, BT), :], ACT.Copy).then_inc(gate_taken, 1)
                act.wait_ge(gate_taken, m)
                for c in range(HALVES):
                    act.wait_ge(results_in[c], m * 16)
                    for at in range(TPC * TOPK):
                        g = c * TPC * TOPK + at
                        last = nc.scalar.activation(back_x[c][:, at, :], back_x[c][:, at, :], ACT.Copy, scale=gate[:, g:g + 1])
                    last.then_inc(weighted[c], 1)
                act.wait_ge(weighted[HALVES - 1], m)

            def turned_in(c, m):
                act.wait_ge(h_turned[c], m)
                nc.scalar.activation(hseq[:, 1 + c * CHUNK:1 + (c + 1) * CHUNK], ps_turn3, ACT.Copy).then_inc(ht_ready[c], 1)

            def mixing(m, last):
                both = range(HALVES)
                act.wait_ge(past_expo, m - BATCH)
                nc.scalar.activation(expo[:, 2:4, :], expo[:, 2:4, :], ACT.Exp).then_inc(past_ex, 1)
                act.wait_ge(r_ready, m - BATCH)
                nc.scalar.activation(e_r, ps_r, ACT.Exp, scale=-1.0).then_inc(er_ready, 1)
                act.wait_ge(now_expo, m - BATCH)
                nc.scalar.activation(expo[:, 0:2, :], expo[:, 0:2, :], ACT.Exp).then_inc(now_ex, 1)
                if not last:
                    weight(m - (BATCH - 1), FIRST)
                for c in both:
                    deviations(c, m, var2_ready, moment2, dev2, dev2_ready)
                if not last:
                    for c in both:
                        deviations(c, m + 1, var_ready, moment, dev, dev_ready)
                for c in both:
                    turned(c, m, h2_turned, ps_half[c], hffn_t[c][:], h2t_ready)
                if not last:
                    for c in both:
                        turned_in(c, m + 1)

            attention(None, 1)
            with act.Fori(1, BATCH) as m:
                attention(m, m + 1)
            attention(BATCH, None)
            plan(FIRST)
            experts(FIRST)
            act.wait_ge(gates_ready, 1)
            weight(1, FIRST)
            for c in range(HALVES):
                deviations(c, BATCH + 1, var_ready, moment, dev, dev_ready)
            for c in range(HALVES):
                turned_in(c, BATCH + 1)
            with act.Fori(BATCH + 1, 2 * BATCH) as m:
                mixing(m, False)
            mixing(2 * BATCH, True)
            plan(SECOND)
            experts(SECOND)
            act.wait_ge(gates_ready, 2)
            with act.Fori(BATCH + 1, 2 * BATCH + 1) as m:
                weight(m, SECOND)

        @block.tensor
        def _(pe):
            def turn(dst, src):
                for j in range(TPC):
                    last = nc.tensor.transpose(dst[:, j * P:(j + 1) * P], src[:, j, 0:D], ident)
                return last

            def bias(dst, column, width, stop):
                return nc.tensor.matmul(dst, ones_bf[:], bias_rows[:, bass.ds(column, width)], start=False, stop=stop)

            def read_state(m):
                pe.wait_ge(state_ready, m)
                for c in range(HALVES):
                    pe.wait_ge(qft_ready[c], m)
                    for j in range(TPC):
                        q = qf_t[c][:, j * P:(j + 1) * P]
                        nc.tensor.matmul(tiles4(ps_half[c])[:, j, :], q, state[:, 0:D], start=True, stop=True)
                        last = nc.tensor.matmul(ps_den[c][:, j, :], q, state[:, D:RES_W], start=True, stop=True)
                last.then_inc(res_ready, 1)

            def project_qkv(c, m):
                pe.wait_ge(ht_ready[c], m)
                for j in range(TPC):
                    tile = c * TPC + j
                    if tile >= 2 or not isinstance(m, int):
                        pe.wait_ge(qkv_taken, m * BT + (tile - 1 - BT))
                    dst = ps_qkv[j % 2][:, 0:3 * D]
                    nc.tensor.matmul(dst, hmix_t[c][:, j * P:(j + 1) * P], wqkv_sb[:], start=True, stop=False)
                    bias(dst, B_QKV, 3 * D, True).then_inc(qkv_done, 1)

            def keys_values(c, m):
                pe.wait_ge(kf_ready[c], m)
                for j in range(TPC):
                    last = nc.tensor.matmul(ps_vk[:, 0:D + 1], kf[c][:, j, :], qkv[c][:, j, 2 * D:3 * D + 1],
                                            start=(c == 0 and j == 0), stop=(c == HALVES - 1 and j == TPC - 1))
                if c == HALVES - 1:
                    last.then_inc(vk_ready, 1)

            def project_out(c, m):
                pe.wait_ge(attnt_ready[c], m)
                for j in range(TPC):
                    dst = tiles4(ps_half[c])[:, j, :]
                    nc.tensor.matmul(dst, attn_t[c][:, j * P:(j + 1) * P], wout_sb[:], start=True, stop=False)
                    last = bias(dst, B_OUT, D, True)
                last.then_inc(out_ready[c], 1)

            def turn_for_router(c, m):
                pe.wait_ge(h2_ready[c], m)
                turn(ps_half[c], hffn[c]).then_inc(h2_turned[c], 1)

            def scores(m):
                for c in range(HALVES):
                    pe.wait_ge(h2t_ready[c], m)
                    for j in range(TPC):
                        last = nc.tensor.matmul(ps_score[:, c * TPC + j, :], hffn_t[c][:, j * P:(j + 1) * P], wrouter_sb[:],
                                                start=True, stop=True)
                last.then_inc(score_ready, 1)

            def ranks(m):
                pe.wait_ge(member_ready, m)
                nc.tensor.matmul(ps_rank, tri_bf[:], member[:], start=True, stop=False)
                for j in range(BT - 1):
                    nc.tensor.matmul(ps_rank[:, j + 1:, :], ones_bf[:],
                                     member[:, j:j + 1, :].to_broadcast([P, BT - 1 - j, NE]), start=False, stop=False)
                nc.tensor.matmul(ps_rank, ones_bf[:], seen[:, None, :].to_broadcast([P, BT, NE]),
                                 start=False, stop=True).then_inc(rank_ready, 1)

            def attention(done, ahead):
                both = range(HALVES)
                if done is not None:
                    read_state(done)
                    for c in both:
                        pe.wait_ge(attn_ready[c], done)
                        turn(ps_half[c], attn[c]).then_inc(attn_turned[c], 1)
                    for c in both:
                        project_out(c, done)
                if ahead is not None:
                    for c in both:
                        pe.wait_ge(h_ready[c], ahead)
                        turn(ps_turn[c], hmix[c]).then_inc(h_turned[c], 1)
                    for c in both:
                        project_qkv(c, ahead)
                if done is not None:
                    for c in both:
                        turn_for_router(c, done)
                    scores(done)
                if ahead is not None:
                    for c in both:
                        keys_values(c, ahead)
                        pe.wait_ge(qf_ready[c], ahead)
                        turn(ps_turn[c], qf[c]).then_inc(qf_turned[c], 1)
                if done is not None:
                    ranks(done)

            def plan(f):
                pe.wait_ge(seen_ready, (f + 1) * BATCH)
                nc.tensor.matmul(ps_count, ones_bf[:], seen[:], start=True, stop=True).then_inc(count_ready, 1)

            def experts(f):
                T, G, B = f * N_TURN, f * N_GATE, f * N_BACK
                loads = f * (LOADED // STEP)

                def expert(t):
                    return pe.value_load(tile_expert[0:1, bass.ds(t, 1)], min_val=0, max_val=NE - 1)

                def turn_x(i, nload):
                    pe.wait_ge(xtile_in[i], nload)
                    nc.tensor.transpose(ps_xt[i % 2][:, 0:P], xtile[i][:, 0:D], ident).then_inc(xtile_turned, 1)

                def up(i, e, n1):
                    pe.wait_ge(xtilet_ready, n1)
                    nc.tensor.matmul(ps_up[i], xtile_t[i][:], wup_sb[:, bass.ds(e * (2 * HID), 2 * HID)], start=True, stop=False)
                    bias(ps_up[i], e * (2 * HID) + B_UP, 2 * HID, True).then_inc(up_ready, 1)

                def turn_gated(i, n1):
                    pe.wait_ge(gated_ready, n1)
                    for h in range(HCH):
                        last = nc.tensor.transpose(ps_gt[i][:, h * P:(h + 1) * P], gated[i][:, h * P:(h + 1) * P], ident)
                    last.then_inc(gated_turned, 1)

                def down(i, e, n1):
                    pe.wait_ge(gatedt_ready, n1)
                    for h in range(HCH):
                        nc.tensor.matmul(ps_y[i][:, 0:D], gated_t[i][:, h * P:(h + 1) * P],
                                         wdown_sb[:, bass.ds(e * (HCH * D) + h * D, D)], start=(h == 0), stop=False)
                    bias(ps_y[i][:, 0:D], e * D + B_DOWN, D, True).then_inc(y_ready, 1)

                pe.wait_ge(table_ready, f + 1)
                for t in range(2):
                    turn_x(t, 16 * (1 + loads))
                up(0, expert(0), 1 + T)
                turn_x(2, 16 * (1 + loads))
                up(1, expert(1), 2 + T)
                turn_gated(0, 1 + G)
                with pe.Fori(0, XTILES // STEP) as n:
                    e = [expert(n * STEP + t) for t in range(2)]
                    for i in range(STEP):
                        e.append(expert(n * STEP + (i + 2)))
                        turn_x((i + 3) % STEP, (n + ((i + 3) // STEP + 1 + loads)) * 16)
                        up(i % 2, e[i + 2], n * STEP + (i + 3 + T))
                        turn_gated((i + 1) % 2, n * STEP + (i + 2 + G))
                        down(i % 2, e[i], n * STEP + (i + 1 + B))

            def turn_in(c, m):
                pe.wait_ge(h_ready[c], m)
                if c:
                    pe.wait_ge(ht_ready[0], m)
                turn(ps_turn3, hmix[c]).then_inc(h_turned[c], 1)

            def project(dst, i, c):
                dst = dst[:, c * CHUNK:(c + 1) * CHUNK]
                nc.tensor.matmul(dst, wnow_sb[:, i, :], hseq[:, 1 + c * CHUNK:1 + (c + 1) * CHUNK], start=True, stop=False)
                return nc.tensor.matmul(dst, wpast_sb[:, i, :], hseq[:, c * CHUNK:(c + 1) * CHUNK], start=False, stop=True)

            def mix_keys(c, m):
                pe.wait_ge(ht_ready[c], m)
                return project(ps_k, 0, c)

            def mix_values():
                for i, dst, ready in ((1, ps_v, v_ready), (2, ps_r, r_ready)):
                    for c in range(HALVES):
                        last = project(dst, i, c)
                    last.then_inc(ready, 1)

            def mixing(m, last):
                both = range(HALVES)
                for c in both:
                    pe.wait_ge(rwkv_ready[c], m - BATCH)
                    for j in range(TPC):
                        tile = slice(c * CHUNK + j * P, c * CHUNK + (j + 1) * P)
                        done = nc.tensor.matmul(tiles4(ps_half[c])[:, j, :], rwkv[:, tile], wo_sb[:], start=True, stop=True)
                    done.then_inc(mixed_ready[c], 1)
                for c in both:
                    turn_for_router(c, m)
                scores(m)
                if not last:
                    for c in both:
                        turn_in(c, m + 1)
                    mix_keys(0, m + 1)
                ranks(m)
                if not last:
                    mix_keys(1, m + 1).then_inc(k_ready, 1)
                    mix_values()

            pe.wait_ge(setup_done, 2)
            pe.wait_ge(weights_in, 16 * len(WEIGHTS))
            pe.wait_ge(rows_in, 16)
            attention(None, 1)
            with pe.Fori(1, BATCH) as m:
                attention(m, m + 1)
            attention(BATCH, None)
            plan(FIRST)
            experts(FIRST)
            for c in range(HALVES):
                turn_in(c, BATCH + 1)
            mix_keys(0, BATCH + 1)
            mix_keys(1, BATCH + 1).then_inc(k_ready, 1)
            mix_values()
            with pe.Fori(BATCH + 1, 2 * BATCH) as m:
                mixing(m, False)
            mixing(2 * BATCH, True)
            plan(SECOND)
            experts(SECOND)

        @block.vector
        def _(dve):
            step = [0]

            def begin():
                dve.sem_clear(dve_step)
                step[0] = 0

            def mark(ins):
                step[0] += 1
                ins.then_inc(dve_step, 1)
                return step[0]

            def need(count):
                dve.wait_ge(dve_step, count)

            def settle(ins):
                need(mark(ins))

            dve.wait_ge(bias_in, 16)
            settle(nc.vector.tensor_copy(bias_parts[:, 0, :], bias_sb[:]))
            settle(nc.vector.tensor_tensor(bias_left[:], bias_sb[:], bias_parts[:, 0, :], ALU.subtract))
            settle(nc.vector.tensor_copy(bias_parts[:, 1, :], bias_left[:]))
            settle(nc.vector.tensor_tensor(bias_left[:], bias_left[:], bias_parts[:, 1, :], ALU.subtract))
            nc.vector.tensor_copy(bias_parts[:, 2, :], bias_left[:]).then_inc(split_done, 1)
            nc.vector.memset(bias_rows[:], 0.0)
            nc.vector.memset(ones_bf[:], 1.0)
            nc.vector.memset(ones8[:], 1.0)
            nc.vector.memset(ln_eps[:], LN_EPS)
            nc.vector.memset(rms_eps[:], RMS_EPS)
            nc.vector.memset(tail_rows[:, 0:D], 0.0)
            nc.vector.memset(tail_rows[:, D + 1:ROW_W], -1.0)
            nc.vector.memset(hseq[:, 0:1], 0.0)
            nc.vector.memset(top[:, 0:1], NO_PAST)
            nc.vector.memset(num[:, 0:1], 0.0)
            nc.vector.memset(den[:, 0:1], 0.0)
            for c in range(HALVES):
                nc.vector.memset(qkv[c][:, :, 3 * D:3 * D + 1], 1.0)
            dve.wait_ge(weights_in, 16 * len(WEIGHTS))
            nc.vector.tensor_scalar(tail_rows[:, D:D + 1], k_sb[:, K_PART:K_PART + 1], float(NO_RESULT), None, ALU.add)
            nc.vector.tensor_copy(tri_bf[:], k_sb[:, K_TRI:K_TRI + P]).then_inc(setup_done, 1)
            dve.wait_ge(rope_in, 16 * len(ROPE))
            for half in range(2):
                cols = slice(half * D, (half + 1) * D)
                for table, src, g in ((rope_c, cos_sb, gqk_sb), (rope_s, sin_sb, gqks_sb)):
                    nc.vector.tensor_tensor(table[:, :, cols], src, g[:, None, cols].to_broadcast([P, SEQ // P, D]), ALU.mult)
            settle(nc.vector.tensor_scalar(mix_left[:], ch_sb[:, V_MIXK:V_MIXR + 1], -1.0, 1.0, ALU.mult, ALU.add))
            for i in range(3):
                nc.vector.tensor_scalar(wnow_sb[:, i, :], wkvr_sb[:, i, :], ch_sb[:, V_MIXK + i:V_MIXK + i + 1], None, ALU.mult)
                nc.vector.tensor_scalar(wpast_sb[:, i, :], wkvr_sb[:, i, :], mix_left[:, i:i + 1], None, ALU.mult)
            dve.wait_ge(decay_ready, 1)
            nc.vector.tensor_scalar(w_sb[:], exp_decay[:], -1.0, None, ALU.mult).then_inc(setup_done, 1)
            dve.wait_ge(setup_done, 2)

            both = range(HALVES)

            def moments(src, stats, moment, ready):
                counted = []
                for c in both:
                    for j in range(TPC):
                        last = nc.vector.bn_stats(stats[c][:, j, :], src[c][:, j, :])
                    counted.append(mark(last))
                for c in both:
                    need(counted[c])
                    for j in range(TPC):
                        last = nc.vector.bn_aggr(moment[c][:, j, :], stats[c][:, j, :])
                    last.then_inc(ready[c], 1)

            def normalise(m, src, moment, dev_ready, dev, rstd, dst, ready):
                inverted = []
                for c in both:
                    dve.wait_ge(dev_ready[c], m)
                    inverted.append(mark(nc.vector.reciprocal(rstd[c][:], dev[c][:])))
                for c in both:
                    need(inverted[c])
                    for j in range(TPC):
                        last = nc.vector.tensor_scalar(dst[c][:, j, 0:D], src[c][:, j, :], moment[c][:, j, 0:1], rstd[c][:, j:j + 1],
                                                       ALU.subtract, ALU.mult)
                    last.then_inc(ready[c], 1)

            def normalise_for_experts(m):
                for c in both:
                    dve.wait_ge(queued[c], m * SCATTERS + (16 - SCATTERS))
                normalise(m, xres, moment2, dev2_ready, dev2, rstd2, hffn, h2_ready)

            def choose(m, f):
                at = m * BT - (1 + f * BATCH) * BT
                for c in both:
                    nc.vector.tensor_copy(hffn[c][:, :, D], k_sb[:, bass.ds(at + (K_TOKEN + c * TPC), TPC)])
                dve.wait_ge(score_ready, m)
                settle(nc.vector.tensor_tensor(score[:], ps_score, rows_sb[:, None, 0:NE].to_broadcast([P, BT, NE]), ALU.add))
                settle(nc.vector.tensor_tensor(biased[:], score[:], rows_sb[:, None, NE:2 * NE].to_broadcast([P, BT, NE]), ALU.add))
                nc.vector.tensor_copy(score_all[:, bass.ds(at, BT), :], score[:])
                for j in range(BT):
                    last = nc.vector.max(top8[:, j, :], biased[:, j, :])
                settle(last)
                for j in range(BT):
                    last = nc.vector.max_index(top_at[:, j, :], top8[:, j, :], biased[:, j, :])
                settle(last)
                settle(nc.vector.tensor_copy(top_f[:], top_at[:, :, 0:TOPK]))
                settle(nc.vector.tensor_tensor(
                    onehot[:], top_f[:, :, :, None].to_broadcast([P, BT, TOPK, NE]),
                    k_sb[:, None, None, K_IOTA:K_IOTA + NE].to_broadcast([P, BT, TOPK, NE]), ALU.is_equal))
                nc.vector.tensor_tensor(member[:], onehot[:, :, 0, :], onehot[:, :, 1, :], ALU.add).then_inc(member_ready, 1)
                for c in both:
                    nc.vector.tensor_copy(hffn[c][:, :, D + 1], top_f[:, c * TPC:(c + 1) * TPC, 1])
                nc.vector.tensor_copy(onehot_all[:, bass.ds(at, BT), :, :], onehot[:])

            def place(m):
                dve.wait_ge(rank_ready, m)
                nc.vector.tensor_reduce(seen_new[:], member[:].rearrange("p j e -> p e j"), AX.X, ALU.add)
                settle(nc.vector.tensor_tensor(place8[:], ps_rank, k_sb[:, None, K_REGION:K_REGION + NE].to_broadcast([P, BT, NE]), ALU.add))
                nc.vector.tensor_tensor(seen[:], seen[:], seen_new[:], ALU.add).then_inc(seen_ready, 1)
                settle(nc.vector.tensor_tensor(picked[:], onehot[:], place8[:, :, None, :].to_broadcast([P, BT, TOPK, NE]), ALU.mult))
                settle(nc.vector.tensor_reduce(place_f[:], picked[:], AX.X, ALU.add))
                nc.vector.tensor_copy(place_i[:], place_f[:].rearrange("p j k -> p (j k)")).then_inc(place_ready, 1)

            def plan(f):
                begin()
                dve.wait_ge(count_ready, f + 1)
                settle(nc.vector.tensor_copy(count[:], ps_count))
                nc.vector.memset(seen[:], 0.0)
                nc.vector.tensor_scalar(tail_f[:], count[:], k_sb[:, K_PART:K_PART + 1], None, ALU.add)
                settle(nc.vector.tensor_scalar(count_i[:], count[:], float(P - 1), None, ALU.add))
                nc.vector.tensor_tensor(tail_f[:], tail_f[:], k_sb[:, K_REGION:K_REGION + NE], ALU.add)
                settle(nc.vector.tensor_scalar(ntile_i[:], count_i[:], P.bit_length() - 1, None, ALU.arith_shift_right))
                nc.vector.tensor_copy(tail_i[:], tail_f[:]).then_inc(tail_ready, 1)
                settle(nc.vector.tensor_copy(ntile[:], ntile_i[:]))
                settle(nc.vector.tensor_tensor_scan(cum[:], ones8[:], ntile[:], 0.0, ALU.mult, ALU.add))
                nc.vector.tensor_scalar(cum_rows[:], cum[:], float(P), None, ALU.mult)
                nc.vector.tensor_scalar(jump[:], ntile[:], -float(P), float(REGION), ALU.mult, ALU.add)
                settle(nc.vector.tensor_scalar(last_row[:], count[:, NE - 1:NE], float((NE - 1) * REGION), None, ALU.add))
                tile_at = k_sb[:, K_TILE:K_TILE + LOADED]
                shape = [P, NE - 1, LOADED]
                settle(nc.vector.tensor_tensor(past, tile_at[:, None, :].to_broadcast(shape),
                                               cum_rows[:, 0:NE - 1, None].to_broadcast(shape), ALU.is_ge))
                settle(nc.vector.tensor_tensor(past_j[0:1], past[0:1], jump[0:1, 0:NE - 1, None].to_broadcast([1, NE - 1, LOADED]), ALU.mult))
                nc.vector.tensor_reduce(expert_all[:], past.rearrange("p e t -> p t e"), AX.X, ALU.add)
                settle(nc.vector.tensor_reduce(row_f[:], past_j[0:1].rearrange("p e t -> p t e"), AX.X, ALU.add))
                nc.vector.tensor_copy(tile_expert[:], expert_all[0:1, :])
                settle(nc.vector.tensor_tensor(row_g[:], row_f[:], tile_at[0:1], ALU.add))
                nc.vector.tensor_scalar(tile_row[:], row_g[:], last_row[0:1, :], None, ALU.min).then_inc(table_ready, 1)
                settle(nc.vector.tensor_reduce(top_all[:], score_all[:], AX.X, ALU.max))
                nc.vector.tensor_tensor(small_a, score_all[:], top_all[:, :, None].to_broadcast([P, TILES, NE]), ALU.subtract).then_inc(gate_in, 1)
                dve.wait_ge(gate_exp, f + 1)
                settle(nc.vector.tensor_tensor(big, onehot_all[:], small_a[:, :, None, :].to_broadcast([P, TILES, TOPK, NE]), ALU.mult))
                settle(nc.vector.tensor_reduce(gate_w[:], big, AX.X, ALU.add))
                settle(nc.vector.tensor_tensor(gate_sum[:], gate_w[:, :, 0], gate_w[:, :, 1], ALU.add))
                settle(nc.vector.reciprocal(gate_sum[:], gate_sum[:]))
                nc.vector.tensor_tensor(gate_all[:], gate_w[:], gate_sum[:, :, None].to_broadcast([P, TILES, TOPK]), ALU.mult).then_inc(gates_ready, 1)

            def experts(f):
                U, G = f * N_UP, f * N_GATE

                def place(i, t, n):
                    dve.wait_ge(xtile_in[i], (n + (1 + f * (LOADED // STEP))) * 16)
                    dve.wait_ge(y_stored[i], (n + (1 + f * (N_BACK // STEP))) * 16)
                    nc.vector.scalar_tensor_tensor(result_row[i][:], xtile[i][:, D + 1:ROW_W], expert_all[:, bass.ds(t, 1)],
                                                   xtile[i][:, D:D + 1], ALU.is_equal, ALU.add)

                def gate_up(i, n1):
                    dve.wait_ge(silu_ready, n1)
                    nc.vector.tensor_tensor(gated[i][:], silu[i][:], ps_up[i][:, HID:2 * HID], ALU.mult).then_inc(gated_ready, 1)

                def turn(i, n1):
                    dve.wait_ge(gated_turned, n1)
                    nc.vector.tensor_copy(gated_t[i][:], ps_gt[i][:, 0:HID]).then_inc(gatedt_ready, 1)

                place(0, 0, 0)
                gate_up(0, 1 + U)
                with dve.Fori(0, XTILES // STEP) as n:
                    for i in range(STEP):
                        turn(i % 2, n * STEP + (i + 1 + G))
                        place((i + 1) % STEP, n * STEP + (i + 1), n + (i + 1) // STEP)
                        gate_up((i + 1) % 2, n * STEP + (i + 2 + U))

            def rotate(c, m):
                dve.wait_ge(qkv_ready[c], m)
                if c:
                    dve.wait_ge(qf_ready[0], m)
                at = slice(c * TPC, (c + 1) * TPC)
                nc.vector.tensor_tensor(rope1[:], qkv[c][:, :, 0:2 * D], rope_c[:, at, :], ALU.mult)
                pairs = lambda a: a.rearrange("p j (m r) -> p j m r", r=2)
                a, s, o = pairs(qkv[c][:, :, 0:2 * D]), pairs(rope_s[:, at, :]), pairs(rope2[:])
                for r in range(2):
                    last = nc.vector.tensor_tensor(o[:, :, :, r], a[:, :, :, 1 - r], s[:, :, :, r], ALU.mult)
                settle(last)
                added = mark(nc.vector.tensor_tensor(rope1[:], rope1[:], rope2[:], ALU.add))
                dve.wait_ge(qkdev_ready[c], m)
                settle(nc.vector.reciprocal(qk_rstd[c][:], qk_dev[c][:]))
                need(added)
                for half, dst, ready in ((1, kf[c], kf_ready[c]), (0, qf[c], qf_ready[c])):
                    for j in range(TPC):
                        last = nc.vector.tensor_scalar(dst[:, j, :], rope1[:, j, half * D:(half + 1) * D],
                                                       qk_rstd[c][:, half, j:j + 1], 0.0, ALU.mult, ALU.max)
                    last.then_inc(ready, 1)

            def divide(m):
                dve.wait_ge(res_ready, m)
                settled = [mark(nc.vector.tensor_scalar(den_a[c][:], ps_den[c], LIN_EPS, None, ALU.add)) for c in both]
                for c in both:
                    need(settled[c])
                    settled[c] = mark(nc.vector.reciprocal(rden[c][:], den_a[c][:]))
                heads = lambda a: a.rearrange("p j (h d) -> p j h d", d=DH)
                for c in both:
                    need(settled[c])
                    nc.vector.tensor_tensor(heads(attn[c][:]), heads(tiles4(ps_half[c])),
                                            rden[c][:, :, :, None].to_broadcast([P, TPC, HEADS, DH]), ALU.mult).then_inc(attn_ready[c], 1)

            def residual(m):
                scaled = []
                for c in both:
                    dve.wait_ge(outdev_ready[c], m)
                    settle(nc.vector.reciprocal(out_rstd[c][:], out_dev[c][:]))
                    for j in range(TPC):
                        last = nc.vector.scalar_tensor_tensor(onorm[c][:, j, :], tiles4(ps_half[c])[:, j, :], out_rstd[c][:, j:j + 1],
                                                              gout_sb[:], ALU.mult, ALU.mult)
                    scaled.append(mark(last))
                for c in both:
                    dve.wait_ge(x_stored[c], m * 16)
                    dve.wait_ge(xold_loaded[c], m * 16)
                    need(scaled[c])
                    nc.vector.tensor_tensor(xres[c][:], onorm[c][:], xold[c][:], ALU.add).then_inc(xres_ready[c], 1)
                for c in both:
                    dve.wait_ge(xres_ready[c], m)
                moments(xres, stats2, moment2, var2_ready)

            def attention(done, ahead):
                begin()
                if done is not None:
                    divide(done)
                if ahead is not None:
                    for c in both:
                        dve.wait_ge(x_loaded[c], ahead * 16)
                    moments(xin, stats, moment, var_ready)
                    normalise(ahead, xin, moment, dev_ready, dev, rstd, hmix, h_ready)
                if done is not None:
                    residual(done)
                    normalise_for_experts(done)
                if ahead is not None:
                    for c in both:
                        rotate(c, ahead)
                if done is not None:
                    choose(done, FIRST)
                    place(done)
                if ahead is not None:
                    dve.wait_ge(vk_ready, ahead)
                    nc.vector.tensor_tensor(state[:, 0:D], ps_vk[:, 0:D], k_sb[:, K_BLOCK:K_BLOCK + P], ALU.mult)
                    nc.vector.tensor_scalar(state[:, D:RES_W], k_sb[:, K_HEAD:K_HEAD + HEADS], ps_vk[:, D:D + 1], None, ALU.mult).then_inc(state_ready, 1)

            def way_in(m):
                for c in both:
                    dve.wait_ge(xmid_ready[c], m - BATCH)
                moments(xmid, stats, moment, var_ready)
                normalise(m, xmid, moment, dev_ready, dev, rstd, hmix, h_ready)

            def recurrences(m):
                before, after = slice(0, SEQ), slice(1, 1 + SEQ)
                first = ch_sb[:, V_FIRST:V_FIRST + 1]
                row = m - BATCH
                dve.wait_ge(k_ready, row)
                settle(nc.vector.tensor_tensor_scan(top[:, after], w_sb[:].to_broadcast([P, SEQ]), ps_k, top[:, 0:1], ALU.add, ALU.max))
                nc.vector.scalar_tensor_tensor(expo[:, 2, :], top[:, before], w_sb[:, 0:1], top[:, after], ALU.add, ALU.subtract)
                nc.vector.tensor_tensor(expo[:, 3, :], ps_k, top[:, after], ALU.subtract).then_inc(past_expo, 1)
                settle(nc.vector.scalar_tensor_tensor(qmax, ps_k, first, top[:, before], ALU.add, ALU.max))
                nc.vector.tensor_tensor(expo[:, 0, :], top[:, before], qmax, ALU.subtract)
                nc.vector.scalar_tensor_tensor(expo[:, 1, :], ps_k, first, qmax, ALU.add, ALU.subtract).then_inc(now_expo, 1)
                dve.wait_ge(past_ex, row)
                dve.wait_ge(v_ready, row)
                settle(nc.vector.tensor_tensor(ev, expo[:, 3, :], ps_v, ALU.mult))
                num_done = mark(nc.vector.tensor_tensor_scan(num[:, after], expo[:, 2, :], ev, num[:, 0:1], ALU.mult, ALU.add))
                den_done = mark(nc.vector.tensor_tensor_scan(den[:, after], expo[:, 2, :], expo[:, 3, :], den[:, 0:1], ALU.mult, ALU.add))
                dve.wait_ge(now_ex, row)
                nc.vector.tensor_tensor(y_b, expo[:, 1, :], ps_v, ALU.mult)
                need(num_done)
                num_done = mark(nc.vector.tensor_tensor(y_num, expo[:, 0, :], num[:, before], ALU.mult))
                need(den_done)
                den_done = mark(nc.vector.tensor_tensor(y_den, expo[:, 0, :], den[:, before], ALU.mult))
                need(num_done)
                nc.vector.tensor_tensor(y_num, y_num, y_b, ALU.add)
                need(den_done)
                settle(nc.vector.tensor_tensor(y_den, y_den, expo[:, 1, :], ALU.add))
                dve.wait_ge(er_ready, row)
                settle(nc.vector.scalar_tensor_tensor(y_den, e_r, 1.0, y_den, ALU.add, ALU.mult))
                inverted = []
                for c in both:
                    part = slice(c * CHUNK, (c + 1) * CHUNK)
                    settle(nc.vector.reciprocal(y_den[:, part], y_den[:, part]))
                    nc.vector.tensor_tensor(rwkv[:, part], y_num[:, part], y_den[:, part], ALU.mult).then_inc(rwkv_ready[c], 1)

            def mixing(m, last):
                begin()
                recurrences(m)
                for c in both:
                    dve.wait_ge(mixed_ready[c], m - BATCH)
                    dve.wait_ge(x_stored[c], m * 16)
                    nc.vector.tensor_tensor(xres[c][:], tiles4(ps_half[c]), xmid[c][:], ALU.add).then_inc(xres_ready[c], 1)
                for c in both:
                    dve.wait_ge(xres_ready[c], m)
                moments(xres, stats2, moment2, var2_ready)
                normalise_for_experts(m)
                if not last:
                    way_in(m + 1)
                choose(m, SECOND)
                place(m)

            nc.vector.memset(seen[:], 0.0)
            for c in range(HALVES):
                dve.sem_inc(x_stored[c], 16)
                dve.sem_inc(out_stored[c], 16)
            attention(None, 1)
            with dve.Fori(1, BATCH) as m:
                attention(m, m + 1)
            attention(BATCH, None)
            plan(FIRST)
            experts(FIRST)
            begin()
            way_in(BATCH + 1)
            with dve.Fori(BATCH + 1, 2 * BATCH) as m:
                mixing(m, False)
            mixing(2 * BATCH, True)
            plan(SECOND)
            experts(SECOND)
            with dve.Fori(BATCH + 1, 2 * BATCH + 1) as m:
                combine(dve, nc.vector, 0, m, SECOND)


def kernel(**inputs):
    import numpy as np
    import concourse.bacc as bacc
    from concourse.bass_utils import run_bass_kernel_spmd

    def wide(v):
        return np.ascontiguousarray(np.broadcast_to(v.reshape(1, -1), (P, v.size)))

    def dense(a):
        return np.ascontiguousarray(a)

    a = {k: np.asarray(v) for k, v in inputs.items()}
    at = lambda name: a["L0_attn_a_" + name]
    mt = lambda name: a["L0_attn_b_" + name]
    ff = lambda name: a["L0_ffn_" + name]

    freq = (1.0 / np.float32(10000.0) ** (np.arange(0, DH, 2, dtype=np.float32) / np.float32(DH))).astype(np.float32)
    angle = np.outer(np.arange(SEQ, dtype=np.float32), freq)
    by_feature = lambda t: dense(np.tile(np.repeat(t, 2, axis=1), (1, HEADS)).reshape(SEQ // P, P, D).transpose(1, 0, 2))
    sign = np.tile(np.array([-1.0, 1.0], np.float32), D // 2)
    cosine = by_feature(np.cos(angle).astype(np.float32))
    sine = dense(by_feature(np.sin(angle).astype(np.float32)) * sign)

    consts = np.zeros((P, K_ALL), np.float32)
    part, feature = np.arange(P), np.arange(D)
    consts[:, K_ID:K_ID + P] = np.eye(P)
    consts[:, K_TRI:K_TRI + P] = np.triu(np.ones((P, P)), 1)
    consts[:, K_BLOCK:K_BLOCK + P] = feature[:, None] // DH == feature[None, :] // DH
    consts[:, K_HEAD:K_HEAD + HEADS] = feature[:, None] // DH == np.arange(HEADS)[None, :]
    consts[:, K_IOTA:K_IOTA + NE] = np.arange(NE)
    consts[:, K_REGION:K_REGION + NE] = np.arange(NE) * REGION
    consts[:, K_PART] = part
    consts[:, K_TILE:K_TILE + LOADED] = np.arange(LOADED) * P
    consts[:, K_TOKEN:K_TOKEN + TILES] = (np.arange(TILES)[None, :] * P + part[:, None]) * TOPK

    swap = lambda g: g.reshape(-1, 2)[:, ::-1].reshape(-1)
    biases = np.concatenate([at("bqkv"), at("bout"), ff("bl1").reshape(-1), ff("bl2").reshape(-1)])
    arrays = {
        "x": dense(at("x").reshape(TOKENS, D)),
        "cosine": cosine, "sine": sine, "consts": consts,
        "w_qkv": dense(at("Wqkv").T), "w_out": dense(at("Wout").T),
        "g_qk": wide(np.concatenate([at("gq"), at("gk")])),
        "g_qk_swapped": wide(np.concatenate([swap(at("gq")), swap(at("gk"))])),
        "g_out": wide(at("gout")), "bias_cols": dense(biases.reshape(P, B_ALL // P)),
        "w_router": dense(ff("Wr").T), "router_rows": wide(np.concatenate([ff("br"), ff("biases_N")])),
        "w_up": dense(ff("Wl1").transpose(1, 0, 2).reshape(D, -1)),
        "w_down": dense(ff("Wl2").reshape(NE, HCH, P, D).transpose(2, 0, 1, 3).reshape(P, -1)),
        "channel": dense(np.stack([mt("time_decay"), mt("time_first"), mt("time_mix_k").reshape(-1),
                                   mt("time_mix_v").reshape(-1), mt("time_mix_r").reshape(-1)], axis=1)),
        "w_k": dense(mt("Wk").T), "w_v": dense(mt("Wv").T), "w_r": dense(mt("Wr").T), "w_o": dense(mt("Wo").T),
    }
    nc = bacc.Bacc("TRN2", target_bir_lowering=False, num_devices=1)
    args = {name: nc.dram_tensor(name, v.shape, mybir.dt.from_np(v.dtype), kind="ExternalInput").ap()
            for name, v in arrays.items()}
    out = nc.dram_tensor("out", (TOKENS, D), F32, kind="ExternalOutput").ap()
    program(nc, out=out, **args)
    result = run_bass_kernel_spmd(nc, [arrays], core_ids=[0])
    return result.results[0]["out"].reshape(BATCH, SEQ, D)
```

```python
from contextlib import ExitStack

import concourse.bass as bass
from concourse import mybir

F32 = mybir.dt.float32
F32R = mybir.dt.float32r
BF16 = mybir.dt.bfloat16
I32 = mybir.dt.int32
U32 = mybir.dt.uint32
ALU = mybir.AluOpType
ACT = mybir.ActivationFunctionType
AX = mybir.AxisListType

P = 128
BATCH, SEQ, D = 8, 1024, 128
TOKENS = BATCH * SEQ
TPC = 4
CHUNK = TPC * P
HALVES = SEQ // CHUNK
CHUNKS = TOKENS // CHUNK
TILES = TOKENS // P
HEADS, DH = 16, 8
NE, TOPK, HID = 8, 2, 256
HCH = HID // P
ROW_W = D + 2
NO_RESULT = TOKENS * TOPK
XPARTS = 2
XROWS = XPARTS * P
REGION = TOKENS + XROWS
STEP = 8
XTILES = -(-(TOKENS * TOPK // XROWS + NE - 1) // STEP) * STEP
LOADED = XTILES + STEP
RES_W = D + HEADS
BT = HALVES * TPC
RING = 4
LN_EPS, RMS_EPS, LIN_EPS = 1e-5, 1.1920929e-07, 1e-6
NO_PAST = -1e38

B_QKV, B_OUT = 0, 3 * D
B_ALL = B_OUT + D

K_ID, K_TRI, K_BLOCK = 0, P, 2 * P
K_HEAD = 3 * P
K_IOTA = K_HEAD + HEADS
K_REGION = K_IOTA + NE
K_PART = K_REGION + NE
K_TILE = K_PART + 1
K_TOKEN = K_TILE + LOADED
K_ALL = K_TOKEN + TILES

V_DECAY, V_FIRST, V_MIXK, V_MIXV, V_MIXR = range(5)


def program(nc, x, cosine, sine, consts, w_qkv, w_out, g_qk, g_qk_swapped, g_out, bias_cols, w_router,
            router_rows, w_up, w_down, up_bias, down_bias, channel, w_k, w_v, w_r, w_o, out):
    with ExitStack() as ctx:
        def sb(name, shape, dt=F32):
            return ctx.enter_context(nc.sbuf_tensor(name, shape, dt))

        def sem(name):
            return ctx.enter_context(nc.semaphore(name))

        def sem2(name):
            return [sem(f"{name}{c}") for c in range(HALVES)]

        def dram(name, shape, dt=F32):
            return nc.dram_tensor(name, shape, dt).ap()

        x1_dram = dram("x1_dram", [TOKENS, D])
        x3_dram = dram("x3_dram", [TOKENS, D])
        queue_dram = dram("queue_dram", [NE * REGION, ROW_W])
        result_dram = dram("result_dram", [NO_RESULT + P + STEP, D])
        split_dram = dram("split_dram", [3, B_ALL], BF16)

        k_sb = sb("k_sb", [P, K_ALL])
        wqkv_sb = sb("wqkv_sb", [P, 3 * D])
        wout_sb = sb("wout_sb", [P, D])
        wrouter_sb = sb("wrouter_sb", [P, NE])
        up_bias_sb = sb("up_bias_sb", [P, NE * 2 * HCH])
        down_bias_sb = sb("down_bias_sb", [P, NE * D])
        rows_sb = sb("rows_sb", [P, 2 * NE])
        up_hi = sb("up_hi", [P, NE * 2 * HID], F32R)
        wdown_sb = sb("wdown_sb", [P, NE * HCH * D])
        gqk_sb = sb("gqk_sb", [P, 2 * D])
        gqks_sb = sb("gqks_sb", [P, 2 * D])
        gout_sb = sb("gout_sb", [P, D])
        rope_c = sb("rope_c", [P, SEQ // P, 2 * D])
        rope_s = sb("rope_s", [P, SEQ // P, 2 * D])
        bias_sb = sb("bias_sb", [P, B_ALL // P])
        bias_left = sb("bias_left", [P, B_ALL // P])
        bias_parts = sb("bias_parts", [P, 3, B_ALL // P], BF16)
        bias_rows = sb("bias_rows", [P, B_ALL], BF16)
        ones_bf = sb("ones_bf", [P, P], BF16)
        tri_bf = sb("tri_bf", [P, P], BF16)
        ones8 = sb("ones8", [P, NE])
        ln_eps = sb("ln_eps", [P, 1])
        rms_eps = sb("rms_eps", [P, 1])
        ch_sb = sb("ch_sb", [P, 5])
        w_sb = sb("w_sb", [P, 1])
        exp_decay = sb("exp_decay", [P, 1])
        mix_left = sb("mix_left", [P, 3])
        wkvr_sb = sb("wkvr_sb", [P, 3, D])
        wnow_sb = sb("wnow_sb", [P, 3, D])
        wpast_sb = sb("wpast_sb", [P, 3, D])
        wo_sb = sb("wo_sb", [P, D])
        tail_rows = sb("tail_rows", [P, ROW_W])
        ident = k_sb[:, K_ID:K_ID + P]

        halves = lambda name, shape, dt=F32: [sb(f"{name}{c}", shape, dt) for c in range(HALVES)]
        xin = halves("xin", [P, TPC, D])
        xold = halves("xold", [P, TPC, D])
        xsum = xold
        xmid = halves("xmid", [P, TPC, D])
        xres = halves("xres", [P, TPC, D])
        hmix = halves("hmix", [P, TPC, D])
        hffn = halves("hffn", [P, TPC, ROW_W])
        stats = halves("stats", [P, TPC, 6])
        moment = halves("moment", [P, TPC, 2])
        dev = halves("dev", [P, TPC])
        rstd = halves("rstd", [P, TPC])
        shift = halves("shift", [P, TPC])
        shift2 = halves("shift2_", [P, TPC])
        stats2 = halves("stats2_", [P, TPC, 6])
        moment2 = halves("moment2_", [P, TPC, 2])
        dev2 = halves("dev2_", [P, TPC])
        rstd2 = halves("rstd2_", [P, TPC])
        hffn_t = halves("hffn_t", [P, CHUNK])

        qkv = halves("qkv", [P, TPC, 3 * D + 1])
        with nc.sbuf_tensor("rotated0", [P, TPC, 2 * D], F32) as rotated0, nc.sbuf_tensor("rotated1", [P, TPC, 2 * D], F32) as rotated1:
            rotated = [rotated0, rotated1]
        tile_up = [sb(f"tile_up{i}", [P, 2, 2 * HID], F32R) for i in range(2)]
        rope2 = sb("rope2", [P, TPC, 2 * D])
        num = sb("num", [P, 1 + SEQ])
        den = sb("den", [P, 1 + SEQ])
        kf, onorm = ([a[:, 1 + c * CHUNK:1 + (c + 1) * CHUNK].rearrange("p (j d) -> p j d", d=D) for c in range(HALVES)]
                     for a in (num, den))
        out_squares = sb("out_squares", [P, TPC, D])
        squares = sb("squares", [P, 2, TPC, D])
        sumsq = halves("sumsq", [P, 2, TPC])
        qk_dev = halves("qk_dev", [P, 2, TPC])
        qk_rstd = halves("qk_rstd", [P, 2, TPC])
        state = sb("state", [P, RES_W])
        den_a = halves("den_a", [P, TPC, HEADS])
        rden = halves("rden", [P, TPC, HEADS])
        out_sum = halves("out_sum", [P, TPC])
        out_dev = halves("out_dev", [P, TPC])
        out_rstd = halves("out_rstd", [P, TPC])

        score = sb("score", [P, BT, NE])
        biased = sb("biased", [P, BT, NE])
        top8 = sb("top8", [P, BT, 8])
        top_at = sb("top_at", [P, BT, 8], U32)
        top_f = sb("top_f", [P, BT, TOPK])
        onehot = sb("onehot", [P, BT, TOPK, NE])
        member = sb("member", [P, BT, NE], BF16)
        seen = sb("seen", [P, NE], BF16)
        seen_new = sb("seen_new", [P, NE])
        place8 = sb("place8", [P, BT, NE])
        picked = sb("picked", [P, BT, TOPK, NE])
        place_f = sb("place_f", [P, BT, TOPK])
        place_i = sb("place_i", [P, BT * TOPK], I32)
        score_all = sb("score_all", [P, TILES, NE])
        onehot_all = sb("onehot_all", [P, TILES, TOPK, NE])
        flat = lambda a: a[:].rearrange("p j n -> p (j n)")
        big = flat(rope2).rearrange("p (t k e) -> p t k e", k=TOPK, e=NE)
        small_a = squares[:].rearrange("p a j n -> p (a j n)")[:, 0:TILES * NE].rearrange("p (t e) -> p t e", e=NE)
        past, past_j = (flat(rotated[i])[:, 0:(NE - 1) * LOADED].rearrange("p (e t) -> p e t", e=NE - 1) for i in range(2))
        cos_sb, sin_sb = (flat(rotated[i]).rearrange("p (t d) -> p t d", d=D) for i in range(2))
        top_all = sb("top_all", [P, TILES])
        gate_w = sb("gate_w", [P, TILES, TOPK])
        gate_sum = sb("gate_sum", [P, TILES])
        gate_all = sb("gate_all", [P, TILES, TOPK])
        count = sb("count", [P, NE])
        count_i = sb("count_i", [P, NE], I32)
        ntile_i = sb("ntile_i", [P, NE], I32)
        ntile = sb("ntile", [P, NE])
        cum = sb("cum", [P, NE])
        cum_rows = sb("cum_rows", [P, NE])
        jump = sb("jump", [P, NE])
        tail_f = sb("tail_f", [P, NE])
        tail_i = sb("tail_i", [P, NE], I32)
        last_row = sb("last_row", [P, 1])
        expert_all = sb("expert_all", [P, LOADED])
        row_f, row_g = (out_squares[:].rearrange("p j n -> p (j n)")[0:1, i * LOADED:(i + 1) * LOADED] for i in range(2))
        tile_row = sb("tile_row", [1, LOADED], I32)
        tile_expert = sb("tile_expert", [1, LOADED], I32)

        xtile = [sb(f"xtile{i}", [P, XPARTS, ROW_W]) for i in range(STEP)]
        result_row = [sb(f"result_row{i}", [P, XPARTS], I32) for i in range(STEP)]
        ytile = [sb(f"ytile{i}", [P, XPARTS, D]) for i in range(STEP)]

        back_x = [qkv[c][:].rearrange("p j n -> p (j n)")[:, 0:TPC * TOPK * D].rearrange("p (m d) -> p m d", d=D) for c in range(HALVES)]
        gate = sb("gate", [P, BT * TOPK])
        gate4 = sb("gate4", [P, RING * TPC * TOPK])
        final_out = xsum + xmid
        hseq = sb("hseq", [P, 1 + SEQ])
        top = sb("top", [P, 1 + SEQ])
        y_num, y_den = (rope_c[:, i * TPC:(i + 1) * TPC, :].rearrange("p j n -> p (j n)") for i in range(2))
        y_b, e_r = (rope_s[:, i * TPC:(i + 1) * TPC, :].rearrange("p j n -> p (j n)") for i in range(2))
        gap, ev = (a[:].rearrange("p j n -> p (j n)") for a in rotated)
        gap_past = rope2[:].rearrange("p j n -> p (j n)")
        rwkv = squares[:].rearrange("p a j n -> p (a j n)")

        hmix_t = halves("hmix_t", [P, CHUNK])
        qf, attn = halves("qf", [P, TPC, D]), halves("attn", [P, TPC, D])
        qf_t, attn_t = halves("qf_t", [P, CHUNK]), halves("attn_t", [P, CHUNK])
        pair2 = lambda name, shape, dt: [sb(f"{name}{i}", shape, dt) for i in range(2)]
        xt_parts = pair2("xt_parts", [P, 2, XROWS], F32R)
        gated = pair2("gated", [P, HCH, XROWS], F32)
        tile_bias = [sb(f"tile_bias{i}", [P, 2 * HCH]) for i in range(STEP)]
        with nc.sbuf_tensor("expo", [P, 4, SEQ], F32) as expo:
            pass
        up_lo = sb("up_lo", [P, NE * 2 * HID], F32R)
        up_raw = expo[:].rearrange("p a n -> p (a n)")
        final_x = ([a.rearrange("p (j d) -> p j d", d=D) for t in (rope_c, rope_s) for a in
                    (t[:].rearrange("p j n -> p (j n)")[:, i * CHUNK:(i + 1) * CHUNK] for i in range(TPC))]
                   + [a[:, 1 + i * CHUNK:1 + (i + 1) * CHUNK].rearrange("p (j d) -> p j d", d=D)
                      for a in (hseq, top, num, den) for i in range(HALVES)])
        final_y = back_x + [expo[:, i, :].rearrange("p (m d) -> p m d", d=D) for i in range(2)]

        banks = ctx.enter_context(nc.psum_tensor("banks", [P, 8, CHUNK], F32))
        bank = [banks[:, i, :] for i in range(8)]
        tiles4 = lambda a: a.rearrange("p (j n) -> p j n", j=TPC)
        ps_half = [bank[0], bank[1]]
        ps_small = bank[2]
        ps_vk = bank[3]
        ps_turn = [bank[4], bank[5]]
        ps_qkv = [bank[6], bank[7]]
        ps_den = [ps_turn[c][:, 0:TPC * HEADS].rearrange("p (j h) -> p j h", j=TPC) for c in range(HALVES)]
        ps_score = ps_small[:, 0:BT * NE].rearrange("p (j e) -> p j e", e=NE)
        ps_rank = ps_small[:, 64:64 + BT * NE].rearrange("p (j e) -> p j e", e=NE)
        ps_count = ps_small[:, 128:128 + NE]
        ps_up = [banks[:, 2 * i:2 * i + 2, :].rearrange("p a (h n) -> p (a h) n", n=XROWS) for i in range(2)]
        ps_xt, ps_y = ([a[:, 0:XROWS] for a in bank[i:i + 2]] for i in (4, 6))
        pair = lambda i: banks[:, i:i + 2, :].rearrange("p a n -> p (a n)")
        ps_r = pair(0)
        ps_turn3 = bank[3]
        ps_k, ps_v = pair(4), pair(6)

        consts_in, weights_in, rope_in, experts_in = sem("consts_in"), sem("weights_in"), sem("rope_in"), sem("experts_in")
        bias_in, split_out, rows_in, rows_zero = sem("bias_in"), sem("split_out"), sem("rows_in"), sem("rows_zero")
        dve_step, act_step, place_step = sem("dve_step"), sem("act_step"), sem("place_step")
        setup_done, split_done = sem("setup_done"), sem("split_done")
        x_loaded, xold_loaded, x_stored = sem2("x_loaded"), sem2("xold_loaded"), sem2("x_stored")
        var_ready, dev_ready, h_ready, h_turned, ht_ready = (
            sem2("var_ready"), sem2("dev_ready"), sem2("h_ready"), sem2("h_turned"), sem2("ht_ready"))
        qkv_done, qkv_taken, qkdev_ready, qkrstd_ready, rotated_ready = (
            sem("qkv_done"), sem("qkv_taken"), sem2("qkdev_ready"), sem2("qkrstd_ready"), sem2("rotated_ready"))
        kf_ready, qf_ready, qf_turned, qft_ready = sem2("kf_ready"), sem2("qf_ready"), sem2("qf_turned"), sem2("qft_ready")
        vk_ready, state_ready, res_ready = sem("vk_ready"), sem("state_ready"), sem("res_ready")
        attn_ready, attn_turned, attnt_ready = sem2("attn_ready"), sem2("attn_turned"), sem2("attnt_ready")
        out_ready, outdev_ready, xres_ready = sem2("out_ready"), sem2("outdev_ready"), sem2("xres_ready")
        scale_ready, scale2_ready = sem2("scale_ready"), sem2("scale2_ready")
        var2_ready, dev2_ready, h2_ready, h2_turned, h2t_ready = (
            sem2("var2_ready"), sem2("dev2_ready"), sem2("h2_ready"), sem2("h2_turned"), sem2("h2t_ready"))
        score_ready, member_ready, rank_ready = sem("score_ready"), sem("member_ready"), sem("rank_ready")
        place_ready = sem("place_ready")
        queued = sem2("queued")
        seen_ready, count_ready, tail_ready, tails_queued = (
            sem("seen_ready"), sem("count_ready"), sem("tail_ready"), sem("tails_queued"))
        table_ready, gate_in, gate_exp = sem("table_ready"), sem("gate_in"), sem("gate_exp")
        xtile_in = [sem(f"xtile_in{i}") for i in range(STEP)]
        hi_ready, lo_ready = sem("hi_ready"), sem("lo_ready")
        xhi_ready, xlo_ready = sem("xhi_ready"), sem("xlo_ready")
        xtile_turned, up_ready, silu_ready, gated_ready = (
            sem("xtile_turned"), sem("up_ready"), sem("silu_ready"), sem("gated_ready"))
        wlo_ready, whi_ready, y_ready, ytile_ready = sem("wlo_ready"), sem("whi_ready"), sem("y_ready"), sem("ytile_ready")
        y_stored = [sem(f"y_stored{i}") for i in range(STEP)]
        results_in, place_taken = sem2("results_in"), sem("place_taken")
        gates_ready, gate_taken, weighted, first_added, xsum_ready = (
            sem("gates_ready"), sem("gate_taken"), sem2("weighted"), sem2("first_added"), sem2("xsum_ready"))
        k_ready, v_ready, r_ready = sem("k_ready"), sem("v_ready"), sem("r_ready")
        past_expo, past_ex, now_expo, gap_ready, now_ex, er_ready = (
            sem("past_expo"), sem("past_ex"), sem("now_expo"), sem("gap_ready"), sem("now_ex"), sem("er_ready"))
        ev_ready = sem("ev_ready")
        xold_copied = sem2("xold_copied")
        rwkv_ready, mixed_ready = sem2("rwkv_ready"), sem2("mixed_ready")
        final_in, out_stored = ([sem(f"{name}{i}") for i in range(RING)] for name in ("final_in", "out_stored"))
        final_x_in = sem("final_x_in")
        final_weighted, final_first, final_ready = sem("final_weighted"), sem("final_first"), sem("final_ready")

        block = ctx.enter_context(nc.Block())

        def rows(dram_ap, chunk):
            return dram_ap[bass.ds(chunk * CHUNK, CHUNK), :].rearrange("(j p) d -> p j d", p=P)

        FIRST, SECOND = 0, 1
        N_TURN, N_WEIGHTS, N_UP, N_GATE, N_BACK = (XTILES + ahead for ahead in (3, 2, 1, 1, 0))
        PLACE_STEPS = 3
        SCATTERS = 16 * TPC * TOPK

        def read(engine, entries, largest):
            return nc.values_load_multi_w_load_instructions(
                entries, engines=[engine], min_val=0, max_val=largest,
                skip_runtime_bounds_check_because="the table's entries are clamped where they are made")[1]

        def round_of(t, i, before, dmas=1):
            if isinstance(t, int):
                return (t // STEP + 1 + before) * (16 * dmas)
            return (t - i % STEP) * (16 * dmas // STEP) + 16 * dmas * (1 + before)

        def stored_before(t, i, f):
            return round_of(t, i, f * (XTILES // STEP) - 1, XPARTS) + 16

        FIRST_USED = [(k_sb[:], consts), (wqkv_sb[:], w_qkv)]
        ROPE = [(cos_sb, cosine), (sin_sb, sine), (gqk_sb[:], g_qk), (gqks_sb[:], g_qk_swapped)]
        WEIGHTS = [(wout_sb[:], w_out), (wrouter_sb[:], w_router), (rows_sb[:], router_rows), (up_bias_sb[:], up_bias), (down_bias_sb[:], down_bias), (gout_sb[:], g_out),
                   (ch_sb[:], channel), (wkvr_sb[:, 0, :], w_k), (wkvr_sb[:, 1, :], w_v), (wkvr_sb[:, 2, :], w_r),
                   (wo_sb[:], w_o)]
        EXPERTS = [(up_raw, w_up), (wdown_sb[:], w_down)]

        @block.sync
        def _(sp):
            sp.dma_start(bias_sb[:], bias_cols).then_inc(bias_in, 16)
            for c in range(HALVES):
                sp.dma_start(xin[c][:], rows(x, c)).then_inc(x_loaded[c], 16)
            for group, loaded in ((FIRST_USED, consts_in), (ROPE, rope_in), (WEIGHTS, weights_in)):
                for dst, src in group:
                    sp.dma_start(dst, src).then_inc(loaded, 16)
            for c in range(HALVES):
                sp.dma_start(xold[c][:], rows(x, c)).then_inc(xold_loaded[c], 16)
            for dst, src in EXPERTS:
                sp.dma_start(dst, src).then_inc(experts_in, 16)

            def load_results(chunk, dst, loaded):
                rows_of = result_dram[bass.ds(chunk * (CHUNK * TOPK), CHUNK * TOPK), :]
                sp.dma_start(dst.rearrange("p (j k) d -> p j k d", k=TOPK),
                             rows_of.rearrange("(j p k) d -> p j k d", p=P, k=TOPK)).then_inc(loaded, 16)

            def store(c, m, dst, row):
                sp.wait_ge(xres_ready[c], m)
                sp.dma_start(rows(dst, row * HALVES + c), xres[c][:]).then_inc(x_stored[c], 16)

            def tails(f):
                sp.wait_ge(tail_ready, f + 1)
                for e in range(NE):
                    row = sp.value_load(tail_i[0:1, e:e + 1], min_val=0, max_val=NE * REGION - XROWS)
                    sp.dma_start(queue_dram[bass.ds(row, XROWS), :].rearrange("(h p) w -> p h w", p=P),
                                 tail_rows[:, None, :].to_broadcast([P, XPARTS, ROW_W])).then_inc(tails_queued, 16)

            def experts(f):
                tails(f)
                for c in range(HALVES):
                    sp.wait_ge(queued[c], 16 + SCATTERS * BATCH * (f + 1))
                sp.wait_ge(tails_queued, 16 * NE * (f + 1))
                sp.wait_ge(table_ready, f + 1)

                def load(t, i):
                    row = sp.value_load(tile_row[0:1, bass.ds(t, 1)], min_val=0, max_val=NE * REGION - XROWS)
                    sp.dma_start(xtile[i][:], queue_dram[bass.ds(row, XROWS), :].rearrange("(h p) w -> p h w", p=P)).then_inc(xtile_in[i], 16)

                for t in range(STEP):
                    load(t, t)
                with sp.Fori(0, XTILES // STEP) as n:
                    for i in range(STEP):
                        sp.wait_ge(gated_ready, n * STEP + (i + 1 + f * N_GATE))
                        load(n * STEP + (i + STEP), i)
                for i in range(STEP):
                    sp.wait_ge(xtile_in[i], 16 * (LOADED // STEP) * (f + 1))
                    sp.wait_ge(y_stored[i], 16 * (XPARTS * (XTILES // STEP) * (f + 1) + 1))
                if f == FIRST:
                    for c in range(HALVES):
                        load_results(c, back_x[c], results_in[c])

            def next_residual(m):
                for c in range(HALVES):
                    store(c, m, x1_dram, m - 1)
                    sp.dma_start(xold[c][:], rows(x, m * HALVES + c)).then_inc(xold_loaded[c], 16)

            for c in range(HALVES):
                sp.wait_ge(h_ready[c], 1)
                sp.dma_start(xin[c][:], rows(x, HALVES + c)).then_inc(x_loaded[c], 16)
            with sp.Fori(1, BATCH - 1) as m:
                for c in range(HALVES):
                    sp.wait_ge(h_ready[c], m + 1)
                    sp.dma_start(xin[c][:], rows(x, m * HALVES + (HALVES + c))).then_inc(x_loaded[c], 16)
                next_residual(m)
            next_residual(BATCH - 1)
            for c in range(HALVES):
                store(c, BATCH, x1_dram, BATCH - 1)
                sp.wait_ge(x_stored[c], 16 * (BATCH + 1))
                sp.dma_start(xin[c][:], rows(x1_dram, c)).then_inc(x_loaded[c], 16)
            experts(FIRST)
            def load_sums(m):
                for c in range(HALVES):
                    sp.wait_ge(xsum_ready[c], m)
                    sp.dma_start(xin[c][:], rows(x1_dram, m * HALVES + c)).then_inc(x_loaded[c], 16)
                    load_results(m * HALVES + c, back_x[c], results_in[c])

            load_sums(1)
            with sp.Fori(BATCH + 1, 2 * BATCH - 1) as m:
                load_sums(m - (BATCH - 1))
                for c in range(HALVES):
                    store(c, m, x3_dram, m - (1 + BATCH))
            for c in range(HALVES):
                store(c, 2 * BATCH - 1, x3_dram, BATCH - 2)
            for c in range(HALVES):
                store(c, 2 * BATCH, x3_dram, BATCH - 1)
                sp.wait_ge(x_stored[c], 16 * (2 * BATCH + 1))
            sp.dma_start(up_raw, w_up).then_inc(experts_in, 16)
            for chunk in range(CHUNKS):
                sp.dma_start(final_x[chunk], rows(x3_dram, chunk)).then_inc(final_x_in, 16)
            experts(SECOND)

            def load_final(i, chunk):
                load_results(chunk, final_y[i], final_in[i])

            def store_final(i, chunk):
                sp.dma_start(rows(out, chunk), final_out[i][:]).then_inc(out_stored[i], 16)

            for i in range(RING):
                load_final(i, i)
            with sp.Fori(1, CHUNKS // RING) as n:
                for i in range(RING):
                    sp.wait_ge(final_ready, n * RING + (i + 1 - RING))
                    load_final(i, n * RING + i)
                    store_final(i, n * RING + (i - RING))
            for i in range(RING):
                sp.wait_ge(final_ready, CHUNKS - RING + i + 1)
                store_final(i, CHUNKS - RING + i)
            for i in range(RING):
                sp.wait_ge(out_stored[i], 16 * (CHUNKS // RING + 1))

        @block.gpsimd
        def _(pool):
            def scatter(m):
                pool.wait_ge(place_ready, m)
                pool.sem_inc(place_taken, 1)
                for c in range(HALVES):
                    for j in range(TPC):
                        for k in range(TOPK):
                            at = (c * TPC + j) * TOPK + k
                            nc.gpsimd.indirect_dma_start(
                                queue_dram, bass.IndirectOffsetOnAxis(ap=place_i[:, at:at + 1], axis=0),
                                hffn[c][:, j, :], None).then_inc(queued[c], 16)

            def experts(f):
                with pool.Fori(0, XTILES // STEP) as n:
                    for i in range(STEP):
                        pool.wait_ge(ytile_ready, n * STEP + (i + 1 + f * N_BACK))
                        pool.sem_inc(place_taken, 1)
                        for h in range(XPARTS):
                            nc.gpsimd.indirect_dma_start(
                                result_dram, bass.IndirectOffsetOnAxis(ap=result_row[i][:, h:h + 1], axis=0),
                                ytile[i][:, h, :], None, bounds_check=NO_RESULT - 1, oob_is_err=False).then_inc(y_stored[i], 16)

            pool.wait_ge(split_done, 1)
            for i in range(3):
                pool.dma_start(split_dram[i, :].rearrange("(p n) -> p n", p=P), bias_parts[:, i, :]).then_inc(split_out, 16)
            pool.wait_ge(split_out, 3 * 16)
            pool.wait_ge(rows_zero, 1)
            pool.dma_start(bias_rows[0:3, :], split_dram).then_inc(rows_in, 16)
            pool.wait_ge(setup_done, 1)
            for c in range(HALVES):
                pool.dma_start(queue_dram[bass.ds((c + 1) * REGION - 1, 1), :], tail_rows[0:1, :]).then_inc(queued[c], 16)
            for i in range(STEP):
                pool.dma_start(result_dram[bass.ds(NO_RESULT + P + i, 1), :], tail_rows[0:1, 0:D]).then_inc(y_stored[i], 16)
            pool.wait_ge(experts_in, 16 * len(EXPERTS))
            nc.gpsimd.tensor_copy(up_hi[:], up_raw).then_inc(hi_ready, 1)
            with pool.Fori(1, BATCH + 1) as m:
                scatter(m)
            experts(FIRST)
            def combine(c, m):
                pool.wait_ge(x_loaded[c], m * 16 + 16 * BATCH)
                pool.wait_ge(weighted[c], m)
                y = back_x[c].rearrange("p (j k) d -> p j k d", k=TOPK)
                nc.gpsimd.tensor_tensor(xsum[c][:], xin[c][:], y[:, :, 0, :], ALU.add).then_inc(first_added[c], 1)
                pool.wait_ge(first_added[c], m)
                nc.gpsimd.tensor_tensor(xsum[c][:], xsum[c][:], y[:, :, 1, :], ALU.add).then_inc(xsum_ready[c], 1)

            def next_sums(m):
                for c in range(HALVES):
                    pool.wait_ge(xold_copied[c], m)
                    pool.wait_ge(h_ready[c], m + BATCH)
                    pool.sem_inc(place_taken, 1)
                    combine(c, m + 1)

            for c in range(HALVES):
                combine(c, 1)
            next_sums(1)
            with pool.Fori(BATCH + 1, 2 * BATCH - 1) as m:
                next_sums(m - (BATCH - 1))
                scatter(m)
            scatter(2 * BATCH - 1)
            scatter(2 * BATCH)
            experts(SECOND)

        @block.scalar
        def _(act):
            step = [0]

            def begin():
                act.sem_clear(act_step)
                step[0] = 0

            def settle(ins):
                step[0] += 1
                ins.then_inc(act_step, 1)
                act.wait_ge(act_step, step[0])

            def deviations(c, m, var, moment, dev, ready):
                act.wait_ge(var[c], m)
                nc.scalar.activation(dev[c][:], moment[c][:, :, 1], ACT.Sqrt, bias=ln_eps[:, 0:1]).then_inc(ready[c], 1)

            def normalise(c, ready, count, src, rstd, shift, dst, normed):
                act.wait_ge(ready[c], count)
                for j in range(TPC):
                    last = nc.scalar.activation(dst[c][:, j, 0:D], src[c][:, j, :], ACT.Identity, bias=shift[c][:, j:j + 1], scale=rstd[c][:, j:j + 1])
                last.then_inc(normed[c], 1)

            def copy_turned(c, m, done, src, dst, ready):
                act.wait_ge(done[c], m)
                nc.scalar.activation(dst, src, ACT.Copy).then_inc(ready[c], 1)

            def empty_qkv(m, tiles):
                for tile in tiles:
                    c, j = divmod(tile, TPC)
                    act.wait_ge(qkv_done, m * BT + (tile + 1 - BT))
                    nc.scalar.activation(qkv[c][:, j, 0:3 * D], ps_qkv[j % 2][:, 0:3 * D], ACT.Copy).then_inc(qkv_taken, 1)

            def norms(c, m):
                act.wait_ge(qkv_taken, m * BT + ((c + 1) * TPC - BT))
                for half in range(2):
                    for j in range(TPC):
                        last = nc.scalar.activation(squares[:, half, j, :], qkv[c][:, j, half * D:(half + 1) * D], ACT.Square,
                                                    accum_out=sumsq[c][:, half, j:j + 1])
                settle(last)
                nc.scalar.activation(qk_dev[c][:], sumsq[c][:], ACT.Sqrt, bias=rms_eps[:, 0:1], scale=1.0 / D).then_inc(qkdev_ready[c], 1)

            def out_norms(c, m):
                act.wait_ge(out_ready[c], m)
                for j in range(TPC):
                    last = nc.scalar.activation(out_squares[:, j, :], tiles4(ps_half[c])[:, j, :], ACT.Square,
                                                accum_out=out_sum[c][:, j:j + 1])
                settle(last)
                nc.scalar.activation(out_dev[c][:], out_sum[c][:], ACT.Sqrt, bias=rms_eps[:, 0:1], scale=1.0 / D).then_inc(outdev_ready[c], 1)

            def scale_relu(c, m):
                act.wait_ge(rotated_ready[c], m)
                act.wait_ge(qkrstd_ready[c], m)
                for half, dst, ready in ((1, kf[c], kf_ready[c]), (0, qf[c], qf_ready[c])):
                    for j in range(TPC):
                        last = nc.scalar.activation(dst[:, j, :], rotated[c][:, j, half * D:(half + 1) * D], ACT.Relu,
                                                    scale=qk_rstd[c][:, half, j:j + 1])
                    last.then_inc(ready, 1)

            def attention(done, turned, ahead):
                both = range(HALVES)
                begin()
                if turned is not None:
                    scale_relu(0, turned)
                if done is not None:
                    for c in both:
                        copy_turned(c, done, attn_turned, ps_half[c], attn_t[c][:], attnt_ready)
                if turned is not None:
                    copy_turned(0, turned, qf_turned, ps_turn[0], qf_t[0][:], qft_ready)
                    scale_relu(1, turned)
                if ahead is not None:
                    for c in both:
                        deviations(c, ahead, var_ready, moment, dev, dev_ready)
                if done is not None:
                    for c in both:
                        out_norms(c, done)
                if turned is not None:
                    copy_turned(1, turned, qf_turned, ps_turn[1], qf_t[1][:], qft_ready)
                if ahead is not None:
                    for c in both:
                        copy_turned(c, ahead, h_turned, ps_turn[c], hmix_t[c][:], ht_ready)
                    empty_qkv(ahead, range(0, 3))
                if done is not None:
                    for c in both:
                        deviations(c, done, var2_ready, moment2, dev2, dev2_ready)
                if ahead is not None:
                    empty_qkv(ahead, range(3, BT))
                if done is not None:
                    for c in both:
                        copy_turned(c, done, h2_turned, ps_half[c], hffn_t[c][:], h2t_ready)
                if ahead is not None:
                    for c in both:
                        norms(c, ahead)

            def plan(f):
                if f == FIRST:
                    act.wait_ge(weights_in, 16 * len(WEIGHTS))
                    nc.scalar.activation(exp_decay[:], ch_sb[:, V_DECAY:V_DECAY + 1], ACT.Exp)
                act.wait_ge(gate_in, f + 1)
                nc.scalar.activation(small_a, small_a, ACT.Exp).then_inc(gate_exp, 1)

            def experts(f):
                def silu_up(t, i):
                    act.wait_ge(up_ready, t + (2 + f * N_UP))
                    at = (i + 1) % 2
                    for h in range(HCH):
                        last = nc.scalar.activation(gated[at][:, h, :], ps_up[at][:, h, :], ACT.Silu, bias=tile_bias[(i + 1) % STEP][:, h:h + 1])
                    last.then_inc(silu_ready, 1)

                def split_x(t, i):
                    act.wait_ge(xtile_turned, t + (4 + f * N_TURN))
                    nc.scalar.activation(xt_parts[(i + 3) % 2][:, 0, :], ps_xt[(i + 3) % 2], ACT.Copy).then_inc(xhi_ready, 1)

                def weights(t, i, e):
                    nc.scalar.activation(tile_up[i % 2][:, 0, :], up_hi[:, bass.ds(e * (2 * HID), 2 * HID)].bitcast(F32), ACT.Copy).then_inc(whi_ready, 1)

                act.wait_ge(table_ready, f + 1)
                act.wait_ge(lo_ready, f + 1)
                e = read(mybir.EngineType.Activation, tile_expert[0:1, 0:2], NE - 1)
                for t in range(-3, 0):
                    if t + 2 >= 0:
                        weights(t, t, e[t + 2])
                    if t + 1 >= 0:
                        silu_up(t, t)
                    split_x(t, t)
                with act.Fori(0, XTILES // STEP) as n:
                    first = n * STEP
                    e = read(mybir.EngineType.Activation, tile_expert[0:1, bass.ds(first + 2, STEP)], NE - 1)
                    for i in range(STEP):
                        weights(first + i, i, e[i])
                        silu_up(first + i, i)
                        split_x(first + i, i)


            def weigh(y, g, done, first=0, step=1):
                for at in range(first, TPC * TOPK, step):
                    last = nc.scalar.activation(y[:, at, :], y[:, at, :], ACT.Copy, scale=g[:, at:at + 1])
                last.then_inc(done, 1)

            def weight(m):
                nc.scalar.activation(gate[:].rearrange("p (j k) -> p j k", k=TOPK),
                                     gate_all[:, bass.ds(m * BT - BT, BT), :], ACT.Copy).then_inc(gate_taken, 1)
                act.wait_ge(gate_taken, m)
                for c in range(HALVES):
                    act.wait_ge(results_in[c], m * 16)
                    weigh(back_x[c], gate[:, c * TPC * TOPK:(c + 1) * TPC * TOPK], weighted[c])
                act.wait_ge(weighted[HALVES - 1], m)

            def weight_final(n):
                nc.scalar.activation(gate4[:].rearrange("p (j k) -> p j k", k=TOPK),
                                     gate_all[:, bass.ds(n * (RING * TPC) - RING * TPC, RING * TPC), :], ACT.Copy).then_inc(gate_taken, 1)
                act.wait_ge(gate_taken, n + BATCH)
                for i in range(RING):
                    act.wait_ge(final_in[i], n * 16)
                    weigh(final_y[i], gate4[:, i * TPC * TOPK:(i + 1) * TPC * TOPK], final_weighted, 1, TOPK)
                act.wait_ge(final_weighted, n * RING)

            def way_in(m):
                for c in range(HALVES):
                    deviations(c, m, var_ready, moment, dev, dev_ready)
                for c in range(HALVES):
                    normalise(c, scale_ready, m - BATCH, xsum, rstd, shift, hmix, h_ready)
                for c in range(HALVES):
                    act.wait_ge(h_turned[c], m)
                    nc.scalar.activation(hseq[:, 1 + c * CHUNK:1 + (c + 1) * CHUNK], ps_turn3, ACT.Copy).then_inc(ht_ready[c], 1)

            def keep_sums(m, before):
                for c in range(HALVES):
                    act.wait_ge(xsum_ready[c], m)
                    if before is not None:
                        act.wait_ge(mixed_ready[c], before)
                    nc.scalar.activation(xmid[c][:], xsum[c][:], ACT.Copy).then_inc(xold_copied[c], 1)

            def exponentials(m):
                act.wait_ge(past_expo, m)
                nc.scalar.activation(expo[:, 2:4, :], expo[:, 2:4, :], ACT.Exp).then_inc(past_ex, 1)
                act.wait_ge(now_expo, m)
                nc.scalar.activation(expo[:, 0, :], gap, ACT.Relu)
                nc.scalar.activation(expo[:, 1, :], gap, ACT.Relu, scale=-1.0).then_inc(gap_ready, 1)
                act.wait_ge(gap_ready, m)
                nc.scalar.activation(expo[:, 0:2, :], expo[:, 0:2, :], ACT.Exp, scale=-1.0).then_inc(now_ex, 1)
                act.wait_ge(r_ready, m)
                nc.scalar.activation(e_r, ps_r, ACT.Exp, scale=-1.0).then_inc(er_ready, 1)

            def mixing(m, ahead, weighed):
                both = range(HALVES)
                if ahead:
                    way_in(m + 1)
                if weighed:
                    weight(m - (BATCH - 2))
                for c in both:
                    act.wait_ge(mixed_ready[c], m - BATCH)
                    act.wait_ge(x_stored[c], m * 16)
                    nc.scalar.activation(xres[c][:], tiles4(ps_half[c]), ACT.Copy).then_inc(xres_ready[c], 1)
                if ahead:
                    keep_sums(m - (BATCH - 1), m - BATCH)
                for c in both:
                    deviations(c, m, var2_ready, moment2, dev2, dev2_ready)
                for c in both:
                    act.wait_ge(queued[c], m * SCATTERS + (16 - SCATTERS))
                    normalise(c, scale2_ready, m - BATCH, xres, rstd2, shift2, hffn, h2_ready)
                for c in both:
                    copy_turned(c, m, h2_turned, ps_half[c], hffn_t[c][:], h2t_ready)
                if ahead:
                    exponentials(m - (BATCH - 1))

            attention(None, None, 1)
            attention(None, 1, 2)
            with act.Fori(1, BATCH - 1) as m:
                attention(m, m + 1, m + 2)
            attention(BATCH - 1, BATCH, None)
            attention(BATCH, None, None)
            plan(FIRST)
            experts(FIRST)
            act.wait_ge(gates_ready, 1)
            weight(1)
            way_in(BATCH + 1)
            keep_sums(1, None)
            weight(2)
            exponentials(1)
            with act.Fori(BATCH + 1, 2 * BATCH - 1) as m:
                mixing(m, True, True)
            mixing(2 * BATCH - 1, True, False)
            mixing(2 * BATCH, False, False)
            plan(SECOND)
            experts(SECOND)
            act.wait_ge(gates_ready, 2)
            with act.Fori(1, CHUNKS // RING + 1) as n:
                weight_final(n)

        @block.tensor
        def _(pe):
            def turn(dst, src):
                for j in range(TPC):
                    last = nc.tensor.transpose(dst[:, j * P:(j + 1) * P], src[:, j, 0:D], ident)
                return last

            def bias(dst, column, width, stop):
                return nc.tensor.matmul(dst, ones_bf[:], bias_rows[:, bass.ds(column, width)], start=False, stop=stop)

            def read_state(m):
                pe.wait_ge(state_ready, m)
                for c in range(HALVES):
                    pe.wait_ge(qft_ready[c], m)
                    for j in range(TPC):
                        q = qf_t[c][:, j * P:(j + 1) * P]
                        nc.tensor.matmul(tiles4(ps_half[c])[:, j, :], q, state[:, 0:D], start=True, stop=True)
                        last = nc.tensor.matmul(ps_den[c][:, j, :], q, state[:, D:RES_W], start=True, stop=True)
                last.then_inc(res_ready, 1)

            def project_qkv(m):
                for tile in range(BT):
                    c, j = divmod(tile, TPC)
                    if j == 0:
                        pe.wait_ge(ht_ready[c], m)
                    if tile >= 2 or not (isinstance(m, int) and m == 1):
                        pe.wait_ge(qkv_taken, m * BT + (tile - 1 - BT))
                    dst = ps_qkv[j % 2][:, 0:3 * D]
                    nc.tensor.matmul(dst, hmix_t[c][:, j * P:(j + 1) * P], wqkv_sb[:], start=True, stop=False)
                    bias(dst, B_QKV, 3 * D, True).then_inc(qkv_done, 1)

            def keys_values(c, m):
                pe.wait_ge(kf_ready[c], m)
                for j in range(TPC):
                    last = nc.tensor.matmul(ps_vk[:, 0:D + 1], kf[c][:, j, :], qkv[c][:, j, 2 * D:3 * D + 1],
                                            start=(c == 0 and j == 0), stop=(c == HALVES - 1 and j == TPC - 1))
                if c == HALVES - 1:
                    last.then_inc(vk_ready, 1)

            def project_out(c, m):
                pe.wait_ge(attnt_ready[c], m)
                for j in range(TPC):
                    dst = tiles4(ps_half[c])[:, j, :]
                    nc.tensor.matmul(dst, attn_t[c][:, j * P:(j + 1) * P], wout_sb[:], start=True, stop=False)
                    last = bias(dst, B_OUT, D, True)
                last.then_inc(out_ready[c], 1)

            def turn_for_router(c, m):
                pe.wait_ge(h2_ready[c], m)
                turn(ps_half[c], hffn[c]).then_inc(h2_turned[c], 1)

            def scores(m):
                for c in range(HALVES):
                    pe.wait_ge(h2t_ready[c], m)
                    for j in range(TPC):
                        last = nc.tensor.matmul(ps_score[:, c * TPC + j, :], hffn_t[c][:, j * P:(j + 1) * P], wrouter_sb[:],
                                                start=True, stop=True)
                last.then_inc(score_ready, 1)

            def ranks(m):
                pe.wait_ge(member_ready, m)
                nc.tensor.matmul(ps_rank, tri_bf[:], member[:], start=True, stop=False)
                for j in range(BT - 1):
                    nc.tensor.matmul(ps_rank[:, j + 1:, :], ones_bf[:],
                                     member[:, j:j + 1, :].to_broadcast([P, BT - 1 - j, NE]), start=False, stop=False)
                nc.tensor.matmul(ps_rank, ones_bf[:], seen[:, None, :].to_broadcast([P, BT, NE]),
                                 start=False, stop=True).then_inc(rank_ready, 1)

            def attention(done, turned, ahead):
                both = range(HALVES)

                def take_keys(c):
                    keys_values(c, turned)
                    pe.wait_ge(qf_ready[c], turned)
                    turn(ps_turn[c], qf[c]).then_inc(qf_turned[c], 1)

                if done is not None:
                    for c in both:
                        pe.wait_ge(attn_ready[c], done)
                        turn(ps_half[c], attn[c]).then_inc(attn_turned[c], 1)
                if turned is not None:
                    take_keys(0)
                if done is not None:
                    for c in both:
                        project_out(c, done)
                if turned is not None:
                    take_keys(1)
                if ahead is not None:
                    for c in both:
                        pe.wait_ge(h_ready[c], ahead)
                        if turned is not None:
                            pe.wait_ge(qft_ready[c], turned)
                        turn(ps_turn[c], hmix[c]).then_inc(h_turned[c], 1)
                    project_qkv(ahead)
                if done is not None:
                    for c in both:
                        turn_for_router(c, done)
                    scores(done)
                if turned is not None:
                    read_state(turned)
                if done is not None:
                    ranks(done)

            def plan(f):
                pe.wait_ge(seen_ready, (f + 1) * BATCH)
                nc.tensor.matmul(ps_count, ones_bf[:], seen[:], start=True, stop=True).then_inc(count_ready, 1)

            def experts(f):
                def up(t, i):
                    pe.wait_ge(xlo_ready, t + (2 + f * N_TURN))
                    pe.wait_ge(whi_ready, t + (2 + f * N_WEIGHTS))
                    pe.wait_ge(wlo_ready, t + (2 + f * N_WEIGHTS))
                    at = (i + 1) % 2
                    for h in range(2 * HCH):
                        cols = slice(h * P, (h + 1) * P)
                        hi, lo = (tile_up[at][:, part, cols] for part in range(2))
                        nc.tensor.matmul(ps_up[at][:, h, :], hi, xt_parts[at][:, 0, :], start=True, stop=False)
                        nc.tensor.matmul(ps_up[at][:, h, :], hi, xt_parts[at][:, 1, :], start=False, stop=False)
                        last = nc.tensor.matmul(ps_up[at][:, h, :], lo, xt_parts[at][:, 0, :], start=False, stop=True)
                    last.then_inc(up_ready, 1)

                def turn_x(t, i):
                    slot = (i + 3) % STEP
                    pe.wait_ge(xtile_in[slot], round_of(t + 3, i + 3, f * (LOADED // STEP)))
                    for part in range(XPARTS):
                        last = nc.tensor.transpose(ps_xt[(i + 3) % 2][:, part * P:(part + 1) * P], xtile[slot][:, part, 0:D], ident)
                    last.then_inc(xtile_turned, 1)

                def down(t, i, e):
                    pe.wait_ge(gated_ready, t + (1 + f * N_GATE))
                    for part in range(XPARTS):
                        tokens = slice(part * P, (part + 1) * P)
                        y = ps_y[i % 2][:, part * D:(part + 1) * D]
                        for h in range(HCH):
                            last = nc.tensor.matmul(y, gated[i % 2][:, h, tokens], wdown_sb[:, bass.ds(e * (HCH * D) + h * D, D)],
                                                    start=(h == 0), stop=(h == HCH - 1))
                    last.then_inc(y_ready, 1)

                pe.wait_ge(table_ready, f + 1)
                for t in range(-3, 0):
                    if t + 1 >= 0:
                        up(t, t)
                    turn_x(t, t)
                with pe.Fori(0, XTILES // STEP) as n:
                    first = n * STEP
                    e = read(mybir.EngineType.PE, tile_expert[0:1, bass.ds(first, STEP)], NE - 1)
                    for i in range(STEP):
                        up(first + i, i)
                        down(first + i, i, e[i])
                        turn_x(first + i, i)

            def turn_in(m):
                for c in range(HALVES):
                    pe.wait_ge(h_ready[c], m)
                    if c:
                        pe.wait_ge(ht_ready[0], m)
                    turn(ps_turn3, hmix[c]).then_inc(h_turned[c], 1)

            def project(dst, i, halves=range(HALVES)):
                for c in halves:
                    part = dst[:, c * CHUNK:(c + 1) * CHUNK]
                    nc.tensor.matmul(part, wnow_sb[:, i, :], hseq[:, 1 + c * CHUNK:1 + (c + 1) * CHUNK], start=True, stop=False)
                    last = nc.tensor.matmul(part, wpast_sb[:, i, :], hseq[:, c * CHUNK:(c + 1) * CHUNK], start=False, stop=True)
                return last

            def mix_keys(m):
                for c in range(HALVES):
                    pe.wait_ge(ht_ready[c], m)
                project(ps_k, 0).then_inc(k_ready, 1)

            def mixing(m, ahead):
                both = range(HALVES)
                pe.wait_ge(er_ready, m - BATCH)
                for c in both:
                    pe.wait_ge(xold_copied[c], m - BATCH)
                    nc.tensor.matmul(ps_half[c], ident, xmid[c][:].rearrange("p j d -> p (j d)"), start=True, stop=False)
                if ahead:
                    turn_in(m + 1)
                    mix_keys(m + 1)
                for c in both:
                    pe.wait_ge(rwkv_ready[c], m - BATCH)
                    for j in range(TPC):
                        tile = slice(c * CHUNK + j * P, c * CHUNK + (j + 1) * P)
                        done = nc.tensor.matmul(tiles4(ps_half[c])[:, j, :], rwkv[:, tile], wo_sb[:], start=False, stop=(j == TPC - 1))
                    done.then_inc(mixed_ready[c], 1)
                if ahead:
                    project(ps_v, 1).then_inc(v_ready, 1)
                for c in both:
                    turn_for_router(c, m)
                scores(m)
                if ahead:
                    project(ps_r, 2, (0,))
                ranks(m)
                if ahead:
                    project(ps_r, 2, (1,)).then_inc(r_ready, 1)

            pe.wait_ge(consts_in, 16 * len(FIRST_USED))
            for c in range(HALVES):
                pe.wait_ge(h_ready[c], 1)
                turn(ps_turn[c], hmix[c]).then_inc(h_turned[c], 1)
            pe.wait_ge(setup_done, 1)
            pe.wait_ge(rows_in, 16)
            project_qkv(1)
            pe.wait_ge(weights_in, 16 * len(WEIGHTS))
            attention(None, 1, 2)
            with pe.Fori(1, BATCH - 1) as m:
                attention(m, m + 1, m + 2)
            attention(BATCH - 1, BATCH, None)
            attention(BATCH, None, None)
            plan(FIRST)
            experts(FIRST)
            turn_in(BATCH + 1)
            mix_keys(BATCH + 1)
            project(ps_v, 1).then_inc(v_ready, 1)
            project(ps_r, 2).then_inc(r_ready, 1)
            with pe.Fori(BATCH + 1, 2 * BATCH) as m:
                mixing(m, True)
            mixing(2 * BATCH, False)
            plan(SECOND)
            experts(SECOND)

        @block.vector
        def _(dve):
            step = [0]

            def begin():
                dve.sem_clear(dve_step)
                step[0] = 0

            def mark(ins):
                step[0] += 1
                ins.then_inc(dve_step, 1)
                return step[0]

            def need(count):
                dve.wait_ge(dve_step, count)

            def settle(ins):
                need(mark(ins))

            dve.wait_ge(bias_in, 16)
            settle(nc.vector.tensor_copy(bias_parts[:, 0, :], bias_sb[:]))
            settle(nc.vector.tensor_tensor(bias_left[:], bias_sb[:], bias_parts[:, 0, :], ALU.subtract))
            settle(nc.vector.tensor_copy(bias_parts[:, 1, :], bias_left[:]))
            settle(nc.vector.tensor_tensor(bias_left[:], bias_left[:], bias_parts[:, 1, :], ALU.subtract))
            nc.vector.tensor_copy(bias_parts[:, 2, :], bias_left[:]).then_inc(split_done, 1)
            nc.vector.memset(bias_rows[:], 0.0).then_inc(rows_zero, 1)
            nc.vector.memset(ln_eps[:], LN_EPS)
            nc.vector.memset(rms_eps[:], RMS_EPS)

            both = range(HALVES)

            def moments(src, stats, moment, ready):
                counted = []
                for c in both:
                    for j in range(TPC):
                        last = nc.vector.bn_stats(stats[c][:, j, :], src[c][:, j, :])
                    counted.append(mark(last))
                for c in both:
                    need(counted[c])
                    for j in range(TPC):
                        last = nc.vector.bn_aggr(moment[c][:, j, :], stats[c][:, j, :])
                    last.then_inc(ready[c], 1)

            def scales(m, moment, dev_ready, dev, rstd, shift, ready):
                inverted = []
                for c in both:
                    dve.wait_ge(dev_ready[c], m)
                    inverted.append(mark(nc.vector.reciprocal(rstd[c][:], dev[c][:])))
                for c in both:
                    need(inverted[c])
                    nc.vector.scalar_tensor_tensor(shift[c][:], moment[c][:, :, 0], -1.0, rstd[c][:], ALU.mult, ALU.mult).then_inc(ready[c], 1)

            def scales_in(m):
                scales(m, moment, dev_ready, dev, rstd, shift, scale_ready)

            def scales_for_experts(m):
                scales(m, moment2, dev2_ready, dev2, rstd2, shift2, scale2_ready)

            def normalise(m, src, moment, dev_ready, dev, rstd, dst, ready):
                inverted = []
                for c in both:
                    dve.wait_ge(dev_ready[c], m)
                    inverted.append(mark(nc.vector.reciprocal(rstd[c][:], dev[c][:])))
                for c in both:
                    need(inverted[c])
                    for j in range(TPC):
                        last = nc.vector.tensor_scalar(dst[c][:, j, 0:D], src[c][:, j, :], moment[c][:, j, 0:1], rstd[c][:, j:j + 1],
                                                       ALU.subtract, ALU.mult)
                    last.then_inc(ready[c], 1)

            def normalise_in(m):
                normalise(m, xin, moment, dev_ready, dev, rstd, hmix, h_ready)

            def normalise_for_experts(m):
                for c in both:
                    dve.wait_ge(queued[c], m * SCATTERS + (16 - SCATTERS))
                normalise(m, xres, moment2, dev2_ready, dev2, rstd2, hffn, h2_ready)

            def choose(m, f):
                at = m * BT - (1 + f * BATCH) * BT
                for c in both:
                    dve.wait_ge(queued[c], m * SCATTERS + (16 - SCATTERS))
                    nc.vector.tensor_copy(hffn[c][:, :, D], k_sb[:, bass.ds(at + (K_TOKEN + c * TPC), TPC)])
                dve.wait_ge(score_ready, m)
                settle(nc.vector.tensor_tensor(score[:], ps_score, rows_sb[:, None, 0:NE].to_broadcast([P, BT, NE]), ALU.add))
                settle(nc.vector.tensor_tensor(biased[:], score[:], rows_sb[:, None, NE:2 * NE].to_broadcast([P, BT, NE]), ALU.add))
                nc.vector.tensor_copy(score_all[:, bass.ds(at, BT), :], score[:])
                for j in range(BT):
                    last = nc.vector.max(top8[:, j, :], biased[:, j, :])
                settle(last)
                for j in range(BT):
                    last = nc.vector.max_index(top_at[:, j, :], top8[:, j, :], biased[:, j, :])
                settle(last)
                settle(nc.vector.tensor_copy(top_f[:], top_at[:, :, 0:TOPK]))
                settle(nc.vector.tensor_tensor(
                    onehot[:], top_f[:, :, :, None].to_broadcast([P, BT, TOPK, NE]),
                    k_sb[:, None, None, K_IOTA:K_IOTA + NE].to_broadcast([P, BT, TOPK, NE]), ALU.is_equal))
                nc.vector.tensor_tensor(member[:], onehot[:, :, 0, :], onehot[:, :, 1, :], ALU.add).then_inc(member_ready, 1)
                for c in both:
                    nc.vector.tensor_copy(hffn[c][:, :, D + 1], top_f[:, c * TPC:(c + 1) * TPC, 1])
                nc.vector.tensor_copy(onehot_all[:, bass.ds(at, BT), :, :], onehot[:])

            def place(m):
                dve.wait_ge(rank_ready, m)
                nc.vector.tensor_reduce(seen_new[:], member[:].rearrange("p j e -> p e j"), AX.X, ALU.add)
                nc.vector.tensor_tensor(place8[:], ps_rank, k_sb[:, None, K_REGION:K_REGION + NE].to_broadcast([P, BT, NE]), ALU.add).then_inc(place_step, 1)
                dve.wait_ge(place_step, m * PLACE_STEPS - 2)
                nc.vector.tensor_tensor(seen[:], seen[:], seen_new[:], ALU.add).then_inc(seen_ready, 1)
                nc.vector.tensor_tensor(picked[:], onehot[:], place8[:, :, None, :].to_broadcast([P, BT, TOPK, NE]), ALU.mult).then_inc(place_step, 1)
                dve.wait_ge(place_step, m * PLACE_STEPS - 1)
                nc.vector.tensor_reduce(place_f[:], picked[:], AX.X, ALU.add).then_inc(place_step, 1)
                dve.wait_ge(place_step, m * PLACE_STEPS)
                nc.vector.tensor_copy(place_i[:], place_f[:].rearrange("p j k -> p (j k)")).then_inc(place_ready, 1)

            def plan(f):
                begin()
                dve.wait_ge(count_ready, f + 1)
                settle(nc.vector.tensor_copy(count[:], ps_count))
                nc.vector.memset(seen[:], 0.0)
                nc.vector.tensor_scalar(tail_f[:], count[:], k_sb[:, K_PART:K_PART + 1], None, ALU.add)
                settle(nc.vector.tensor_scalar(count_i[:], count[:], float(XROWS - 1), None, ALU.add))
                nc.vector.tensor_tensor(tail_f[:], tail_f[:], k_sb[:, K_REGION:K_REGION + NE], ALU.add)
                settle(nc.vector.tensor_scalar(ntile_i[:], count_i[:], XROWS.bit_length() - 1, None, ALU.arith_shift_right))
                nc.vector.tensor_copy(tail_i[:], tail_f[:]).then_inc(tail_ready, 1)
                settle(nc.vector.tensor_copy(ntile[:], ntile_i[:]))
                settle(nc.vector.tensor_tensor_scan(cum[:], ones8[:], ntile[:], 0.0, ALU.mult, ALU.add))
                nc.vector.tensor_scalar(cum_rows[:], cum[:], float(XROWS), None, ALU.mult)
                nc.vector.tensor_scalar(jump[:], ntile[:], -float(XROWS), float(REGION), ALU.mult, ALU.add)
                settle(nc.vector.tensor_scalar(last_row[:], count[:, NE - 1:NE], float((NE - 1) * REGION), None, ALU.add))
                tile_at = k_sb[:, K_TILE:K_TILE + LOADED]
                shape = [P, NE - 1, LOADED]
                settle(nc.vector.tensor_tensor(past, tile_at[:, None, :].to_broadcast(shape),
                                               cum_rows[:, 0:NE - 1, None].to_broadcast(shape), ALU.is_ge))
                settle(nc.vector.tensor_tensor(past_j[0:1], past[0:1], jump[0:1, 0:NE - 1, None].to_broadcast([1, NE - 1, LOADED]), ALU.mult))
                nc.vector.tensor_reduce(expert_all[:], past.rearrange("p e t -> p t e"), AX.X, ALU.add)
                settle(nc.vector.tensor_reduce(row_f, past_j[0:1].rearrange("p e t -> p t e"), AX.X, ALU.add))
                nc.vector.tensor_copy(tile_expert[:], expert_all[0:1, :])
                settle(nc.vector.tensor_tensor(row_g, row_f, tile_at[0:1], ALU.add))
                nc.vector.tensor_scalar(tile_row[:], row_g, last_row[0:1, :], None, ALU.min).then_inc(table_ready, 1)
                settle(nc.vector.tensor_reduce(top_all[:], score_all[:], AX.X, ALU.max))
                nc.vector.tensor_tensor(small_a, score_all[:], top_all[:, :, None].to_broadcast([P, TILES, NE]), ALU.subtract).then_inc(gate_in, 1)
                dve.wait_ge(gate_exp, f + 1)
                if f == FIRST:
                    nc.vector.tensor_scalar(w_sb[:], exp_decay[:], -1.0, None, ALU.mult)
                settle(nc.vector.tensor_tensor(big, onehot_all[:], small_a[:, :, None, :].to_broadcast([P, TILES, TOPK, NE]), ALU.mult))
                settle(nc.vector.tensor_reduce(gate_w[:], big, AX.X, ALU.add))
                settle(nc.vector.tensor_tensor(gate_sum[:], gate_w[:, :, 0], gate_w[:, :, 1], ALU.add))
                settle(nc.vector.reciprocal(gate_sum[:], gate_sum[:]))
                nc.vector.tensor_tensor(gate_all[:], gate_w[:], gate_sum[:, :, None].to_broadcast([P, TILES, TOPK]), ALU.mult).then_inc(gates_ready, 1)
                if f == FIRST:
                    dve.wait_ge(hi_ready, 1)
                else:
                    dve.wait_ge(experts_in, 16 * (len(EXPERTS) + 1))
                nc.vector.tensor_tensor(up_lo[:], up_raw, up_hi[:].bitcast(F32), ALU.subtract).then_inc(lo_ready, 1)

            def experts(f):
                def place_rows(t, i):
                    slot = (i + 2) % STEP
                    dve.wait_ge(xtile_in[slot], round_of(t + 2, i + 2, f * (LOADED // STEP)))
                    dve.wait_ge(y_stored[slot], stored_before(t + 2, i + 2, f))
                    nc.vector.scalar_tensor_tensor(result_row[slot][:], xtile[slot][:, :, D + 1], expert_all[:, bass.ds(t + 2, 1)],
                                                   xtile[slot][:, :, D], ALU.is_equal, ALU.add)

                def gate(t, i):
                    dve.wait_ge(silu_ready, t + (2 + f * N_UP))
                    at = (i + 1) % 2
                    for h in range(HCH):
                        last = nc.vector.scalar_tensor_tensor(gated[at][:, h, :], ps_up[at][:, HCH + h, :],
                                                              tile_bias[(i + 1) % STEP][:, HCH + h:HCH + h + 1], gated[at][:, h, :], ALU.add, ALU.mult)
                    last.then_inc(gated_ready, 1)

                def split_x(t, i, e):
                    nc.vector.tensor_copy(tile_bias[(i + 3) % STEP][:], up_bias_sb[:, bass.ds(e * (2 * HCH), 2 * HCH)])
                    dve.wait_ge(xhi_ready, t + (4 + f * N_TURN))
                    at = (i + 3) % 2
                    nc.vector.tensor_tensor(xt_parts[at][:, 1, :], ps_xt[at], xt_parts[at][:, 0, :].bitcast(F32),
                                            ALU.subtract).then_inc(xlo_ready, 1)

                def weights(t, i, e):
                    nc.vector.tensor_copy(tile_up[i % 2][:, 1, :], up_lo[:, bass.ds(e * (2 * HID), 2 * HID)].bitcast(F32)).then_inc(wlo_ready, 1)

                def add_bias(t, i, e):
                    dve.wait_ge(y_ready, t + (1 + f * N_BACK))
                    dve.wait_ge(y_stored[i], stored_before(t, i, f))
                    nc.vector.tensor_tensor(ytile[i][:], ps_y[i % 2].rearrange("p (h d) -> p h d", d=D),
                                            down_bias_sb[:, bass.ds(e * D, D)][:, None, :].to_broadcast([P, XPARTS, D]), ALU.add).then_inc(ytile_ready, 1)

                dve.wait_ge(table_ready, f + 1)
                dve.wait_ge(lo_ready, f + 1)
                e = read(mybir.EngineType.DVE, tile_expert[0:1, 0:3], NE - 1)
                for t in range(-3, 0):
                    if t + 2 >= 0:
                        place_rows(t, t)
                        weights(t, t, e[t + 2])
                    if t + 1 >= 0:
                        gate(t, t)
                    split_x(t, t, e[t + 3])
                with dve.Fori(0, XTILES // STEP) as n:
                    first = n * STEP
                    e = read(mybir.EngineType.DVE, tile_expert[0:1, bass.ds(first, STEP + 3)], NE - 1)
                    for i in range(STEP):
                        place_rows(first + i, i)
                        weights(first + i, i, e[i + 2])
                        gate(first + i, i)
                        add_bias(first + i, i, e[i])
                        split_x(first + i, i, e[i + 3])

            def invert_norms(m):
                for c in both:
                    dve.wait_ge(qkdev_ready[c], m)
                    nc.vector.reciprocal(qk_rstd[c][:], qk_dev[c][:]).then_inc(qkrstd_ready[c], 1)

            def rotate(c, m):
                dve.wait_ge(qkv_taken, m * BT + ((c + 1) * TPC - BT))
                at = slice(c * TPC, (c + 1) * TPC)
                nc.vector.tensor_tensor(rotated[c][:], qkv[c][:, :, 0:2 * D], rope_c[:, at, :], ALU.mult)
                pairs = lambda a: a.rearrange("p j (m r) -> p j m r", r=2)
                a, s, o = pairs(qkv[c][:, :, 0:2 * D]), pairs(rope_s[:, at, :]), pairs(rope2[:])
                for r in range(2):
                    last = nc.vector.tensor_tensor(o[:, :, :, r], a[:, :, :, 1 - r], s[:, :, :, r], ALU.mult)
                settle(last)
                nc.vector.tensor_tensor(rotated[c][:], rotated[c][:], rope2[:], ALU.add).then_inc(rotated_ready[c], 1)
                dve.wait_ge(rotated_ready[c], m)

            def divide(m):
                dve.wait_ge(res_ready, m)
                settled = [mark(nc.vector.tensor_scalar(den_a[c][:], ps_den[c], LIN_EPS, None, ALU.add)) for c in both]
                for c in both:
                    need(settled[c])
                    settled[c] = mark(nc.vector.reciprocal(rden[c][:], den_a[c][:]))
                heads = lambda a: a.rearrange("p j (h d) -> p j h d", d=DH)
                for c in both:
                    need(settled[c])
                    nc.vector.tensor_tensor(heads(attn[c][:]), heads(tiles4(ps_half[c])),
                                            rden[c][:, :, :, None].to_broadcast([P, TPC, HEADS, DH]), ALU.mult).then_inc(attn_ready[c], 1)

            def residual(m):
                scaled = []
                for c in both:
                    dve.wait_ge(outdev_ready[c], m)
                    settle(nc.vector.reciprocal(out_rstd[c][:], out_dev[c][:]))
                    for j in range(TPC):
                        last = nc.vector.scalar_tensor_tensor(onorm[c][:, j, :], tiles4(ps_half[c])[:, j, :], out_rstd[c][:, j:j + 1],
                                                              gout_sb[:], ALU.mult, ALU.mult)
                    scaled.append(mark(last))
                for c in both:
                    dve.wait_ge(x_stored[c], m * 16)
                    dve.wait_ge(xold_loaded[c], m * 16)
                    need(scaled[c])
                    nc.vector.tensor_tensor(xres[c][:], onorm[c][:], xold[c][:], ALU.add).then_inc(xres_ready[c], 1)
                for c in both:
                    dve.wait_ge(xres_ready[c], m)
                moments(xres, stats2, moment2, var2_ready)

            def attention(done, turned, ahead):
                if turned is not None:
                    invert_norms(turned)
                if done is not None:
                    divide(done)
                if turned is not None:
                    rotate(1, turned)
                if ahead is not None:
                    for c in both:
                        dve.wait_ge(x_loaded[c], ahead * 16)
                    moments(xin, stats, moment, var_ready)
                    normalise_in(ahead)
                if done is not None:
                    residual(done)
                    normalise_for_experts(done)
                if turned is not None:
                    dve.wait_ge(vk_ready, turned)
                    nc.vector.tensor_tensor(state[:, 0:D], ps_vk[:, 0:D], k_sb[:, K_BLOCK:K_BLOCK + P], ALU.mult)
                    nc.vector.tensor_scalar(state[:, D:RES_W], k_sb[:, K_HEAD:K_HEAD + HEADS], ps_vk[:, D:D + 1], None, ALU.mult).then_inc(state_ready, 1)
                if ahead is not None:
                    rotate(0, ahead)
                if done is not None:
                    choose(done, FIRST)
                    begin()
                    place(done)

            def way_in_moments(m):
                for c in both:
                    dve.wait_ge(xsum_ready[c], m - BATCH)
                moments(xsum, stats, moment, var_ready)

            before, after = slice(0, SEQ), slice(1, 1 + SEQ)

            def maxima(row):
                dve.wait_ge(k_ready, row)
                return mark(nc.vector.tensor_tensor_scan(top[:, after], w_sb[:].to_broadcast([P, SEQ]), ps_k, top[:, 0:1], ALU.add, ALU.max))

            def exponents(row, scanned):
                need(scanned)
                settle(nc.vector.scalar_tensor_tensor(gap_past, top[:, before], w_sb[:, 0:1], ps_k, ALU.add, ALU.subtract))
                nc.vector.tensor_scalar(expo[:, 2, :], gap_past, 0.0, None, ALU.min)
                nc.vector.tensor_scalar(expo[:, 3, :], gap_past, -1.0, 0.0, ALU.mult, ALU.min).then_inc(past_expo, 1)
                nc.vector.scalar_tensor_tensor(gap, ps_k, ch_sb[:, V_FIRST:V_FIRST + 1], top[:, before],
                                               ALU.add, ALU.subtract).then_inc(now_expo, 1)
                dve.wait_ge(now_expo, row)

            def weighted_values(row):
                dve.wait_ge(past_ex, row)
                dve.wait_ge(v_ready, row)
                nc.vector.tensor_tensor(ev, expo[:, 3, :], ps_v, ALU.mult).then_inc(ev_ready, 1)

            def states(row):
                dve.wait_ge(ev_ready, row)
                return (mark(nc.vector.tensor_tensor_scan(num[:, after], expo[:, 2, :], ev, num[:, 0:1], ALU.mult, ALU.add)),
                        mark(nc.vector.tensor_tensor_scan(den[:, after], expo[:, 2, :], expo[:, 3, :], den[:, 0:1], ALU.mult, ALU.add)))

            def own_values(row):
                dve.wait_ge(now_ex, row)
                nc.vector.tensor_tensor(y_b, expo[:, 1, :], ps_v, ALU.mult)

            def outputs(row, num_done, den_done):
                need(num_done)
                num_done = mark(nc.vector.tensor_tensor(y_num, expo[:, 0, :], num[:, before], ALU.mult))
                need(den_done)
                den_done = mark(nc.vector.tensor_tensor(y_den, expo[:, 0, :], den[:, before], ALU.mult))
                need(num_done)
                nc.vector.tensor_tensor(y_num, y_num, y_b, ALU.add)
                need(den_done)
                settle(nc.vector.tensor_tensor(y_den, y_den, expo[:, 1, :], ALU.add))
                dve.wait_ge(er_ready, row)
                settle(nc.vector.scalar_tensor_tensor(y_den, e_r, 1.0, y_den, ALU.add, ALU.mult))
                for c in both:
                    part = slice(c * CHUNK, (c + 1) * CHUNK)
                    settle(nc.vector.reciprocal(y_den[:, part], y_den[:, part]))
                    nc.vector.tensor_tensor(rwkv[:, part], y_num[:, part], y_den[:, part], ALU.mult).then_inc(rwkv_ready[c], 1)

            def mixing(m, ahead, two_ahead):
                scans = states(m - BATCH)
                own_values(m - BATCH)
                if ahead:
                    scales_in(m + 1)
                outputs(m - BATCH, *scans)
                if ahead:
                    scanned = maxima(m - (BATCH - 1))
                for c in both:
                    dve.wait_ge(xres_ready[c], m)
                moments(xres, stats2, moment2, var2_ready)
                scales_for_experts(m)
                if ahead:
                    exponents(m - (BATCH - 1), scanned)
                if two_ahead:
                    way_in_moments(m + 2)
                choose(m, SECOND)
                begin()
                if ahead:
                    weighted_values(m - (BATCH - 1))
                place(m)

            begin()
            for c in both:
                dve.wait_ge(x_loaded[c], 16)
            moments(xin, stats, moment, var_ready)
            nc.vector.memset(ones_bf[:], 1.0)
            nc.vector.memset(tail_rows[:, 0:D], 0.0)
            nc.vector.memset(tail_rows[:, D + 1:ROW_W], -1.0)
            for c in both:
                nc.vector.memset(qkv[c][:, :, 3 * D:3 * D + 1], 1.0)
            dve.wait_ge(consts_in, 16 * len(FIRST_USED))
            nc.vector.tensor_scalar(tail_rows[:, D:D + 1], k_sb[:, K_PART:K_PART + 1], float(NO_RESULT), None, ALU.add)
            nc.vector.tensor_copy(tri_bf[:], k_sb[:, K_TRI:K_TRI + P]).then_inc(setup_done, 1)
            normalise_in(1)
            dve.wait_ge(rope_in, 16 * len(ROPE))
            for half in range(2):
                cols = slice(half * D, (half + 1) * D)
                for table, src, g in ((rope_c, cos_sb, gqk_sb), (rope_s, sin_sb, gqks_sb)):
                    last = nc.vector.tensor_tensor(table[:, :, cols], src, g[:, None, cols].to_broadcast([P, SEQ // P, D]), ALU.mult)
            settle(last)
            rotate(0, 1)
            dve.wait_ge(weights_in, 16 * len(WEIGHTS))
            settle(nc.vector.tensor_scalar(mix_left[:], ch_sb[:, V_MIXK:V_MIXR + 1], -1.0, 1.0, ALU.mult, ALU.add))
            for i in range(3):
                nc.vector.tensor_scalar(wnow_sb[:, i, :], wkvr_sb[:, i, :], ch_sb[:, V_MIXK + i:V_MIXK + i + 1], None, ALU.mult)
                nc.vector.tensor_scalar(wpast_sb[:, i, :], wkvr_sb[:, i, :], mix_left[:, i:i + 1], None, ALU.mult)
            nc.vector.memset(ones8[:], 1.0)
            nc.vector.memset(hseq[:, 0:1], 0.0)
            nc.vector.memset(top[:, 0:1], NO_PAST)
            nc.vector.memset(num[:, 0:1], 0.0)
            nc.vector.memset(den[:, 0:1], 0.0)
            settle(nc.vector.memset(seen[:], 0.0))
            for c in range(HALVES):
                dve.sem_inc(x_stored[c], 16)
            for i in range(RING):
                dve.sem_inc(out_stored[i], 16)
            begin()
            attention(None, 1, 2)
            begin()
            with dve.Fori(1, BATCH - 1) as m:
                attention(m, m + 1, m + 2)
            attention(BATCH - 1, BATCH, None)
            attention(BATCH, None, None)
            plan(FIRST)
            experts(FIRST)
            begin()
            way_in_moments(BATCH + 1)
            scales_in(BATCH + 1)
            exponents(1, maxima(1))
            way_in_moments(BATCH + 2)
            begin()
            weighted_values(1)
            with dve.Fori(BATCH + 1, 2 * BATCH - 1) as m:
                mixing(m, True, True)
            mixing(2 * BATCH - 1, True, False)
            mixing(2 * BATCH, False, False)
            plan(SECOND)
            experts(SECOND)
            dve.wait_ge(final_x_in, 16 * CHUNKS)
            for chunk in range(CHUNKS):
                n, i = divmod(chunk, RING)
                y = final_y[i].rearrange("p (j k) d -> p j k d", k=TOPK)
                dve.wait_ge(out_stored[i], (n + 1) * 16)
                dve.wait_ge(final_in[i], (n + 1) * 16)
                for j in range(TPC):
                    last = nc.vector.scalar_tensor_tensor(final_out[i][:, j, :], y[:, j, 0, :], gate_all[:, chunk * TPC + j, 0:1],
                                                          final_x[chunk][:, j, :], ALU.mult, ALU.add)
                last.then_inc(final_first, 1)
                dve.wait_ge(final_first, chunk + 1)
                dve.wait_ge(final_weighted, chunk + 1)
                nc.vector.tensor_tensor(final_out[i][:], final_out[i][:], y[:, :, 1, :], ALU.add).then_inc(final_ready, 1)


def kernel(**inputs):
    import numpy as np
    import concourse.bacc as bacc
    from concourse.bass_utils import run_bass_kernel_spmd

    def wide(v):
        return np.ascontiguousarray(np.broadcast_to(v.reshape(1, -1), (P, v.size)))

    def dense(a):
        return np.ascontiguousarray(a)

    a = {k: np.asarray(v) for k, v in inputs.items()}
    at = lambda name: a["L0_attn_a_" + name]
    mt = lambda name: a["L0_attn_b_" + name]
    ff = lambda name: a["L0_ffn_" + name]

    freq = (1.0 / np.float32(10000.0) ** (np.arange(0, DH, 2, dtype=np.float32) / np.float32(DH))).astype(np.float32)
    angle = np.outer(np.arange(SEQ, dtype=np.float32), freq)
    by_feature = lambda t: dense(np.tile(np.repeat(t, 2, axis=1), (1, HEADS)).reshape(SEQ // P, P, D).transpose(1, 0, 2))
    sign = np.tile(np.array([-1.0, 1.0], np.float32), D // 2)
    cosine = by_feature(np.cos(angle).astype(np.float32))
    sine = dense(by_feature(np.sin(angle).astype(np.float32)) * sign)

    consts = np.zeros((P, K_ALL), np.float32)
    part, feature = np.arange(P), np.arange(D)
    consts[:, K_ID:K_ID + P] = np.eye(P)
    consts[:, K_TRI:K_TRI + P] = np.triu(np.ones((P, P)), 1)
    consts[:, K_BLOCK:K_BLOCK + P] = feature[:, None] // DH == feature[None, :] // DH
    consts[:, K_HEAD:K_HEAD + HEADS] = feature[:, None] // DH == np.arange(HEADS)[None, :]
    consts[:, K_IOTA:K_IOTA + NE] = np.arange(NE)
    consts[:, K_REGION:K_REGION + NE] = np.arange(NE) * REGION
    consts[:, K_PART] = part
    consts[:, K_TILE:K_TILE + LOADED] = np.arange(LOADED) * XROWS
    consts[:, K_TOKEN:K_TOKEN + TILES] = (np.arange(TILES)[None, :] * P + part[:, None]) * TOPK

    swap = lambda g: g.reshape(-1, 2)[:, ::-1].reshape(-1)
    biases = np.concatenate([at("bqkv"), at("bout")])
    arrays = {
        "x": dense(at("x").reshape(TOKENS, D)),
        "cosine": cosine, "sine": sine, "consts": consts,
        "w_qkv": dense(at("Wqkv").T), "w_out": dense(at("Wout").T),
        "g_qk": wide(np.concatenate([at("gq"), at("gk")])),
        "g_qk_swapped": wide(np.concatenate([swap(at("gq")), swap(at("gk"))])),
        "g_out": wide(at("gout")), "bias_cols": dense(biases.reshape(P, B_ALL // P)),
        "w_router": dense(ff("Wr").T), "router_rows": wide(np.concatenate([ff("br"), ff("biases_N")])),
        "w_up": dense(ff("Wl1").transpose(1, 0, 2).reshape(D, -1)),
        "up_bias": dense(ff("bl1").reshape(NE * 2 * HCH, P).T),
        "down_bias": wide(ff("bl2").reshape(-1)),
        "w_down": dense(ff("Wl2").reshape(NE, HCH, P, D).transpose(2, 0, 1, 3).reshape(P, -1)),
        "channel": dense(np.stack([mt("time_decay"), mt("time_first"), mt("time_mix_k").reshape(-1),
                                   mt("time_mix_v").reshape(-1), mt("time_mix_r").reshape(-1)], axis=1)),
        "w_k": dense(mt("Wk").T), "w_v": dense(mt("Wv").T), "w_r": dense(mt("Wr").T), "w_o": dense(mt("Wo").T),
    }
    nc = bacc.Bacc("TRN2", target_bir_lowering=False, num_devices=1)
    args = {name: nc.dram_tensor(name, v.shape, mybir.dt.from_np(v.dtype), kind="ExternalInput").ap()
            for name, v in arrays.items()}
    out = nc.dram_tensor("out", (TOKENS, D), F32, kind="ExternalOutput").ap()
    program(nc, out=out, **args)
    result = run_bass_kernel_spmd(nc, [arrays], core_ids=[0])
    return result.results[0]["out"].reshape(BATCH, SEQ, D)
```
